# Optimizing a Trainium2 kernel written in Bass

```python
import numpy as np
import jax
import jax.numpy as jnp

def _softmax(x, axis=-1):
    return jax.nn.softmax(x, axis=axis)

def _gelu(x):
    return jax.nn.gelu(x, approximate=True)

def _silu(x):
    return jax.nn.silu(x)

def _sigmoid(x):
    return jax.nn.sigmoid(x)

def _layernorm(x, axis=-1, eps=1e-05):
    m = jnp.mean(x, axis=axis, keepdims=True)
    v = jnp.var(x, axis=axis, keepdims=True)
    return (x - m) / jnp.sqrt(v + eps)

def _scatter_add(tgt, idx, src, axis=0):
    return tgt.at[idx].add(src)

def _segment_sum(src, seg, n):
    return jax.ops.segment_sum(src, seg, n)
kernel_name = 'mk_gnn_resnorm_d4_gnn_r8_a96822'

def setup_inputs(seed: int=0):
    np.random.seed(seed)
    _w = jnp.asarray

    def _rec_inputs():
        import jax
        import jax.numpy as jnp
        _gk = jax.random.key(seed)
        x = -0.000202 + 1 * jax.random.normal(jax.random.fold_in(_gk, 1), (6250, 128), jnp.float32)
        _s = jax.random.randint(jax.random.fold_in(_gk, 2), (50000,), 0, 6250, jnp.int32)
        _d = jax.random.randint(jax.random.fold_in(_gk, 3), (50000,), 0, 6250, jnp.int32)
        _loop = jnp.arange(6250, dtype=jnp.int32)
        src = jnp.concatenate([_s, _d, _loop])
        dst = jnp.concatenate([_d, _s, _loop])
        _o = jnp.argsort(dst, stable=True)
        src = src[_o]
        dst = dst[_o]
        edge_attr_128 = -8.16379e-05 + 0.999858 * jax.random.normal(jax.random.fold_in(_gk, 12), (106250, 128), jnp.float32)
        edge_attr_16 = 0.000254156 + 0.999948 * jax.random.normal(jax.random.fold_in(_gk, 13), (106250, 16), jnp.float32)
        return (x, src, dst, edge_attr_128, edge_attr_16)
    x, src, dst, edge_attr_128, edge_attr_16 = _rec_inputs()

    def _L0_gnn_setup():
        import jax, jax.numpy as jnp
        import numpy as np
        N_NODES = 6250
        N_EDGES = 100000
        F_X = 128
        F_E = 128
        HIDDEN = 512
        F_OUT = 128
        key = jax.random.key(seed)
        k1, k2, k3, k4, k5, k6 = jax.random.split(key, 6)
        nodes = jax.random.normal(k1, (N_NODES, F_X), dtype=jnp.float32)
        edge_attr = jax.random.normal(k2, (N_EDGES, F_E), dtype=jnp.float32)
        senders = jax.random.randint(k3, (N_EDGES,), 0, N_NODES, dtype=jnp.int32)
        receivers = jax.random.randint(k4, (N_EDGES,), 0, N_NODES, dtype=jnp.int32)
        W1 = jax.random.normal(k5, (F_E + F_X, HIDDEN), dtype=jnp.float32) * (1.0 / np.sqrt(F_E + F_X))
        b1 = jnp.zeros((HIDDEN,), dtype=jnp.float32)
        W2 = jax.random.normal(k6, (HIDDEN, F_OUT), dtype=jnp.float32) * (1.0 / np.sqrt(HIDDEN))
        b2 = jnp.zeros((F_OUT,), dtype=jnp.float32)
        return {'nodes': nodes, 'edge_attr': edge_attr, 'senders': senders, 'receivers': receivers, 'W1': W1, 'b1': b1, 'W2': W2, 'b2': b2}
    _L0_gnn_all = _L0_gnn_setup()
    _L0_gnn_in = {k: v for k, v in _L0_gnn_all.items() if k in ('W1', 'b1', 'W2', 'b2')}
    del _L0_gnn_all

    def _L1_gnn_setup():
        import jax, jax.numpy as jnp
        import numpy as np
        N, E, D = (12500, 200000, 128)
        H = 2 * D
        BN_EPS = 1e-05

        def _bn(h, gamma, beta):
            mu = jnp.mean(h, axis=0)
            var = jnp.mean(jnp.square(h - mu), axis=0)
            return (h - mu) * jax.lax.rsqrt(var + BN_EPS) * gamma + beta
        key = jax.random.key(seed)
        ks = jax.random.split(key, 8)
        x = jax.random.normal(ks[0], (N, D), dtype=jnp.float32)
        edge_index = jax.random.randint(ks[1], (2, E), 0, N, dtype=jnp.int64)
        s1 = 1.0 / np.sqrt(D)
        s2 = 1.0 / np.sqrt(H)
        W1 = jax.random.uniform(ks[2], (D, H), jnp.float32, -s1, s1)
        b1 = jax.random.uniform(ks[3], (H,), jnp.float32, -s1, s1)
        W2 = jax.random.uniform(ks[4], (H, D), jnp.float32, -s2, s2)
        b2 = jax.random.uniform(ks[5], (D,), jnp.float32, -s2, s2)
        return {'x': x, 'edge_index': edge_index, 'eps': jnp.zeros((), jnp.float32), 'W1': W1, 'b1': b1, 'g1': jnp.ones((H,), jnp.float32), 'be1': jnp.zeros((H,), jnp.float32), 'W2': W2, 'b2': b2, 'g2': jnp.ones((D,), jnp.float32), 'be2': jnp.zeros((D,), jnp.float32)}
    _L1_gnn_all = _L1_gnn_setup()
    _L1_gnn_in = {k: v for k, v in _L1_gnn_all.items() if k in ('eps', 'W1', 'b1', 'g1', 'be1', 'W2', 'b2', 'g2', 'be2')}
    del _L1_gnn_all

    def _L2_gnn_setup():
        import jax, jax.numpy as jnp
        import numpy as np
        N, D, H, O, E = (6250, 128, 256, 128, 100000)

        def _sage_conv(x, src, dst, W_l, W_r, b, n_nodes):
            agg = jax.ops.segment_sum(x[src], dst, num_segments=n_nodes)
            cnt = jax.ops.segment_sum(jnp.ones(src.shape[0], x.dtype), dst, num_segments=n_nodes)
            agg = agg / jnp.maximum(cnt, 1.0)[:, None]
            return agg @ W_l + b + x @ W_r
        key = jax.random.key(seed)
        ks = jax.random.split(key, 8)
        x = jax.random.normal(ks[0], (N, D), dtype=jnp.float32)
        edge_index = jax.random.randint(ks[1], (2, E), 0, N, dtype=jnp.int64)
        s = lambda k, shp: jax.random.normal(k, shp, dtype=jnp.float32) / np.sqrt(shp[0])
        return {'x': x, 'edge_index': edge_index, 'W1_l': s(ks[2], (D, H)), 'W1_r': s(ks[3], (D, H)), 'b1': jnp.zeros((H,), jnp.float32), 'W2_l': s(ks[4], (H, O)), 'W2_r': s(ks[5], (H, O)), 'b2': jnp.zeros((O,), jnp.float32)}
    _L2_gnn_all = _L2_gnn_setup()
    _L2_gnn_in = {k: v for k, v in _L2_gnn_all.items() if k in ('W1_l', 'W1_r', 'b1', 'W2_l', 'W2_r', 'b2')}
    del _L2_gnn_all

    def _L3_gnn_setup():
        import jax, jax.numpy as jnp
        import numpy as np
        N, IN, OUT, H, ED, E = (6250, 128, 128, 3, 16, 100000)
        NEG_SLOPE = 0.2
        LN_EPS = 1e-05

        def gat_block(x, edge_index, edge_attr, W, W_edge, att_src, att_dst, att_edge, gat_bias, lin_W, lin_b, ln_g, ln_b):
            row, col = (edge_index[0], edge_index[1])
            n = x.shape[0]
            deg = jax.ops.segment_sum(jnp.ones((edge_attr.shape[0],), x.dtype), col, num_segments=n)
            loop_attr = jax.ops.segment_sum(edge_attr, col, num_segments=n) / jnp.maximum(deg, 1.0)[:, None]
            loop = jnp.arange(n, dtype=row.dtype)
            row2 = jnp.concatenate([row, loop])
            col2 = jnp.concatenate([col, loop])
            ea2 = jnp.concatenate([edge_attr, loop_attr], axis=0)
            xp = (x @ W).reshape(n, H, OUT)
            a_src = jnp.einsum('nhc,hc->nh', xp, att_src)
            a_dst = jnp.einsum('nhc,hc->nh', xp, att_dst)
            ep = (ea2 @ W_edge).reshape(-1, H, OUT)
            a_edge = jnp.einsum('ehc,hc->eh', ep, att_edge)
            alpha = a_src[row2] + a_dst[col2] + a_edge
            alpha = jnp.where(alpha >= 0, alpha, NEG_SLOPE * alpha)
            m = jax.ops.segment_max(alpha, col2, num_segments=n)
            ex = jnp.exp(alpha - m[col2])
            denom = jax.ops.segment_sum(ex, col2, num_segments=n)
            attn = ex / denom[col2]
            msg = attn[:, :, None] * xp[row2]
            agg = jax.ops.segment_sum(msg, col2, num_segments=n)
            x_gat = agg.reshape(n, H * OUT) + gat_bias
            y = x_gat @ lin_W + lin_b
            h = x + y
            mu = h.mean(-1, keepdims=True)
            var = ((h - mu) ** 2).mean(-1, keepdims=True)
            return (h - mu) * jax.lax.rsqrt(var + LN_EPS) * ln_g + ln_b
        key = jax.random.key(seed)
        ks = jax.random.split(key, 12)
        s = lambda k, shape, fan: jax.random.normal(k, shape, jnp.float32) / np.sqrt(fan)
        return {'x': jax.random.normal(ks[0], (N, IN), jnp.float32), 'edge_index': jax.random.randint(ks[1], (2, E), 0, N, jnp.int64), 'edge_attr': jax.random.normal(ks[2], (E, ED), jnp.float32), 'W': s(ks[3], (IN, H * OUT), IN), 'W_edge': s(ks[4], (ED, H * OUT), ED), 'att_src': s(ks[5], (H, OUT), OUT), 'att_dst': s(ks[6], (H, OUT), OUT), 'att_edge': s(ks[7], (H, OUT), OUT), 'gat_bias': jnp.zeros((H * OUT,), jnp.float32), 'lin_W': s(ks[8], (H * OUT, OUT), H * OUT), 'lin_b': jnp.zeros((OUT,), jnp.float32), 'ln_g': jnp.ones((OUT,), jnp.float32), 'ln_b': jnp.zeros((OUT,), jnp.float32)}
    _L3_gnn_all = _L3_gnn_setup()
    _L3_gnn_in = {k: v for k, v in _L3_gnn_all.items() if k in ('W', 'W_edge', 'att_src', 'att_dst', 'att_edge', 'gat_bias', 'lin_W', 'lin_b', 'ln_g', 'ln_b')}
    del _L3_gnn_all
    return {'x': x, 'src': src, 'dst': dst, 'edge_attr_128': edge_attr_128, 'edge_attr_16': edge_attr_16, 'L0_gnn_W1': _L0_gnn_in['W1'], 'L0_gnn_b1': _L0_gnn_in['b1'], 'L0_gnn_W2': _L0_gnn_in['W2'], 'L0_gnn_b2': _L0_gnn_in['b2'], 'L1_gnn_eps': _L1_gnn_in['eps'], 'L1_gnn_W1': _L1_gnn_in['W1'], 'L1_gnn_b1': _L1_gnn_in['b1'], 'L1_gnn_g1': _L1_gnn_in['g1'], 'L1_gnn_be1': _L1_gnn_in['be1'], 'L1_gnn_W2': _L1_gnn_in['W2'], 'L1_gnn_b2': _L1_gnn_in['b2'], 'L1_gnn_g2': _L1_gnn_in['g2'], 'L1_gnn_be2': _L1_gnn_in['be2'], 'L2_gnn_W1_l': _L2_gnn_in['W1_l'], 'L2_gnn_W1_r': _L2_gnn_in['W1_r'], 'L2_gnn_b1': _L2_gnn_in['b1'], 'L2_gnn_W2_l': _L2_gnn_in['W2_l'], 'L2_gnn_W2_r': _L2_gnn_in['W2_r'], 'L2_gnn_b2': _L2_gnn_in['b2'], 'L3_gnn_W': _L3_gnn_in['W'], 'L3_gnn_W_edge': _L3_gnn_in['W_edge'], 'L3_gnn_att_src': _L3_gnn_in['att_src'], 'L3_gnn_att_dst': _L3_gnn_in['att_dst'], 'L3_gnn_att_edge': _L3_gnn_in['att_edge'], 'L3_gnn_gat_bias': _L3_gnn_in['gat_bias'], 'L3_gnn_lin_W': _L3_gnn_in['lin_W'], 'L3_gnn_lin_b': _L3_gnn_in['lin_b'], 'L3_gnn_ln_g': _L3_gnn_in['ln_g'], 'L3_gnn_ln_b': _L3_gnn_in['ln_b']}

def reference(x, src, dst, edge_attr_128, edge_attr_16, L0_gnn_W1, L0_gnn_b1, L0_gnn_W2, L0_gnn_b2, L1_gnn_eps, L1_gnn_W1, L1_gnn_b1, L1_gnn_g1, L1_gnn_be1, L1_gnn_W2, L1_gnn_b2, L1_gnn_g2, L1_gnn_be2, L2_gnn_W1_l, L2_gnn_W1_r, L2_gnn_b1, L2_gnn_W2_l, L2_gnn_W2_r, L2_gnn_b2, L3_gnn_W, L3_gnn_W_edge, L3_gnn_att_src, L3_gnn_att_dst, L3_gnn_att_edge, L3_gnn_gat_bias, L3_gnn_lin_W, L3_gnn_lin_b, L3_gnn_ln_g, L3_gnn_ln_b):
    import jax
    import jax.numpy as jnp

    def _L0_gnn_ref(nodes, edge_attr, senders, receivers, W1, b1, W2, b2):
        import jax, jax.numpy as jnp
        import numpy as np
        N_NODES = 6250
        N_EDGES = 100000
        F_X = 128
        F_E = 128
        HIDDEN = 512
        F_OUT = 128
        agg = jax.ops.segment_sum(edge_attr, receivers, num_segments=N_NODES)
        x = jnp.concatenate([agg, nodes], axis=1)
        h = jax.nn.relu(x @ W1 + b1)
        return h @ W2 + b2

    def _L1_gnn_ref(x, edge_index, eps, W1, b1, g1, be1, W2, b2, g2, be2):
        import jax, jax.numpy as jnp
        import numpy as np
        N, E, D = (12500, 200000, 128)
        H = 2 * D
        BN_EPS = 1e-05

        def _bn(h, gamma, beta):
            mu = jnp.mean(h, axis=0)
            var = jnp.mean(jnp.square(h - mu), axis=0)
            return (h - mu) * jax.lax.rsqrt(var + BN_EPS) * gamma + beta
        identity = x
        src, dst = (edge_index[0], edge_index[1])
        agg = jax.ops.segment_sum(x[src], dst, num_segments=x.shape[0])
        h = (1.0 + eps) * x + agg
        h = _bn(h @ W1 + b1, g1, be1)
        h = jax.nn.relu(h)
        h = h @ W2 + b2
        h = _bn(h, g2, be2)
        return jax.nn.relu(h + identity)

    def _L2_gnn_ref(x, edge_index, W1_l, W1_r, b1, W2_l, W2_r, b2):
        import jax, jax.numpy as jnp
        import numpy as np
        N, D, H, O, E = (6250, 128, 256, 128, 100000)

        def _sage_conv(x, src, dst, W_l, W_r, b, n_nodes):
            agg = jax.ops.segment_sum(x[src], dst, num_segments=n_nodes)
            cnt = jax.ops.segment_sum(jnp.ones(src.shape[0], x.dtype), dst, num_segments=n_nodes)
            agg = agg / jnp.maximum(cnt, 1.0)[:, None]
            return agg @ W_l + b + x @ W_r
        src, dst = (edge_index[0], edge_index[1])
        h = jax.nn.relu(_sage_conv(x, src, dst, W1_l, W1_r, b1, N))
        out = _sage_conv(h, src, dst, W2_l, W2_r, b2, N)
        return out

    def _L3_gnn_ref(x, edge_index, edge_attr, W, W_edge, att_src, att_dst, att_edge, gat_bias, lin_W, lin_b, ln_g, ln_b):
        import jax, jax.numpy as jnp
        import numpy as np
        N, IN, OUT, H, ED, E = (6250, 128, 128, 3, 16, 100000)
        NEG_SLOPE = 0.2
        LN_EPS = 1e-05

        def gat_block(x, edge_index, edge_attr, W, W_edge, att_src, att_dst, att_edge, gat_bias, lin_W, lin_b, ln_g, ln_b):
            row, col = (edge_index[0], edge_index[1])
            n = x.shape[0]
            deg = jax.ops.segment_sum(jnp.ones((edge_attr.shape[0],), x.dtype), col, num_segments=n)
            loop_attr = jax.ops.segment_sum(edge_attr, col, num_segments=n) / jnp.maximum(deg, 1.0)[:, None]
            loop = jnp.arange(n, dtype=row.dtype)
            row2 = jnp.concatenate([row, loop])
            col2 = jnp.concatenate([col, loop])
            ea2 = jnp.concatenate([edge_attr, loop_attr], axis=0)
            xp = (x @ W).reshape(n, H, OUT)
            a_src = jnp.einsum('nhc,hc->nh', xp, att_src)
            a_dst = jnp.einsum('nhc,hc->nh', xp, att_dst)
            ep = (ea2 @ W_edge).reshape(-1, H, OUT)
            a_edge = jnp.einsum('ehc,hc->eh', ep, att_edge)
            alpha = a_src[row2] + a_dst[col2] + a_edge
            alpha = jnp.where(alpha >= 0, alpha, NEG_SLOPE * alpha)
            m = jax.ops.segment_max(alpha, col2, num_segments=n)
            ex = jnp.exp(alpha - m[col2])
            denom = jax.ops.segment_sum(ex, col2, num_segments=n)
            attn = ex / denom[col2]
            msg = attn[:, :, None] * xp[row2]
            agg = jax.ops.segment_sum(msg, col2, num_segments=n)
            x_gat = agg.reshape(n, H * OUT) + gat_bias
            y = x_gat @ lin_W + lin_b
            h = x + y
            mu = h.mean(-1, keepdims=True)
            var = ((h - mu) ** 2).mean(-1, keepdims=True)
            return (h - mu) * jax.lax.rsqrt(var + LN_EPS) * ln_g + ln_b
        return gat_block(x, edge_index, edge_attr, W, W_edge, att_src, att_dst, att_edge, gat_bias, lin_W, lin_b, ln_g, ln_b)
    edge_index = jnp.stack([src, dst])
    x = _layernorm(x + _L0_gnn_ref(x, edge_attr_128, src, dst, L0_gnn_W1, L0_gnn_b1, L0_gnn_W2, L0_gnn_b2), axis=-1)
    x = _layernorm(x + _L1_gnn_ref(x, edge_index, L1_gnn_eps, L1_gnn_W1, L1_gnn_b1, L1_gnn_g1, L1_gnn_be1, L1_gnn_W2, L1_gnn_b2, L1_gnn_g2, L1_gnn_be2), axis=-1)
    x = _layernorm(x + _L2_gnn_ref(x, edge_index, L2_gnn_W1_l, L2_gnn_W1_r, L2_gnn_b1, L2_gnn_W2_l, L2_gnn_W2_r, L2_gnn_b2), axis=-1)
    x = _layernorm(x + _L3_gnn_ref(x, edge_index, edge_attr_16, L3_gnn_W, L3_gnn_W_edge, L3_gnn_att_src, L3_gnn_att_dst, L3_gnn_att_edge, L3_gnn_gat_bias, L3_gnn_lin_W, L3_gnn_lin_b, L3_gnn_ln_g, L3_gnn_ln_b), axis=-1)
    return x

_drawn_inputs = setup_inputs


def setup_inputs(seed=0):
    import zlib

    import numpy as np

    out = dict(_drawn_inputs(seed))
    spreads = {'L0_gnn_b1': (0.0, 0.1),
     'L0_gnn_b2': (0.0, 0.1),
     'L1_gnn_g1': (1.0, 0.2),
     'L1_gnn_be1': (0.0, 0.278),
     'L1_gnn_g2': (1.0, 0.2),
     'L1_gnn_be2': (0.0, 0.1),
     'L2_gnn_b1': (0.0, 0.1),
     'L2_gnn_b2': (0.0, 0.1),
     'L3_gnn_gat_bias': (0.0, 0.1),
     'L3_gnn_lin_b': (0.0, 0.1),
     'L3_gnn_ln_g': (1.0, 0.2),
     'L3_gnn_ln_b': (0.0, 0.1)}
    factors = {'L1_gnn_b1': 8.0, 'L1_gnn_b2': 8.0, 'L3_gnn_att_dst': 2.859}
    for name, (base, spread) in spreads.items():
        noise = np.random.default_rng([zlib.crc32(name.encode()), seed]).standard_normal(out[name].shape)
        drawn = base * np.exp(spread * noise) if base else spread * noise
        out[name] = jnp.asarray(drawn.astype(out[name].dtype))
    for name, factor in factors.items():
        out[name] = (out[name] * factor).astype(out[name].dtype)
    return out
```

```python
from contextlib import ExitStack

import concourse.bass as bass
from concourse import mybir

F32 = mybir.dt.float32
I32 = mybir.dt.int32
ALU = mybir.AluOpType
ACT = mybir.ActivationFunctionType
AX = mybir.AxisListType

P = 128
CH = 4
GE = P * CH
RING = 4
W = 40
HEADS = 3
EF = 16
ROW3 = 132
NORM_EPS = 1e-5
SLOPE = 0.2
BIG = 1e30
NOWHERE = 20000


class Count:

    def __init__(self):
        self.n = 0

    def up(self):
        self.n += 1
        return 1


def gnn_stack(nc, t, out):
    N = t["x"].shape[0]
    E = t["src"].shape[0]
    H0 = t["L0_gnn_W1"].shape[1] // P
    H1 = t["L1_gnn_W1"].shape[1] // P
    NG = -(-E // (GE * RING)) * RING
    NIT = NG // RING
    EP = NG * GE
    NK = -(-N // W)
    NA = max(N + W, NK * W)
    TN = 125
    TP = 2
    PN = TN * TP
    NT = N // TN
    NP = N // PN
    EPP = EP // P
    FULL = E // GE
    TAIL_P = (E - FULL * GE) // CH
    TAIL_C = (E - FULL * GE) % CH
    assert N % PN == 0 and NP % 2 == 1 and FULL == NG - 1 and TAIL_C and NA < 8192 and N < NOWHERE

    ctx = ExitStack()
    with ctx:
        def sb(name, shape, dt=F32):
            return ctx.enter_context(nc.sbuf_tensor(name, shape, dt))

        def sem(name):
            return ctx.enter_context(nc.semaphore(name))

        def sems(name, n):
            return [sem(f"{name}{i}") for i in range(n)]

        def dram(name, shape, dt=F32):
            return nc.dram_tensor(name, shape, dt, kind="Internal").ap()

        src_d = dram("src_filled", (EP,), I32)
        dst_d = dram("dst_filled", (EP + 2,), I32)
        x1_d = dram("x1_rows", (N, P))
        x2_d = dram("x2_rows", (N, P))
        z_d = dram("z_rows", (N, P))
        q_d = dram("q_rows", (N, P))
        t3_d = dram("x3_rows", (N, ROW3))
        sums_d = dram("node_sums", (1 + HEADS, N))
        rcnt_d = dram("rcnt", (N,))
        push_d = dram("pushed", (EP, 2 * HEADS))
        xe_d = dram("x3_of_edges", (EP, P))
        as_d = dram("src_and_edge_score", (EP, HEADS))
        at_d = dram("attention", (EP, HEADS))
        wl_d = dram("loop_weight", (EP, HEADS))

        wide = sb("wide", [P, 3, NA])
        wide_f = wide[:, :, :].rearrange("p a n -> p (a n)")
        rcnt = wide[:, 1, 0:N]
        nsum = sb("nsum", [1 + HEADS, NA])
        rows = sb("rows", [P, RING, CH, ROW3])
        onehot = sb("onehot", [P, RING, CH, W])
        weighted = sb("weighted", [P, RING, CH, HEADS, W])
        idx = sb("idx", [P, RING, CH], I32)
        ea = sb("ea", [P, RING, CH, EF])
        prod = sb("prod", [P, RING, CH, HEADS, EF])
        one_ae = sb("one_ae", [P, RING, CH, 1 + HEADS])
        asum = sb("asum", [P, RING, CH, HEADS])
        att = sb("att", [P, RING, CH, HEADS])
        dst_rel = sb("dst_rel", [P, (NG + RING) * CH])
        dst_left = sb("dst_left", [P, NG * CH])
        dst_i = wide_f[:, 4 * NG * CH:5 * NG * CH].bitcast(I32)
        meta = sb("meta", [1, NIT, RING + 1], I32)
        base_i = sb("base_i", [1, NG], I32)
        base_f = sb("base_f", [1, NG])
        iota_w = sb("iota_w", [P, W])
        iota_x = sb("iota_x", [P, W])
        wrap_x = sb("wrap_x", [P, W])
        onehot_x = sb("onehot_x", [P, CH, W])
        weighted_x = sb("weighted_x", [P, CH, HEADS, W])
        ident = sb("ident", [P, P])
        ones = sb("ones", [P, P])
        fill_i = sb("fill_i", [1, GE], I32)
        mark_i = sb("mark_i", [1, GE], I32)
        zeros = sb("zeros", [P, EPP])
        missed = sb("missed", [P, NIT])
        xb = sb("xb", [TN, 2, TP, P])
        yb = sb("yb", [TN, 2, TP, ROW3])
        zb = sb("zb", [TN, 2, TP, P])
        rb = sb("rb", [TN, 2, TP, P])
        ub = sb("ub", [TN, 2, TP, P])
        xT = sb("xT", [P, 2, PN])
        aT = sb("aT", [P, 2, 3, PN])
        hT = sb("hT", [P, 2, H0, PN])
        st = sb("st", [TN, 2, TP, 6])
        mv = sb("mv", [TN, 2, TP, 2])
        rstd = sb("rstd", [TN, 2, TP])
        norm_eps = sb("norm_eps", [P, 1])
        w01 = sb("w01", [P, 2, H0 * P])
        w02 = sb("w02", [P, H0, P])
        w11 = sb("w11", [P, H1 * P])
        w12 = sb("w12", [P, H1, P])
        w21 = sb("w21", [P, 2, H1 * P])
        w22 = sb("w22", [P, H1, 2, P])
        w3 = sb("w3", [P, HEADS, P])
        lin = sb("lin", [P, HEADS, P])
        w3T = sb("w3T", [P, HEADS, P])
        fused3 = sb("fused3", [P, HEADS, P])
        att_b = sb("att_b", [P, 2, HEADS, P])
        v6 = sb("v6", [P, 2 * HEADS])
        we = sb("we", [EF, HEADS, P])
        ae_b = sb("ae_b", [EF, HEADS, P])
        we3 = sb("we3", [EF, HEADS])
        we_d = sb("we_d", [EF, HEADS, EF])
        we_b = sb("we_b", [P, HEADS, EF])
        col = sb("col", [P, 32])
        b01, b11, g11, e11, b12, g12, e12, b21, gatb = (0, 4, 6, 8, 10, 11, 12, 13, 15)
        eps1 = col[:, 20:21]
        row2 = sb("row2", [1, 4, P])
        ln_gb = sb("ln_gb", [TN, 2, P])
        bn1 = sb("bn1", [P, H1, NP, 6])
        bn2 = sb("bn2", [P, NP, 6])
        bnm = sb("bnm", [P, H1 + 1, 2])
        bns = sb("bns", [P, H1 + 1, 2])
        cntB = sb("cntB", [NT, 1 + HEADS, TN])
        endB = sb("endB", [NT, TN])
        begB = sb("begB", [NT, TN])
        rcB = sb("rcB", [NT, TN])
        meanB = sb("meanB", [NT, HEADS, TN])
        tri = sb("tri", [NT, NT])
        carB = sb("carB", [NT, 1])
        amean = sb("amean", [TN, NT, HEADS])
        beg_i = sb("beg_i", [TN, NT], I32)
        end_i = sb("end_i", [TN, NT], I32)
        push = sb("push", [TN, NT, 2 * HEADS])
        psum6 = sb("psum6", [TN, 2, TP, HEADS])
        wloop = sb("wloop", [TN, NT, HEADS])
        ends = sb("ends", [P, 2, 2, 2 * HEADS])
        goes = sb("goes", [2 * HEADS, 2, P])
        carry = sb("carry", [2 * HEADS, 2, P + 1])
        start = sb("start", [P, 16])
        allc = sb("allc", [P, 2])
        totB = sb("totB", [NT, 1])

        ps = [ctx.enter_context(nc.psum_tensor(f"ps{i}", [P, 512], F32)) for i in range(8)]
        ps_t = [ps[0][:, PN * s:PN * s + PN] for s in range(2)]
        ps_h = [ps[1 + m][:, 0:PN] for m in range(4)]
        ps_y = [ps[5 + s][0:TN, 0:TP * P].rearrange("p (t f) -> p t f", t=TP) for s in range(2)]
        ps_b = [ps[5 + s][:, 0:PN] for s in range(2)]
        ps_z = [ps[5 + s][0:TN, 0:TP * 2 * P].rearrange("p (t k f) -> p t k f", t=TP, k=2) for s in range(2)]
        ps_a = [ps[4 + i][:, 0:HEADS * W] for i in range(RING)]
        ps_n = [ps[4 + i][0:1 + HEADS, 128:128 + W] for i in range(RING)]
        ps_x = ps[0][:, 0:HEADS * W]
        ps_xn = ps[0][0:1 + HEADS, 128:128 + W]
        ps_m = ps[7]
        ps_v = [ps[7][0:TN, 16 * s:16 * s + TP * 2 * HEADS].rearrange("p (t k) -> p t k", t=TP) for s in range(2)]
        ps_l = [[ps[1 + 2 * s + k][0:TN, 0:HEADS * P] for k in range(TP)] for s in range(2)]

        filled = sem("filled")
        w_in = sem("w_in")
        consts = sem("consts")
        dsts_in = sem("dsts_in")
        dve_step = sem("dve_step")
        prep_pe = sem("prep_pe")
        prep_dve = sem("prep_dve")
        rows_loaded = sems("rows_loaded", RING)
        rows_landed = sems("rows_landed", RING)
        idx_landed = sems("idx_landed", RING)
        ea_landed = sems("ea_landed", RING)
        att_landed = sems("att_landed", RING)
        xe_stored = sems("xe_stored", RING)
        as_stored = sems("as_stored", RING)
        onehot_ready = sem("onehot_ready")
        weighted_ready = sem("weighted_ready")
        scores_ready = sem("scores_ready")
        prod_ready = sem("prod_ready")
        group_summed = sem("group_summed")
        psum_free = sem("psum_free")
        x_onehot = sem("x_onehot")
        x_summed = sem("x_summed")
        x_added = sem("x_added")
        asum_ready = sem("asum_ready")
        push_zeroed = sem("push_zeroed")
        pushed = sem("pushed")
        sums_out = sem("sums_out")
        sums_in = sem("sums_in")
        rc_out = sem("rc_out")
        rc_in = sem("rc_in")
        scan_in = sem("scan_in")
        scan_pe = sem("scan_pe")
        scan_dve = sem("scan_dve")
        scan_act = sem("scan_act")
        scan_out = sem("scan_out")
        wl_in = sem("wl_in")
        tail_in = sem("tail_in")
        ea_tail = sem("ea_tail")
        node_rc = sem("node_rc")
        node_dve = sem("node_dve")
        node_pe = sem("node_pe")
        dst_ready = sem("dst_ready")
        bn_var = sem("bn_var")
        bn_root = sem("bn_root")
        bn_ready = sem("bn_ready")
        x_iota = sem("x_iota")
        x_wrap = sem("x_wrap")
        scan_exp = sem("scan_exp")
        scan_done = sem("scan_done")

        root = sem("root")

        class Stage:

            def __init__(self, name, kinds):
                def of(kind):
                    return sem(f"{name}_{kind}") if kind in kinds.split() else None

                self.x = sems(f"{name}_x_landed", 2) if "x" in kinds.split() else None
                self.stored = sems(f"{name}_stored", 2) if "stored" in kinds.split() else None
                self.T = of("T")
                self.xT = of("xT")
                self.a = of("a")
                self.H = of("H")
                self.h = of("h")
                self.Y = of("Y")
                self.step = of("step")
                self.done = of("done")

        d0 = Stage("d0", "x stored T xT H h Y step done")
        d1a = Stage("d1a", "x T a H h done")
        d1b = Stage("d1b", "xT h Y done")
        d1c = Stage("d1c", "x stored xT Y step done")
        d2a = Stage("d2a", "x stored T xT a H h Y done")
        d2b = Stage("d2b", "x stored T xT a H h Y step done")
        d3 = Stage("d3", "x stored T xT a Y step done")

        L0, G1, G2A, G2B, C3 = range(5)
        GATHERS = {G1: 0, G2A: 1, G2B: 2}
        A3 = 3
        LEAD = 2
        SUMMED = lambda a: a * NG
        ONEHOTS = lambda a: a * (NG + LEAD)
        FREED = lambda a: RING + a * NG
        LANDED = lambda k: 16 * NIT * CH * k

        def arrived(a, i, u):
            if a in GATHERS:
                return rows_landed[i], LANDED(GATHERS[a]) + 16 * CH * (u + 1)
            return rows_loaded[i], 16 * ((NIT if a == C3 else 0) + u + 1)

        def pairs(eng, body):
            body(0, 0, 0, True)
            body(1, 0, 1, True)
            with eng.Fori(1, NP // 2) as u:
                body(2 * u, u, 0, False)
                body(2 * u + 1, u, 1, False)
            body(NP - 1, NP // 2, 0, False)

        def tiles_of(a, q, width=P):
            return a.rearrange("(q t p) f -> p q t f", t=TP, p=TN)[:, bass.ds(q, 1), :, 0:width]

        def blk(a, q):
            return a[:, bass.ds(PN * q, PN)]

        def group_of(a, g, width):
            return a.rearrange("(g p c) f -> p g (c f)", p=P, c=CH)[:, bass.ds(g, 1), :]

        def planes(at, n):
            return wide_f[:, at * EPP:(at + n) * EPP].rearrange("p (h j) -> p h j", j=EPP)

        PU = wide_f[:, 0:2 * HEADS * EPP]
        AL, XLP = planes(0, HEADS), planes(HEADS, HEADS)
        AS = wide_f[:, 2 * HEADS * EPP:3 * HEADS * EPP]
        EXP_ = planes(2 * HEADS, HEADS)
        FW, BW = planes(3 * HEADS, HEADS), planes(4 * HEADS, HEADS)
        FILLP = planes(3 * HEADS, 2 * HEADS)
        EX = wide_f[:, 3 * HEADS * EPP:4 * HEADS * EPP]
        XL = wide_f[:, 0:HEADS * EPP]
        DI = [wide_f[:, (5 * HEADS + n) * EPP:(5 * HEADS + n + 1) * EPP].bitcast(I32) for n in range(3)]
        CF, CB, NF, NB = (wide_f[:, (6 * HEADS + n) * EPP:(6 * HEADS + n + 1) * EPP] for n in range(4))
        SCANS = ((2 * HEADS, 1), (HEADS, 2), (HEADS, 2))
        STEPS3 = 1 + TP * HEADS + 6 + 3 + 5
        CONSTS = 16
        w_loads = Count()
        wloop_f = wloop[:, :, :].rearrange("p j h -> p (j h)")

        block = ctx.enter_context(nc.Block())

        @block.sync
        def _(sp):
            sp.wait_ge(consts, 3)
            sp.dma_start(src_d[0:E].unsqueeze(0), t["src"].unsqueeze(0)).then_inc(filled, 16)
            sp.dma_start(src_d[E:EP].unsqueeze(0), fill_i[:, 0:EP - E]).then_inc(filled, 16)
            sp.dma_start(dst_d[1:1 + E].unsqueeze(0), t["dst"].unsqueeze(0)).then_inc(filled, 16)
            sp.dma_start(dst_d[1 + E:2 + EP].unsqueeze(0), mark_i[:, 1:2 + EP - E]).then_inc(filled, 16)
            sp.dma_start(dst_d[0:1].unsqueeze(0), mark_i[:, 0:1]).then_inc(filled, 16)

            ea0 = t["edge_attr_128"]

            def load_edges(g, i):
                sp.dma_start(rows[:, i:i + 1, :, 0:P],
                             ea0[0:FULL * GE, :].rearrange("(g p c) f -> p g c f", p=P, c=CH)[:, bass.ds(g, 1), :, :]
                             ).then_inc(rows_loaded[i], 16)

            sp.wait_ge(consts, 4)
            for i in range(RING):
                load_edges(i, i)
                if i == 1:
                    sp.wait_ge(filled, 80)
                    sp.dma_start(dst_i.rearrange("p (g c) -> p g c", c=CH),
                                 dst_d[1:1 + EP].rearrange("(g p c) -> p g c", p=P, c=CH)).then_inc(dsts_in, 16)
                    first = dst_d[1:1 + EP].rearrange("(g e) -> g e", e=GE)[:, 0:1].rearrange("g e -> e g")
                    with nc.allow_non_contiguous_dma(reason="one word of each group"):
                        sp.dma_start(base_i[:, :], first).then_inc(dsts_in, 16)
            with sp.Fori(1, NIT - 1) as u:
                for i in range(RING):
                    sp.wait_ge(group_summed, RING * u + i - RING + 1)
                    load_edges(RING * u + i, i)
            for i in range(RING):
                g = NG - RING + i
                sp.wait_ge(group_summed, g - RING + 1)
                if g < FULL:
                    load_edges(g, i)
                else:
                    sp.dma_start(rows[0:TAIL_P, i, :, 0:P],
                                 ea0[FULL * GE:FULL * GE + TAIL_P * CH, :].rearrange("(p c) f -> p c f", c=CH)
                                 ).then_inc(tail_in, 16)
                    sp.wait_ge(tail_in, 16)
                    sp.dma_start(rows[TAIL_P:TAIL_P + 1, i, 0:TAIL_C, 0:P],
                                 ea0[E - TAIL_C:E, :].unsqueeze(0)).then_inc(rows_loaded[i], 16)

            def load_rows(s_, a, last_store=None):
                def body(q, u, s, first):
                    if not first:
                        sp.wait_ge(s_.done, q - 1)
                    sp.dma_start(xb[:, s:s + 1, :, :], tiles_of(a, q)).then_inc(s_.x[s], 16)
                pairs(sp, body)

            def load_idx(k, g, i):
                sp.dma_start(idx[:, i:i + 1, :], src_d.rearrange("(g p c) -> p g c", p=P, c=CH)[:, bass.ds(g, 1), :]
                             ).then_inc(idx_landed[i], 16)

            def gather_idx(k, a):
                for i in range(RING):
                    sp.wait_ge(group_summed, SUMMED(a))
                    load_idx(k, i, i)
                with sp.Fori(1, NIT) as u:
                    for i in range(RING):
                        sp.wait_ge(group_summed, SUMMED(a) + RING * u + i - RING + 1)
                        load_idx(k, RING * u + i, i)

            def stored(s_, n=1):
                sp.wait_ge(s_.stored[0], 16 * n * (NP // 2 + 1))
                sp.wait_ge(s_.stored[1], 16 * n * (NP // 2))

            load_rows(d0, t["x"])
            gather_idx(GATHERS[G1], G1)
            sp.wait_ge(d0.done, NP)
            stored(d0)
            sp.wait_ge(psum_free, FREED(G1 + 1))
            sp.dma_start(sums_d, nsum[:, 0:N]).then_inc(sums_out, 16)
            sp.wait_ge(sums_out, 16)
            sp.dma_start(cntB[:, :, :], sums_d.rearrange("k (j p) -> j k p", p=TN)).then_inc(sums_in, 16)
            load_rows(d1a, x1_d)
            sp.wait_ge(d1a.done, NP)
            load_rows(d1c, x1_d)
            sp.wait_ge(node_rc, 1)
            sp.dma_start(rcnt_d.rearrange("(j p) -> j p", p=TN), rcB[:, :]).then_inc(rc_out, 16)
            sp.wait_ge(rc_out, 16)
            sp.wait_ge(d1c.done, NP)
            sp.dma_start(rcnt, rcnt_d.unsqueeze(0).to_broadcast([P, N])).then_inc(rc_in, 16)
            gather_idx(GATHERS[G2A], G2A)
            stored(d1c)
            load_rows(d2a, x2_d)
            gather_idx(GATHERS[G2B], G2B)
            sp.wait_ge(d2a.done, NP)
            stored(d2a, 2)
            load_rows(d2b, q_d)

            def store_xe(g, i):
                sp.dma_start(xe_d.rearrange("(g p c) f -> p g c f", p=P, c=CH)[:, bass.ds(g, 1), :, :],
                             rows[:, i:i + 1, :, 0:P]).then_inc(xe_stored[i], 16)

            def next_idx(u, i):
                sp.wait_ge(xe_stored[i], 16 * u)
                load_idx(A3, RING * u + i, i)

            sp.wait_ge(group_summed, SUMMED(C3))
            for i in range(RING):
                load_idx(A3, i, i)
            with sp.Fori(0, NIT - 1) as u:
                for i in range(RING):
                    sp.wait_ge(asum_ready, RING * u + i + 1)
                    store_xe(RING * u + i, i)
                    if i > 0:
                        next_idx(u + 1, i - 1)
                next_idx(u + 1, RING - 1)
            for i in range(RING):
                sp.wait_ge(asum_ready, NG - RING + i + 1)
                store_xe(NG - RING + i, i)
            for i in range(RING):
                sp.wait_ge(xe_stored[i], 16 * NIT)
                sp.wait_ge(as_stored[i], 16 * NIT)

            sp.dma_start(AS, as_d.rearrange("(p j) h -> p (j h)", p=P)).then_inc(scan_in, 16)
            sp.wait_ge(pushed, 16 * NT)
            sp.dma_start(PU, push_d.rearrange("(p j) h -> p (j h)", p=P)).then_inc(scan_in, 16)
            for n in range(3):
                sp.dma_start(DI[n], dst_d[n:n + EP].rearrange("(p j) -> p j", p=P)).then_inc(scan_in, 16)
            sp.wait_ge(scan_done, 1)
            sp.dma_start(at_d.rearrange("(p j) h -> p (j h)", p=P), EX).then_inc(scan_out, 16)
            sp.dma_start(wl_d.rearrange("(p j) h -> p (j h)", p=P), XL).then_inc(scan_out, 16)
            sp.wait_ge(scan_out, 32)

            def load_c3(g, u, i):
                sp.dma_start(rows[:, i:i + 1, :, 0:P],
                             xe_d.rearrange("(g p c) f -> p g c f", p=P, c=CH)[:, bass.ds(g, 1), :, :]
                             ).then_inc(rows_loaded[i], 16)
                sp.dma_start(att[:, i:i + 1, :, :].rearrange("p i c h -> p i (c h)"),
                             group_of(at_d, g, HEADS)).then_inc(att_landed[i], 16)

            for i in range(RING):
                load_c3(i, 0, i)
            with sp.Fori(1, NIT) as u:
                for i in range(RING):
                    sp.wait_ge(group_summed, SUMMED(C3) + RING * u + i - RING + 1)
                    load_c3(RING * u + i, u, i)
            load_rows(d3, t3_d)

        @block.gpsimd
        def _(pool):
            pool.memset(ident[:, :], 0.0).then_inc(consts, 1)
            pool.memset(fill_i[:, :], 0).then_inc(consts, 1)
            pool.memset(mark_i[:, :], NOWHERE).then_inc(consts, 1)
            pool.memset(rows[:, :, :, :], 0.0).then_inc(consts, 1)
            pool.memset(ones[:, :], 1.0).then_inc(consts, 1)
            pool.memset(tri[:, :], 1.0).then_inc(consts, 1)
            pool.iota(iota_w[:, :], pattern=[[1, W]], base=0, channel_multiplier=0,
                      allow_small_or_imprecise_dtypes=True).then_inc(consts, 1)
            pool.wait_ge(consts, 7)
            pool.affine_select(out=ident[:, :], in_=ident[:, :], compare_op=ALU.not_equal, fill=1.0, base=0,
                               pattern=[[-1, P]], channel_multiplier=1).then_inc(consts, 1)
            pool.affine_select(out=tri[:, :], in_=tri[:, :], compare_op=ALU.is_gt, fill=0.0, base=0,
                               pattern=[[1, NT]], channel_multiplier=-1).then_inc(consts, 1)
            pool.memset(one_ae[:, :, :, :], 1.0).then_inc(consts, 1)
            pool.memset(zeros[:, :], 0.0).then_inc(consts, 1)
            pool.memset(nsum[:, :], 0.0).then_inc(consts, 1)
            pool.memset(row2[:, :, :], 0.0).then_inc(consts, 1)
            pool.memset(wloop[:, :, :], 1.0).then_inc(consts, 1)
            pool.memset(yb[:, :, :, :], 0.0).then_inc(consts, 1)
            pool.memset(norm_eps[:, :], NORM_EPS).then_inc(consts, 1)

            def store_rows(s_, jobs):
                def body(q, u, s, first):
                    pool.wait_ge(s_.done, q + 1)
                    for buf, a, width in jobs:
                        pool.dma_start(tiles_of(a, q, width), buf[:, s:s + 1, :, 0:width]).then_inc(s_.stored[s], 16)
                pairs(pool, body)
                pool.wait_ge(s_.stored[0], 16 * len(jobs) * (NP // 2 + 1))
                pool.wait_ge(s_.stored[1], 16 * len(jobs) * (NP // 2))

            idx_next = [pool.alloc_register(f"idx_next{i}") for i in range(RING)]
            for i in range(RING):
                pool.reg_mov(idx_next[i], 16)

            def gather(table, width):
                pool.wait_ge(consts, 4)
                with pool.Fori(0, NIT):
                    for i in range(RING):
                        pool.wait_ge(idx_landed[i], pool.snap(idx_next[i], min_val=16, max_val=1 << 20))
                        pool.reg_add(idx_next[i], idx_next[i], 16)
                        for c in range(CH):
                            pool.indirect_dma_start(
                                out=rows[:, i, c, 0:width], out_offset=None, in_=table,
                                in_offset=bass.IndirectOffsetOnAxis(ap=idx[:, i, c:c + 1], axis=0),
                            ).then_inc(rows_landed[i], 16)

            store_rows(d0, [(yb, x1_d, P)])
            gather(x1_d, P)
            store_rows(d1c, [(yb, x2_d, P)])
            gather(x2_d, P)
            store_rows(d2a, [(yb, z_d, P), (zb, q_d, P)])
            gather(z_d, P)
            store_rows(d2b, [(yb, t3_d, ROW3)])

            pool.wait_ge(push_zeroed, 16 * 2 * HEADS)
            for j in range(NT):
                pool.indirect_dma_start(
                    out=push_d, out_offset=bass.IndirectOffsetOnAxis(ap=beg_i[:, j:j + 1], axis=0),
                    in_=push[:, j, :], in_offset=None, bounds_check=EP - 1, oob_is_err=False).then_inc(pushed, 16)

            gather(t3_d, ROW3)

            pool.wait_ge(scan_out, 32)
            for j in range(NT):
                pool.indirect_dma_start(
                    out=wloop[:, j, :], out_offset=None, in_=wl_d,
                    in_offset=bass.IndirectOffsetOnAxis(ap=end_i[:, j:j + 1], axis=0),
                    bounds_check=EP - 1, oob_is_err=False).then_inc(wl_in, 16)

            def weigh(u, i, first):
                g = RING * u + i
                pool.wait_ge(onehot_ready, ONEHOTS(C3) + g + 1)
                pool.wait_ge(att_landed[i], 16 * (u + 1))
                if not first:
                    pool.wait_ge(group_summed, SUMMED(C3) + g - RING + 1)
                pool.tensor_tensor(weighted[:, i, :, :, :],
                                   onehot[:, i, :, :].unsqueeze(2).to_broadcast([P, CH, HEADS, W]),
                                   att[:, i, :, :].unsqueeze(3).to_broadcast([P, CH, HEADS, W]),
                                   ALU.mult).then_inc(weighted_ready, 1)

            for i in range(RING):
                weigh(0, i, True)
            with pool.Fori(1, NIT) as u:
                for i in range(RING):
                    weigh(u, i, False)

            def store_out(q, u, s, first):
                pool.wait_ge(d3.done, q + 1)
                pool.dma_start(tiles_of(out, q), yb[:, s:s + 1, :, 0:P]).then_inc(d3.stored[s], 16)
            pairs(pool, store_out)
            pool.wait_ge(d3.stored[0], 16 * (NP // 2 + 1))
            pool.wait_ge(d3.stored[1], 16 * (NP // 2))

        @block.scalar
        def _(act):
            def load(dst, src):
                w_loads.up()
                act.dma_start(dst, src).then_inc(w_in, 16)

            def load_col(at, src, n):
                load(col[:, at:at + n], src.rearrange("(m p) -> p m", p=P))

            with nc.allow_non_contiguous_dma(reason="biases by feature"):
                load(w01[:, :, :], t["L0_gnn_W1"].rearrange("(k p) m -> p k m", p=P))
                load(w02[:, :, :], t["L0_gnn_W2"].rearrange("(k p) m -> p k m", p=P))
                load_col(b01, t["L0_gnn_b1"], H0)
                act.wait_ge(consts, CONSTS)
                load(row2[:, 0, :], t["L0_gnn_b2"].unsqueeze(0))
                load(row2[:, 2, :], t["L2_gnn_b2"].unsqueeze(0))
                load(row2[:, 3, :], t["L3_gnn_lin_b"].unsqueeze(0))
                load(w11[:, :], t["L1_gnn_W1"])
                load(w12[:, :, :], t["L1_gnn_W2"].rearrange("(k p) m -> p k m", p=P))
                for at, name, n in ((b11, "L1_gnn_b1", H1), (g11, "L1_gnn_g1", H1), (e11, "L1_gnn_be1", H1),
                                    (b12, "L1_gnn_b2", 1), (g12, "L1_gnn_g2", 1), (e12, "L1_gnn_be2", 1),
                                    (b21, "L2_gnn_b1", H1), (gatb, "L3_gnn_gat_bias", HEADS)):
                    load_col(at, t[name], n)
                load(eps1, t["L1_gnn_eps"].to_broadcast([P, 1]))
                load(w21[:, 0, :], t["L2_gnn_W1_l"])
                load(w21[:, 1, :], t["L2_gnn_W1_r"])
                load(w22[:, :, 0, :], t["L2_gnn_W2_l"].rearrange("(k p) m -> p k m", p=P))
                load(w22[:, :, 1, :], t["L2_gnn_W2_r"].rearrange("(k p) m -> p k m", p=P))
                load(w3[:, :, :].rearrange("p h c -> p (h c)"), t["L3_gnn_W"])
                load(lin[:, :, :], t["L3_gnn_lin_W"].rearrange("(h p) m -> p h m", p=P))
                for n, name in enumerate(("L3_gnn_att_src", "L3_gnn_att_dst")):
                    load(att_b[:, n, :, :].rearrange("p h c -> p (h c)"),
                         t[name].rearrange("h c -> (h c)").unsqueeze(0).to_broadcast([P, HEADS * P]))
                load(we[:, :, :].rearrange("p h c -> p (h c)"), t["L3_gnn_W_edge"])
                load(ae_b[:, :, :].rearrange("p h c -> p (h c)"),
                     t["L3_gnn_att_edge"].rearrange("h c -> (h c)").unsqueeze(0).to_broadcast([EF, HEADS * P]))
                for n, name in enumerate(("L3_gnn_ln_g", "L3_gnn_ln_b")):
                    load(ln_gb[:, n, :], t[name].unsqueeze(0).to_broadcast([TN, P]))
            for k in range(2 * HEADS):
                act.dma_start(push_d.rearrange("(p j) h -> p (j h)", p=P)[:, k * EPP:(k + 1) * EPP], zeros[:, :]
                              ).then_inc(push_zeroed, 16)

            ea16 = t["edge_attr_16"]

            def load_ea(g, i):
                act.dma_start(ea[:, i:i + 1, :, :].rearrange("p i c k -> p i (c k)"),
                              ea16[0:FULL * GE, :].rearrange("(g p c) k -> p g (c k)", p=P, c=CH)[:, bass.ds(g, 1), :]
                              ).then_inc(ea_landed[i], 16)

            def load_ea_tail(i, n):
                act.dma_start(ea[0:TAIL_P, i, :, :],
                              ea16[FULL * GE:FULL * GE + TAIL_P * CH, :].rearrange("(p c) k -> p c k", c=CH)
                              ).then_inc(ea_tail, 16)
                act.wait_ge(ea_tail, 16 * n)
                act.dma_start(ea[TAIL_P:TAIL_P + 1, i, 0:TAIL_C, :], ea16[E - TAIL_C:E, :].unsqueeze(0)
                              ).then_inc(ea_landed[i], 16)

            def deviations(s_, s, steps):
                act.wait_ge(s_.step, steps)
                act.activation(rstd[:, s, :], mv[:, s, :, 1], ACT.Sqrt, bias=norm_eps[0:TN, :]).then_inc(root, 1)

            def relu_rows(s_, n_h, bias, use_slot, before=None):
                def body(q, u, s, first):
                    act.wait_ge(s_.T, q + 1)
                    act.activation(xT[:, s, :], ps_t[s], ACT.Copy).then_inc(s_.xT, 1)
                    if before and not (first and s == 0):
                        before(q - 1, 1 - s)
                    if not first:
                        act.wait_ge(s_.Y, q - 1)
                    for m in range(n_h):
                        act.wait_ge(s_.H, n_h * q + m + 1)
                        act.activation(hT[:, s, m, :], ps_h[2 * s + m if use_slot else m], ACT.Relu,
                                       bias=col[:, bias + m:bias + m + 1]).then_inc(s_.h, 1)
                return body

            act.wait_ge(w_in, 16 * w_loads.n)
            for i in range(RING):
                load_ea(i, i)

            def deviations0(q, s):
                deviations(d0, s, 6 * q + 5)
            pairs(act, relu_rows(d0, H0, b01, False, deviations0))
            deviations0(NP - 1, 0)

            with act.Fori(1, NIT - 1) as u:
                for i in range(RING):
                    act.wait_ge(scores_ready, 1 + RING * u + i - RING + 1)
                    load_ea(RING * u + i, i)
            for i in range(RING):
                g = NG - RING + i
                act.wait_ge(scores_ready, 1 + g - RING + 1)
                if g < FULL:
                    load_ea(g, i)
                else:
                    load_ea_tail(i, 1)

            def hidden1(q, u, s, first):
                for m in range(H1):
                    act.wait_ge(d1a.H, H1 * q + m + 1)
                    act.activation(blk(wide[:, m, :], q), ps_h[2 * s + m], ACT.Identity,
                                   bias=col[:, b11 + m:b11 + m + 1]).then_inc(d1a.h, 1)
            pairs(act, hidden1)

            def norm1(q, u, s, first):
                if not first:
                    act.wait_ge(d1b.Y, q - 1)
                for m in range(H1):
                    act.activation(hT[:, s, m, :], blk(wide[:, m, :], q), ACT.Relu, bias=bns[:, m, 1:2],
                                   scale=bns[:, m, 0:1]).then_inc(d1b.h, 1)
            act.wait_ge(bn_var, 1)
            act.activation(bns[:, 0:H1, 1], bns[:, 0:H1, 1], ACT.Sqrt, bias=norm_eps[:, :]).then_inc(bn_root, 1)
            act.wait_ge(bn_ready, 1)
            pairs(act, norm1)

            def deviations1(q, s):
                deviations(d1c, s, 7 * q + 6)

            def norm2(q, u, s, first):
                if not first:
                    act.wait_ge(d1c.Y, q - 1)
                act.activation(xT[:, s, :], blk(wide[:, 0, :], q), ACT.Identity, bias=bns[:, H1, 1:2],
                               scale=bns[:, H1, 0:1]).then_inc(d1c.xT, 1)
                if not (first and s == 0):
                    deviations1(q - 1, 1 - s)
            act.wait_ge(bn_var, 2)
            act.activation(bns[:, H1, 1:2], bns[:, H1, 1:2], ACT.Sqrt, bias=norm_eps[:, :]).then_inc(bn_root, 1)
            act.wait_ge(bn_ready, 2)
            pairs(act, norm2)
            deviations1(NP - 1, 0)

            pairs(act, relu_rows(d2a, H1, b21, True))

            def x3T(q, u, s, first):
                deviations(d2b, s, 8 * q + 5)
                act.wait_ge(d2b.T, q + 1)
                act.activation(xT[:, s, :], ps_t[s], ACT.Copy).then_inc(d2b.xT, 1)
            pairs(act, x3T)

            act.wait_ge(scores_ready, 1 + NG)
            for i in range(RING):
                load_ea(i, i)

            def store_as(g, i):
                act.wait_ge(asum_ready, g + 1)
                act.dma_start(group_of(as_d, g, HEADS), asum[:, i:i + 1, :, :].rearrange("p i c h -> p i (c h)")
                              ).then_inc(as_stored[i], 16)

            with act.Fori(0, NIT - 2) as u:
                for i in range(RING):
                    store_as(RING * u + i, i)
                    load_ea(RING * (u + 1) + i, i)
            for i in range(RING):
                g = NG - 2 * RING + i
                store_as(g, i)
                if g + RING < FULL:
                    load_ea(g + RING, i)
                else:
                    load_ea_tail(i, 2)
            for i in range(RING):
                store_as(NG - RING + i, i)

            act.wait_ge(scan_exp, 1)
            act.activation(EXP_, EXP_, ACT.Exp).then_inc(scan_act, 1)
            act.wait_ge(scan_exp, 2)
            act.activation(XLP, XLP, ACT.Exp).then_inc(scan_act, 1)

            act.wait_ge(psum_free, FREED(C3 + 1))

            def deviations3(q, s):
                n = STEPS3 * q + 1 + TP * HEADS
                deviations(d3, s, n + 4)
                deviations(d3, s, n + 6 + 3 + 4)

            def operands3(q, u, s, first):
                act.wait_ge(d3.T, q + 1)
                if not first:
                    act.wait_ge(d3.Y, q - 1)
                act.activation(xT[:, s, :], ps_t[s], ACT.Copy).then_inc(d3.xT, 1)
                act.activation(aT[:, s, :, :], wide[:, :, bass.ds(PN * q, PN)], ACT.Copy).then_inc(d3.a, 1)
                if not (first and s == 0):
                    deviations3(q - 1, 1 - s)
            pairs(act, operands3)
            deviations3(NP - 1, 0)

        @block.tensor
        def _(pe):
            extra = pe.alloc_register("pe_extra")
            flag_reg = pe.alloc_register("pe_flag")
            pe.reg_mov(extra, 0)
            meta_f = meta[:, :, :].rearrange("a n k -> a (n k)")

            pe.wait_ge(consts, CONSTS)
            pe.wait_ge(prep_dve, 1)
            pe.matmul(ps_m[:, 0:NG], ones[0:1, 0:P], base_f[:, :], start=True, stop=True).then_inc(prep_pe, 1)
            pe.wait_ge(prep_dve, 2)
            pe.matmul(ps_m[0:1, 256:256 + NIT], ones[:, 0:1], missed[:, :], start=True, stop=True).then_inc(prep_pe, 1)
            pe.wait_ge(dst_ready, 1)

            def sums(a, sums_too=False, weigh=False):
                width = HEADS * W if weigh else W

                def product(i, operand, of_sums, to, to_n, sum_sem):
                    for c in range(CH):
                        mm = pe.matmul(to[:, 0:width], rows[:, i, c, 0:P], operand[c], start=(c == 0), stop=(c == CH - 1))
                    if sums_too:
                        for c in range(CH):
                            mm = pe.matmul(to_n, one_ae[:, i, c, :], of_sums[:, c, :], start=(c == 0), stop=(c == CH - 1))
                    mm.then_inc(sum_sem, 1)

                def operands(of_1, of_w):
                    return [(of_w[:, c, :, :].rearrange("p h w -> p (h w)") if weigh else of_1[:, c, :]) for c in range(CH)]

                with pe.Fori(0, NIT) as u:
                    pe.reg_load(flag_reg, meta_f[0:1, bass.ds((RING + 1) * u + RING, 1)])
                    missing = pe.snap(flag_reg, min_val=0, max_val=CH * RING * P)
                    with pe.If(missing > 0):
                        for i in range(RING):
                            with pe.Fori(0, NK):
                                if sums_too:
                                    pe.wait_ge(scores_ready, 1 + RING * u + i + 1)
                                pe.wait_ge(*arrived(a, i, u))
                                pe.reg_add(extra, extra, 1)
                                pe.wait_ge(x_onehot, pe.snap(extra, min_val=1, max_val=1 << 20))
                                product(i, operands(onehot_x, weighted_x), onehot_x, ps_x, ps_xn, x_summed)
                    for i in range(RING):
                        g = RING * u + i
                        if weigh:
                            pe.wait_ge(weighted_ready, g + 1)
                        else:
                            pe.wait_ge(onehot_ready, ONEHOTS(a) + g + 1)
                        if sums_too:
                            pe.wait_ge(scores_ready, 1 + g + 1)
                        pe.wait_ge(*arrived(a, i, u))
                        pe.wait_ge(psum_free, SUMMED(a) + g + 1)
                        product(i, operands(onehot[:, i, :, :], weighted[:, i, :, :, :]), onehot[:, i, :, :],
                                ps_a[i], ps_n[i], group_summed)
                pe.wait_ge(psum_free, FREED(a + 1))

            def transpose_rows(s_, q, u, s):
                pe.wait_ge(s_.x[s], 16 * (u + 1))
                for k in range(TP):
                    mm = pe.transpose(ps_t[s][:, TN * k:TN * (k + 1)], xb[:, s, k, :], ident[0:TN, 0:TN])
                mm.then_inc(s_.T, 1)

            sums(L0)
            pe.wait_ge(w_in, 16 * w_loads.n)

            def layer0(q, u, s, first):
                transpose_rows(d0, q, u, s)
                pe.wait_ge(d0.xT, q + 1)
                for m in range(H0):
                    if not (first and s == 0):
                        pe.wait_ge(d0.h, H0 * (q - 1) + m + 1)
                    pe.matmul(ps_h[m], w01[:, 0, m * P:(m + 1) * P], blk(wide[:, 2, :], q), start=True, stop=False)
                    pe.matmul(ps_h[m], w01[:, 1, m * P:(m + 1) * P], xT[:, s, :], start=False, stop=True).then_inc(d0.H, 1)
                pe.wait_ge(d0.h, H0 * (q + 1))
                if not first:
                    pe.wait_ge(d0.done, q - 1)
                for k in range(TP):
                    for m in range(H0):
                        pe.matmul(ps_y[s][:, k, :], hT[:, s, m, TN * k:TN * (k + 1)], w02[:, m, :], start=(m == 0), stop=False)
                    mm = pe.matmul(ps_y[s][:, k, :], ones[0:1, 0:TN], row2[:, 0, :], start=False, stop=True)
                mm.then_inc(d0.Y, 1)
            pairs(pe, layer0)

            pe.wait_ge(prep_dve, 3)
            pe.matmul(ps_m[:, 0:HEADS * EF], ones[0:EF, 0:P], we_d[:, :, :].rearrange("k h e -> k (h e)"),
                      start=True, stop=True).then_inc(prep_pe, 1)
            for h in range(HEADS):
                mm = pe.transpose(ps[6][:, h * P:(h + 1) * P], w3[:, h, :], ident[:, :])
            mm.then_inc(prep_pe, 1)
            pe.wait_ge(prep_dve, 5)
            for h in range(HEADS):
                mm = pe.matmul(ps[6][:, h * P:(h + 1) * P], w3T[:, h, :], lin[:, h, :], start=True, stop=True)
            mm.then_inc(prep_pe, 1)
            for h in range(HEADS):
                mm = pe.matmul(ps_m[0:1, 256:256 + P], col[:, gatb + h:gatb + h + 1], lin[:, h, :],
                               start=(h == 0), stop=(h == HEADS - 1))
            mm.then_inc(prep_pe, 1)
            pe.wait_ge(prep_dve, 7)

            sums(G1, sums_too=True)

            def layer1(q, u, s, first):
                transpose_rows(d1a, q, u, s)
                pe.wait_ge(d1a.a, q + 1)
                if not first:
                    pe.wait_ge(d1a.h, H1 * (q - 1))
                for m in range(H1):
                    pe.matmul(ps_h[2 * s + m], w11[:, m * P:(m + 1) * P], aT[:, s, 0, :], start=True, stop=True).then_inc(d1a.H, 1)
            pairs(pe, layer1)

            def layer1b(q, u, s, first):
                pe.wait_ge(d1b.h, H1 * (q + 1))
                if not first:
                    pe.wait_ge(d1b.xT, q - 1)
                for m in range(H1):
                    mm = pe.matmul(ps_b[s], w12[:, m, :], hT[:, s, m, :], start=(m == 0), stop=(m == H1 - 1))
                mm.then_inc(d1b.Y, 1)
            pairs(pe, layer1b)

            def layer1c(q, u, s, first):
                pe.wait_ge(d1c.xT, q + 1)
                if not first:
                    pe.wait_ge(d1c.done, q - 1)
                for k in range(TP):
                    mm = pe.transpose(ps_y[s][:, k, :], xT[:, s, TN * k:TN * (k + 1)], ident[:, :])
                mm.then_inc(d1c.Y, 1)
            pairs(pe, layer1c)

            pe.wait_ge(node_dve, 1)
            pe.matmul(ps_m[0:NT, 0:1], tri[:, :], totB[:, :], start=True, stop=True).then_inc(node_pe, 1)
            pe.wait_ge(node_dve, 2)
            for n, a in enumerate((begB[:, :], endB[:, :], *(meanB[:, h, :] for h in range(HEADS)))):
                mm = pe.transpose(ps_m[0:TN, 64 + n * NT:64 + (n + 1) * NT], a, ident[0:NT, 0:NT])
            mm.then_inc(node_pe, 1)
            pe.wait_ge(node_dve, 3)

            sums(G2A)

            def layer2(q, u, s, first):
                transpose_rows(d2a, q, u, s)
                pe.wait_ge(d2a.xT, q + 1)
                pe.wait_ge(d2a.a, q + 1)
                if not first:
                    pe.wait_ge(d2a.h, H1 * (q - 1))
                for m in range(H1):
                    pe.matmul(ps_h[2 * s + m], w21[:, 0, m * P:(m + 1) * P], aT[:, s, 0, :], start=True, stop=False)
                    pe.matmul(ps_h[2 * s + m], w21[:, 1, m * P:(m + 1) * P], xT[:, s, :], start=False, stop=True).then_inc(d2a.H, 1)
                pe.wait_ge(d2a.h, H1 * (q + 1))
                if not first:
                    pe.wait_ge(d2a.done, q - 1)
                for k in range(TP):
                    to = ps_z[s][:, k, :, :].rearrange("p k f -> p (k f)")
                    for m in range(H1):
                        pe.matmul(to, hT[:, s, m, TN * k:TN * (k + 1)], w22[:, m, :, :].rearrange("p k f -> p (k f)"),
                                  start=(m == 0), stop=False)
                    mm = pe.matmul(to, ones[0:1, 0:TN], row2[:, 1:3, :].rearrange("p k f -> p (k f)"), start=False, stop=True)
                mm.then_inc(d2a.Y, 1)
            pairs(pe, layer2)
            pe.wait_ge(d2a.done, NP)

            sums(G2B)

            def layer2b(q, u, s, first):
                pe.wait_ge(d2b.a, q + 1)
                if not first:
                    pe.wait_ge(d2b.done, q - 1)
                for k in range(TP):
                    mm = pe.transpose(ps_y[s][:, k, :], aT[:, s, 0, TN * k:TN * (k + 1)], ident[:, :])
                mm.then_inc(d2b.Y, 1)
                pe.wait_ge(d2b.h, q + 1)
                for k in range(TP):
                    mm = pe.transpose(ps_t[s][:, TN * k:TN * (k + 1)], yb[:, s, k, 0:P], ident[0:TN, 0:TN])
                mm.then_inc(d2b.T, 1)
                pe.wait_ge(d2b.xT, q + 1)
                for k in range(TP):
                    mm = pe.matmul(ps_v[s][:, k, :], xT[:, s, TN * k:TN * (k + 1)], v6[:, :], start=True, stop=True)
                mm.then_inc(d2b.H, 1)
            pairs(pe, layer2b)

            for k, (n, dirs) in enumerate(SCANS):
                pe.wait_ge(scan_dve, 2 * k + 1)
                for d in range(dirs):
                    pe.transpose(ps_m[0:n, 2 * d * P:(2 * d + 1) * P], ends[:, d, 0, 0:n], ident[:, :])
                    mm = pe.transpose(ps_m[0:n, (2 * d + 1) * P:(2 * d + 2) * P], ends[:, d, 1, 0:n], ident[:, :])
                mm.then_inc(scan_pe, 1)
                pe.wait_ge(scan_dve, 2 * k + 2)
                for d in range(dirs):
                    mm = pe.transpose(ps[6][:, 8 * d:8 * d + n], carry[0:n, d, d:d + P], ident[0:n, 0:n])
                mm.then_inc(scan_pe, 1)

            sums(C3, weigh=True)

            def layer3(q, u, s, first):
                transpose_rows(d3, q, u, s)
                pe.wait_ge(d3.xT, q + 1)
                pe.wait_ge(d3.a, q + 1)
                if not first:
                    pe.wait_ge(d3.step, STEPS3 * (q - 2) + 1 + TP * HEADS)
                for k in range(TP):
                    pe.matmul(ps_l[s][k], xT[:, s, TN * k:TN * (k + 1)], fused3[:, :, :].rearrange("p h f -> p (h f)"),
                              start=True, stop=True)
                    for h in range(HEADS):
                        pe.matmul(ps_y[s][:, k, :], aT[:, s, h, TN * k:TN * (k + 1)], fused3[:, h, :], start=(h == 0), stop=False)
                    mm = pe.matmul(ps_y[s][:, k, :], ones[0:1, 0:TN], row2[:, 3, :], start=False, stop=True)
                mm.then_inc(d3.Y, 1)
            pairs(pe, layer3)

        @block.vector
        def _(v):
            extra = v.alloc_register("dve_extra")
            v.reg_mov(extra, 0)
            norms = v.alloc_register("dve_norms")
            v.reg_mov(norms, 0)
            v.memset(prod[:, :, :, :, :], 0.0).then_inc(scores_ready, 1)
            regs = [v.alloc_register(f"dve_meta{i}") for i in range(RING + 1)]
            meta_f = meta[:, :, :].rearrange("a n k -> a (n k)")
            NE = NG * CH
            tmp = [wide_f[:, i * NE:(i + 1) * NE] for i in range(4)]
            step = Count()

            for i in range(RING):
                v.memset(dst_rel[:, NE + CH * i:NE + CH * (i + 1)], -1.0).then_inc(psum_free, 1)
            v.wait_ge(dsts_in, 32)
            v.tensor_copy(base_f[:, :], base_i[:, :]).then_inc(prep_dve, 1)
            v.tensor_copy(tmp[0], dst_i).then_inc(dve_step, step.up())
            v.tensor_copy(meta[:, :, 0:RING], base_i[:, :].rearrange("a (n k) -> a n k", k=RING)).then_inc(dve_step, step.up())
            v.wait_ge(dve_step, step.n)
            v.wait_ge(prep_pe, 1)
            v.tensor_tensor(dst_rel[:, 0:NE].rearrange("p (g c) -> p g c", c=CH),
                            tmp[0].rearrange("p (g c) -> p g c", c=CH),
                            ps_m[:, 0:NG].unsqueeze(2).to_broadcast([P, NG, CH]), ALU.subtract).then_inc(dve_step, step.up())
            v.wait_ge(dve_step, step.n)
            v.tensor_scalar(tmp[1], dst_rel[:, 0:NE], 0.0, float(W - 1), ALU.max, ALU.min).then_inc(dve_step, step.up())
            v.wait_ge(dve_step, step.n)
            v.tensor_tensor(tmp[2], tmp[1], dst_rel[:, 0:NE], ALU.not_equal).then_inc(dve_step, step.up())
            v.wait_ge(dve_step, step.n)
            v.scalar_tensor_tensor(tmp[1], tmp[0], 1.0, tmp[2], ALU.add, ALU.mult).then_inc(dve_step, step.up())
            v.scalar_tensor_tensor(tmp[3], tmp[0], float(N), tmp[2], ALU.is_lt, ALU.mult).then_inc(dve_step, step.up())
            v.wait_ge(dve_step, step.n)
            v.tensor_scalar(dst_left[:, :], tmp[1], -1.0, None, ALU.add).then_inc(dve_step, step.up())
            v.tensor_reduce(missed[:, :], tmp[3].rearrange("p (n k) -> p n k", n=NIT), AX.X, ALU.add).then_inc(prep_dve, 1)
            v.wait_ge(prep_pe, 2)
            v.tensor_copy(meta[:, :, RING], ps_m[0:1, 256:256 + NIT]).then_inc(dst_ready, 1)
            v.wait_ge(dst_ready, 1)
            v.wait_ge(dve_step, step.n)
            v.wait_ge(consts, CONSTS)
            v.tensor_copy(iota_x[:, :], iota_w[:, :]).then_inc(x_iota, 1)

            def scores(k, u):
                n = NG * k + RING * u
                v.wait_ge(scores_ready, 1 + n)
                for i in range(RING):
                    v.wait_ge(ea_landed[i], 16 * (NIT * k + u + 1))
                    v.tensor_tensor(prod[:, i, :, :, :], ea[:, i, :, :].unsqueeze(2).to_broadcast([P, CH, HEADS, EF]),
                                    we_b[:, :, :].unsqueeze(1).to_broadcast([P, CH, HEADS, EF]), ALU.mult).then_inc(prod_ready, 1)
                for i in range(RING):
                    v.wait_ge(prod_ready, n + i + 1)
                    v.tensor_reduce(one_ae[:, i, :, 1:1 + HEADS], prod[:, i, :, :, :], AX.X, ALU.add).then_inc(scores_ready, 1)

            def sums(a, sums_too=False, weigh=False):
                def make(g, i):
                    v.tensor_tensor(onehot[:, i, :, :],
                                    dst_rel[:, bass.ds(CH * g, CH)].unsqueeze(2).to_broadcast([P, CH, W]),
                                    iota_w[:, :].unsqueeze(1).to_broadcast([P, CH, W]), ALU.is_equal).then_inc(onehot_ready, 1)

                def add(base, frm, frm_n, done):
                    if sums_too:
                        part = nsum[:, bass.ds(base, W)]
                        v.tensor_tensor(part, part, frm_n, ALU.add)
                    acc = wide[:, :, bass.ds(base, W)] if weigh else wide[:, 2, bass.ds(base, W)]
                    frm = frm.rearrange("p (h w) -> p h w", w=W) if weigh else frm[:, 0:W]
                    v.tensor_tensor(acc, acc, frm, ALU.add).then_inc(done, 1)

                if weigh:
                    v.memset(wide[:, :, :], 0.0).then_inc(dve_step, step.up())
                else:
                    v.memset(wide[:, 2, :], 0.0).then_inc(dve_step, step.up())
                for g in range(LEAD):
                    make(g, g)
                v.wait_ge(dve_step, step.n)
                with v.Fori(0, NIT) as u:
                    v.reg_load(regs, meta_f[0:1, bass.ds((RING + 1) * u, RING + 1)])
                    bases = [v.snap(r, min_val=0, max_val=N - 1) for r in regs[:RING]]
                    missing = v.snap(regs[RING], min_val=0, max_val=CH * RING * P)
                    if sums_too:
                        scores(0, u)
                    with v.If(missing > 0):
                        for i in range(RING):
                            g = RING * u + i
                            with v.Fori(0, NK) as k:
                                if weigh:
                                    v.wait_ge(att_landed[i], 16 * (u + 1))
                                v.wait_ge(psum_free, FREED(a) + RING * u)
                                v.reg_add(extra, extra, 1)
                                n = v.snap(extra, min_val=1, max_val=1 << 20)
                                v.wait_ge(x_iota, n)
                                if weigh:
                                    for c in range(CH):
                                        for h in range(HEADS):
                                            op = v.tensor_scalar(weighted_x[:, c, h, :], iota_x[:, :],
                                                                 dst_left[:, bass.ds(CH * g + c, 1)], att[:, i, c, h:h + 1],
                                                                 ALU.is_equal, ALU.mult)
                                    op.then_inc(x_onehot, 1)
                                else:
                                    v.tensor_tensor(onehot_x[:, :, :],
                                                    dst_left[:, bass.ds(CH * g, CH)].unsqueeze(2).to_broadcast([P, CH, W]),
                                                    iota_x[:, :].unsqueeze(1).to_broadcast([P, CH, W]), ALU.is_equal
                                                    ).then_inc(x_onehot, 1)
                                v.wait_ge(x_onehot, n)
                                v.tensor_scalar(wrap_x[:, :], iota_x[:, :], float((NK - 1) * W), float(-NK * W), ALU.is_ge, ALU.mult
                                                ).then_inc(x_wrap, 1)
                                v.wait_ge(x_wrap, n)
                                v.scalar_tensor_tensor(iota_x[:, :], iota_x[:, :], float(W), wrap_x[:, :], ALU.add, ALU.add
                                                       ).then_inc(x_iota, 1)
                                v.wait_ge(x_summed, n)
                                add(W * k, ps_x, ps_xn, x_added)
                                v.wait_ge(x_added, n)
                    for i in range(RING):
                        g = RING * u + i
                        make(g + LEAD, (i + LEAD) % RING)
                        v.wait_ge(group_summed, SUMMED(a) + g + 1)
                        v.wait_ge(psum_free, FREED(a) + g)
                        add(bases[i], ps_a[i], ps_n[i], psum_free)
                v.wait_ge(psum_free, FREED(a + 1))

            def layer_norm(s_, s, n, r, o, last):
                for k in range(TP):
                    v.bn_stats(st[:, s, k, :], r[:, s, k, :]).then_inc(s_.step, 1)
                v.wait_ge(s_.step, n + 2)
                v.reg_add(norms, norms, 1)
                for k in range(TP):
                    v.bn_aggr(mv[:, s, k, :], st[:, s, k, :]).then_inc(s_.step, 1)
                v.wait_ge(root, v.snap(norms, min_val=1, max_val=1 << 20))
                v.reciprocal(rstd[:, s, :], rstd[:, s, :]).then_inc(s_.step, 1)
                v.wait_ge(s_.step, n + 5)
                for k in range(TP):
                    op = v.tensor_scalar(o[:, s, k, 0:P], r[:, s, k, :], mv[:, s, k, 0:1], rstd[:, s, k:k + 1],
                                         ALU.subtract, ALU.mult)
                op.then_inc(last, 1)

            sums(L0)

            def layer0(q, u, s, first):
                n = 6 * q
                v.wait_ge(d0.Y, q + 1)
                v.tensor_tensor(rb[:, s, :, :], ps_y[s], xb[:, s, :, :], ALU.add).then_inc(d0.step, 1)
                v.wait_ge(d0.step, n + 1)
                if not first:
                    v.wait_ge(d0.stored[s], 16 * u)
                layer_norm(d0, s, n + 1, rb, yb, d0.done)
            pairs(v, layer0)

            v.wait_ge(w_in, 16 * w_loads.n)
            hT_f = hT[:, 0, :, :].rearrange("p m n -> p (m n)")
            hw = HEADS * P
            part = [hT_f[:, 0:hw], hT_f[:, hw:2 * hw]]
            part_e = hT[0:EF, 1, :, :].rearrange("p m n -> p (m n)")[:, 0:hw]
            for n in range(2):
                v.tensor_tensor(part[n], w3[:, :, :].rearrange("p h c -> p (h c)"),
                                att_b[:, n, :, :].rearrange("p h c -> p (h c)"), ALU.mult).then_inc(dve_step, step.up())
            v.tensor_tensor(part_e, we[:, :, :].rearrange("p h c -> p (h c)"),
                            ae_b[:, :, :].rearrange("p h c -> p (h c)"), ALU.mult).then_inc(dve_step, step.up())
            v.wait_ge(dve_step, step.n)
            for n in range(2):
                v.tensor_reduce(v6[:, HEADS * n:HEADS * (n + 1)], part[n].rearrange("p (h c) -> p h c", c=P), AX.X, ALU.add)
            v.tensor_reduce(we3[:, :], part_e.rearrange("p (h c) -> p h c", c=P), AX.X, ALU.add).then_inc(dve_step, step.up())
            v.tensor_scalar(eps1, eps1, 1.0, None, ALU.add).then_inc(dve_step, step.up())
            v.wait_ge(dve_step, step.n)
            v.tensor_tensor(we_d[:, :, :], ident[0:EF, 0:EF].unsqueeze(1).to_broadcast([EF, HEADS, EF]),
                            we3[:, :].unsqueeze(2).to_broadcast([EF, HEADS, EF]), ALU.mult).then_inc(prep_dve, 1)
            v.wait_ge(prep_pe, 3)
            v.tensor_copy(we_b[:, :, :], ps_m[:, 0:HEADS * EF].rearrange("p (h e) -> p h e", e=EF)).then_inc(prep_dve, 1)
            v.wait_ge(prep_pe, 4)
            v.tensor_copy(w3T[:, :, :], ps[6][:, 0:hw].rearrange("p (h c) -> p h c", c=P)).then_inc(prep_dve, 1)
            v.wait_ge(prep_pe, 5)
            v.tensor_copy(fused3[:, :, :], ps[6][:, 0:hw].rearrange("p (h c) -> p h c", c=P)).then_inc(prep_dve, 1)
            v.wait_ge(prep_pe, 6)
            v.tensor_tensor(row2[:, 3, :], row2[:, 3, :], ps_m[0:1, 256:256 + P], ALU.add).then_inc(prep_dve, 1)
            v.wait_ge(prep_dve, 7)

            sums(G1, sums_too=True)

            def stats1(q):
                v.wait_ge(d1a.h, H1 * (q + 1))
                for m in range(H1):
                    op = v.bn_stats(bn1[:, m, bass.ds(q, 1), :], blk(wide[:, m, :], q))
                op.then_inc(d1a.done, 1)

            def layer1(q, u, s, first):
                v.wait_ge(d1a.T, q + 1)
                if not first:
                    v.wait_ge(d1a.H, H1 * (q - 1))
                v.scalar_tensor_tensor(aT[:, s, 0, :], ps_t[s], eps1, blk(wide[:, 2, :], q), ALU.mult, ALU.add
                                       ).then_inc(d1a.a, 1)
                if not (first and s == 0):
                    stats1(q - 1)
            pairs(v, layer1)
            stats1(NP - 1)
            v.wait_ge(d1a.done, NP)

            def norm(lo, hi, frm, g, e):
                for m in range(lo, hi):
                    v.bn_aggr(bnm[:, m, :], frm[m - lo]).then_inc(dve_step, step.up())
                v.wait_ge(dve_step, step.n)
                v.tensor_copy(bns[:, lo:hi, 1], bnm[:, lo:hi, 1]).then_inc(bn_var, 1)
                v.wait_ge(bn_root, 1 if lo == 0 else 2)
                v.reciprocal(bns[:, lo:hi, 0], bns[:, lo:hi, 1]).then_inc(dve_step, step.up())
                v.wait_ge(dve_step, step.n)
                v.tensor_tensor(bns[:, lo:hi, 0], bns[:, lo:hi, 0], col[:, g:g + hi - lo], ALU.mult).then_inc(dve_step, step.up())
                v.wait_ge(dve_step, step.n)
                v.tensor_tensor(bnm[:, lo:hi, 0], bnm[:, lo:hi, 0], bns[:, lo:hi, 0], ALU.mult).then_inc(dve_step, step.up())
                v.wait_ge(dve_step, step.n)
                v.tensor_tensor(bns[:, lo:hi, 1], col[:, e:e + hi - lo], bnm[:, lo:hi, 0], ALU.subtract).then_inc(bn_ready, 1)

            norm(0, H1, [bn1[:, m, :, :].rearrange("p q k -> p (q k)") for m in range(H1)], g11, e11)

            def stats2(q, u, s, first):
                v.wait_ge(d1b.Y, q + 1)
                v.tensor_scalar(blk(wide[:, 0, :], q), ps_b[s], col[:, b12:b12 + 1], None, ALU.add).then_inc(d1b.xT, 1)
                v.wait_ge(d1b.xT, q + 1)
                v.bn_stats(bn2[:, bass.ds(q, 1), :], blk(wide[:, 0, :], q)).then_inc(d1b.done, 1)
            pairs(v, stats2)
            v.wait_ge(d1b.done, NP)
            norm(H1, H1 + 1, [bn2[:, :, :].rearrange("p q k -> p (q k)")], g12, e12)

            def layer1c(q, u, s, first):
                n = 7 * q
                v.wait_ge(d1c.Y, q + 1)
                v.wait_ge(d1c.x[s], 16 * (u + 1))
                v.tensor_tensor(rb[:, s, :, :], ps_y[s], xb[:, s, :, :], ALU.add).then_inc(d1c.step, 1)
                v.wait_ge(d1c.step, n + 1)
                v.scalar_tensor_tensor(ub[:, s, :, :], rb[:, s, :, :], 0.0, xb[:, s, :, :], ALU.max, ALU.add).then_inc(d1c.step, 1)
                v.wait_ge(d1c.step, n + 2)
                if not first:
                    v.wait_ge(d1c.stored[s], 16 * u)
                layer_norm(d1c, s, n + 2, ub, yb, d1c.done)
            pairs(v, layer1c)

            v.wait_ge(sums_in, 16)
            cnt = cntB[:, 0, :]
            v.tensor_tensor_scan(endB[:, :], ones[0:NT, 0:TN], cnt, 0.0, ALU.mult, ALU.add).then_inc(dve_step, step.up())
            v.tensor_scalar(rcB[:, :], cnt, 1.0, None, ALU.max).then_inc(dve_step, step.up())
            v.wait_ge(dve_step, step.n)
            v.tensor_copy(totB[:, :], endB[:, TN - 1:TN]).then_inc(node_dve, 1)
            v.reciprocal(rcB[:, :], rcB[:, :]).then_inc(node_rc, 1)
            v.wait_ge(node_rc, 1)
            v.tensor_tensor(meanB[:, :, :], cntB[:, 1:1 + HEADS, :], rcB[:, :].unsqueeze(1).to_broadcast([NT, HEADS, TN]),
                            ALU.mult).then_inc(dve_step, step.up())
            v.tensor_scalar(begB[:, :], cnt, 0.0, float(4 * EP), ALU.is_equal, ALU.mult).then_inc(dve_step, step.up())
            v.wait_ge(node_pe, 1)
            v.tensor_copy(carB[:, :], ps_m[0:NT, 0:1]).then_inc(dve_step, step.up())
            v.wait_ge(dve_step, step.n)
            v.scalar_tensor_tensor(endB[:, :], endB[:, :], carB[:, 0:1], begB[:, :], ALU.add, ALU.add).then_inc(dve_step, step.up())
            v.wait_ge(dve_step, step.n)
            v.tensor_tensor(begB[:, :], endB[:, :], cnt, ALU.subtract).then_inc(dve_step, step.up())
            v.wait_ge(dve_step, step.n)
            v.tensor_scalar(endB[:, :], endB[:, :], -1.0, None, ALU.add).then_inc(node_dve, 1)
            v.wait_ge(node_pe, 2)
            v.tensor_copy(beg_i[:, :], ps_m[0:TN, 64:64 + NT])
            v.tensor_copy(end_i[:, :], ps_m[0:TN, 64 + NT:64 + 2 * NT])
            v.tensor_copy(amean[:, :, :], ps_m[0:TN, 64 + 2 * NT:64 + (2 + HEADS) * NT].rearrange("p (h j) -> p j h", h=HEADS)
                          ).then_inc(node_dve, 1)
            v.wait_ge(node_dve, 3)

            sums(G2A)
            v.wait_ge(rc_in, 16)

            def mean(s_, q, s):
                v.tensor_tensor(aT[:, s, 0, :], blk(wide[:, 2, :], q), blk(rcnt, q), ALU.mult).then_inc(s_.a, 1)

            def rest2(q, u, s, first):
                v.wait_ge(d2a.Y, q + 1)
                if not first:
                    v.wait_ge(d2a.stored[s], 32 * u)
                v.tensor_copy(yb[:, s, :, 0:P], ps_z[s][:, :, 0, :])
                v.tensor_tensor(zb[:, s, :, :], ps_z[s][:, :, 1, :], xb[:, s, :, :], ALU.add).then_inc(d2a.done, 1)

            def layer2(q, u, s, first):
                if not first:
                    v.wait_ge(d2a.H, H1 * (q - 1))
                mean(d2a, q, s)
                rest2(q, u, s, first)
            pairs(v, layer2)

            sums(G2B)

            def scores2(q, u, s):
                n = 8 * q + 6
                v.wait_ge(d2b.H, q + 1)
                pj = push[:, bass.ds(TP * q, TP), :]
                v.tensor_copy(yb[:, s, :, P:P + HEADS], ps_v[s][:, :, 0:HEADS])
                v.tensor_copy(pj[:, :, 0:HEADS], ps_v[s][:, :, HEADS:2 * HEADS])
                v.tensor_tensor(psum6[:, s, :, :], ps_v[s][:, :, 0:HEADS], amean[:, bass.ds(TP * q, TP), :], ALU.add
                                ).then_inc(d2b.step, 1)
                v.wait_ge(d2b.step, n + 1)
                v.tensor_tensor(psum6[:, s, :, :], psum6[:, s, :, :], ps_v[s][:, :, HEADS:2 * HEADS], ALU.add).then_inc(d2b.step, 1)
                v.wait_ge(d2b.step, n + 2)
                v.scalar_tensor_tensor(pj[:, :, HEADS:2 * HEADS], psum6[:, s, :, :], SLOPE, psum6[:, s, :, :],
                                       ALU.mult, ALU.max).then_inc(d2b.done, 1)

            def layer2b(q, u, s, first):
                n = 8 * q
                if not first:
                    v.wait_ge(d2b.Y, q - 1)
                mean(d2b, q, s)
                v.wait_ge(d2b.Y, q + 1)
                v.wait_ge(d2b.x[s], 16 * (u + 1))
                v.tensor_tensor(rb[:, s, :, :], ps_y[s], xb[:, s, :, :], ALU.add).then_inc(d2b.step, 1)
                v.wait_ge(d2b.step, n + 1)
                if not first:
                    v.wait_ge(d2b.stored[s], 16 * u)
                layer_norm(d2b, s, n + 1, rb, yb, d2b.h)
                scores2(q, u, s)
            pairs(v, layer2b)

            def edge_scores(g, u, i, first):
                v.wait_ge(scores_ready, 1 + NG + g + 1)
                v.wait_ge(rows_landed[i], LANDED(A3) + 16 * CH * (u + 1))
                if not first:
                    v.wait_ge(as_stored[i], 16 * u)
                v.tensor_tensor(asum[:, i, :, :], rows[:, i, :, P:P + HEADS], one_ae[:, i, :, 1:1 + HEADS], ALU.add
                                ).then_inc(asum_ready, 1)

            scores(1, 0)
            for i in range(RING):
                edge_scores(i, 0, i, True)
            with v.Fori(1, NIT) as u:
                scores(1, u)
                for i in range(RING):
                    edge_scores(RING * u + i, u, i, False)

            v.wait_ge(scan_in, 16 * 5)
            v.tensor_tensor(CF, DI[1], DI[0], ALU.is_equal).then_inc(dve_step, step.up())
            v.tensor_tensor(CB, DI[1], DI[2], ALU.is_equal).then_inc(dve_step, step.up())
            v.wait_ge(dve_step, step.n)
            v.tensor_scalar(NF, CF, -1.0, BIG, ALU.add, ALU.mult).then_inc(dve_step, step.up())
            v.tensor_scalar(NB, CB, -1.0, BIG, ALU.add, ALU.mult).then_inc(dve_step, step.up())
            v.tensor_reduce(allc[:, 0:1], CF, AX.X, ALU.min).then_inc(dve_step, step.up())
            v.tensor_reduce(allc[:, 1:2], CB, AX.X, ALU.min).then_inc(dve_step, step.up())
            v.wait_ge(dve_step, step.n)
            edge_by_edge = lambda a, n: a.rearrange("p (j h) -> p h j", h=n)

            def scan(k, values, to, take_max):
                n, dirs = SCANS[k]
                nothing = -BIG if take_max else 0.0
                op0, op1 = (ALU.add, ALU.max) if take_max else (ALU.mult, ALU.add)
                goes_on = ((NF, NB) if take_max else (CF, CB))
                way = (slice(None, None, 1), slice(None, None, -1))

                def run(start):
                    for d in range(dirs):
                        for h in range(n):
                            v.tensor_tensor_scan(to[d][:, h, :][:, way[d]], goes_on[d][:, way[d]], values[:, h, :][:, way[d]],
                                                 start(d, h), op0, op1).then_inc(dve_step, step.up())
                    v.wait_ge(dve_step, step.n)

                run(lambda d, h: nothing)
                for d in range(dirs):
                    last = EPP - 1 if d == 0 else 0
                    v.tensor_copy(ends[:, d, 0, 0:n], to[d][:, :, last])
                    op = v.tensor_copy(ends[:, d, 1, 0:n], allc[:, d:d + 1].to_broadcast([P, n]))
                op.then_inc(scan_dve, 1)
                v.memset(carry[:, :, :], nothing).then_inc(dve_step, step.up())
                v.wait_ge(scan_pe, 2 * k + 1)
                for d in range(dirs):
                    flags = ps_m[0:n, (2 * d + 1) * P:(2 * d + 2) * P]
                    if take_max:
                        op = v.tensor_scalar(goes[0:n, d, :], flags, -1.0, BIG, ALU.add, ALU.mult)
                    else:
                        op = v.tensor_copy(goes[0:n, d, :], flags)
                    op.then_inc(dve_step, step.up())
                v.wait_ge(dve_step, step.n)
                for d in range(dirs):
                    op = v.tensor_tensor_scan(carry[0:n, d, 1 - d:1 - d + P][:, way[d]], goes[0:n, d, :][:, way[d]],
                                              ps_m[0:n, 2 * d * P:(2 * d + 1) * P][:, way[d]], nothing, op0, op1)
                op.then_inc(scan_dve, 1)
                v.wait_ge(scan_pe, 2 * k + 2)
                for d in range(dirs):
                    v.tensor_copy(start[:, 8 * d:8 * d + n], ps[6][:, 8 * d:8 * d + n]).then_inc(dve_step, step.up())
                v.wait_ge(dve_step, step.n)
                run(lambda d, h: start[:, 8 * d + h:8 * d + h + 1])

            scan(0, edge_by_edge(PU, 2 * HEADS), (FILLP,), False)
            v.tensor_tensor(AL, FILLP[:, 0:HEADS, :], edge_by_edge(AS, HEADS), ALU.add).then_inc(dve_step, step.up())
            v.tensor_copy(XLP, FILLP[:, HEADS:2 * HEADS, :]).then_inc(dve_step, step.up())
            v.wait_ge(dve_step, step.n)
            v.scalar_tensor_tensor(AL, AL, SLOPE, AL, ALU.mult, ALU.max).then_inc(dve_step, step.up())
            v.wait_ge(dve_step, step.n)
            scan(1, AL, (FW, BW), True)
            v.tensor_tensor(FW, FW, BW, ALU.max).then_inc(dve_step, step.up())
            v.wait_ge(dve_step, step.n)
            v.tensor_tensor(FW, FW, XLP, ALU.max).then_inc(dve_step, step.up())
            v.wait_ge(dve_step, step.n)
            v.tensor_tensor(EXP_, AL, FW, ALU.subtract).then_inc(scan_exp, 1)
            v.tensor_tensor(XLP, XLP, FW, ALU.subtract).then_inc(scan_exp, 1)
            v.wait_ge(scan_act, 2)
            v.wait_ge(scan_exp, 2)
            scan(2, EXP_, (FW, BW), False)
            v.tensor_tensor(FW, FW, BW, ALU.add).then_inc(dve_step, step.up())
            v.wait_ge(dve_step, step.n)
            v.tensor_tensor(FW, FW, EXP_, ALU.subtract).then_inc(dve_step, step.up())
            v.wait_ge(dve_step, step.n)
            v.tensor_tensor(FW, FW, XLP, ALU.add).then_inc(dve_step, step.up())
            v.wait_ge(dve_step, step.n)
            v.reciprocal(BW, FW).then_inc(dve_step, step.up())
            v.wait_ge(dve_step, step.n)
            v.tensor_tensor(edge_by_edge(EX, HEADS), EXP_, BW, ALU.mult)
            v.tensor_tensor(edge_by_edge(XL, HEADS), XLP, BW, ALU.mult).then_inc(scan_done, 1)
            v.wait_ge(scan_out, 32)

            sums(C3, weigh=True)
            v.wait_ge(wl_in, 16 * NT)

            def layer3(q, u, s, first):
                n = STEPS3 * q
                v.wait_ge(d3.Y, q + 1)
                v.tensor_tensor(rb[:, s, :, :], ps_y[s], xb[:, s, :, :], ALU.add).then_inc(d3.step, 1)
                for h in range(HEADS):
                    v.wait_ge(d3.step, n + 1 + TP * h)
                    for k in range(TP):
                        v.scalar_tensor_tensor(rb[:, s, k, :], ps_l[s][k][:, h * P:(h + 1) * P],
                                               wloop_f[:, bass.ds(HEADS * (TP * q + k) + h, 1)], rb[:, s, k, :],
                                               ALU.mult, ALU.add).then_inc(d3.step, 1)
                n = n + 1 + TP * HEADS
                v.wait_ge(d3.step, n)
                layer_norm(d3, s, n, rb, ub, d3.step)
                n = n + 6
                v.wait_ge(d3.step, n)
                gb = [ln_gb[:, k, :].unsqueeze(1).to_broadcast([TN, TP, P]) for k in range(2)]
                v.tensor_tensor(ub[:, s, :, :], ub[:, s, :, :], gb[0], ALU.mult).then_inc(d3.step, 1)
                v.wait_ge(d3.step, n + 1)
                v.tensor_tensor(ub[:, s, :, :], ub[:, s, :, :], gb[1], ALU.add).then_inc(d3.step, 1)
                v.wait_ge(d3.step, n + 2)
                v.tensor_tensor(ub[:, s, :, :], ub[:, s, :, :], xb[:, s, :, :], ALU.add).then_inc(d3.step, 1)
                v.wait_ge(d3.step, n + 3)
                if not first:
                    v.wait_ge(d3.stored[s], 16 * u)
                layer_norm(d3, s, n + 3, ub, yb, d3.done)
            pairs(v, layer3)


_INS = ["x", "src", "dst", "edge_attr_128", "edge_attr_16", "L0_gnn_W1", "L0_gnn_b1", "L0_gnn_W2", "L0_gnn_b2",
        "L1_gnn_eps", "L1_gnn_W1", "L1_gnn_b1", "L1_gnn_g1", "L1_gnn_be1", "L1_gnn_W2", "L1_gnn_b2", "L1_gnn_g2",
        "L1_gnn_be2", "L2_gnn_W1_l", "L2_gnn_W1_r", "L2_gnn_b1", "L2_gnn_W2_l", "L2_gnn_W2_r", "L2_gnn_b2",
        "L3_gnn_W", "L3_gnn_W_edge", "L3_gnn_att_src", "L3_gnn_att_dst", "L3_gnn_att_edge", "L3_gnn_gat_bias",
        "L3_gnn_lin_W", "L3_gnn_lin_b", "L3_gnn_ln_g", "L3_gnn_ln_b"]


def kernel(**inputs):
    import numpy as _np
    import concourse.bacc as _bacc
    from concourse import mybir as _mybir
    from concourse.bass_utils import run_bass_kernel_spmd as _run

    nc = _bacc.Bacc("TRN2", target_bir_lowering=False, num_devices=1)
    arrays, args = {}, {}
    for name in _INS:
        a = _np.ascontiguousarray(inputs[name])
        if _np.ndim(inputs[name]) == 0:
            a = a.reshape(1, 1)
        arrays[f"in_{name}"] = a
        args[name] = nc.dram_tensor(f"in_{name}", a.shape, _mybir.dt.from_np(a.dtype), kind="ExternalInput").ap()
    shape = inputs["x"].shape
    out = nc.dram_tensor("out", shape, F32, kind="ExternalOutput").ap()
    gnn_stack(nc, args, out)
    r = _run(nc, [arrays], core_ids=[0])
    return r.results[0]["out"]
```

```python
from contextlib import ExitStack

import concourse.bass as bass
from concourse import mybir

F32 = mybir.dt.float32
I32 = mybir.dt.int32
F16 = mybir.dt.float16
ALU = mybir.AluOpType
ACT = mybir.ActivationFunctionType
AX = mybir.AxisListType

P = 128
CH = 4
HALF = 2
CW = CH // HALF
GE = P * CH
HE = GE // HALF
RING = 4
W = 19
HEADS = 3
EF = 16
ROW3 = 132
NORM_EPS = 1e-5
SLOPE = 0.2
BIG = 1e30
NOWHERE = 20000


class Count:

    def __init__(self):
        self.n = 0

    def up(self):
        self.n += 1
        return 1


def gnn_stack(nc, t, out):
    N = t["x"].shape[0]
    E = t["src"].shape[0]
    H0 = t["L0_gnn_W1"].shape[1] // P
    H1 = t["L1_gnn_W1"].shape[1] // P
    NG = -(-E // (GE * RING)) * RING
    NIT = NG // RING
    EP = NG * GE
    NK = -(-N // W)
    NA = max(N + W, NK * W, -(-N // P) * P)
    TN = 125
    TP = 2
    PN = TN * TP
    NT = N // TN
    NP = N // PN
    EPP = EP // P
    FULL = E // GE
    TAIL = E - FULL * GE - HE
    TAIL_P = TAIL // CW
    NH = NG * HALF
    NE = NG * CH
    NQ = -(-N // P)
    KW = NQ * W
    AH = RING * HALF
    AW = AH * W
    TB = 2
    NS = NIT // TB
    QS = 7
    SL = NQ // QS
    HR = 104
    HJ = NH // HR
    assert N % PN == 0 and NP % 2 == 1 and FULL == NG - 1 and 0 < TAIL < HE and TAIL % CW == 0
    assert NA < 8192 and N < NOWHERE and NIT % 4 == 0 and NQ == SL * QS and NH == HR * HJ
    assert TB * AW <= 512 and HJ * HR <= 512 and HE <= 2048

    ctx = ExitStack()
    with ctx:
        def sb(name, shape, dt=F32):
            return ctx.enter_context(nc.sbuf_tensor(name, shape, dt))

        def sem(name):
            return ctx.enter_context(nc.semaphore(name))

        def sems(name, n):
            return [sem(f"{name}{i}") for i in range(n)]

        def dram(name, shape, dt=F32):
            return nc.dram_tensor(name, shape, dt, kind="Internal").ap()

        src_d = dram("src_filled", (EP,), I32)
        dst_d = dram("dst_filled", (EP + 2,), I32)
        x1_d = dram("x1_rows", (N, P))
        x2_d = dram("x2_rows", (N, P))
        z_d = dram("z_rows", (N, P))
        q_d = dram("q_rows", (N, P))
        t3_d = dram("x3_rows", (N, ROW3))
        sums_d = dram("node_sums", (1 + HEADS, N))
        adj_d = dram("adjacency", (NIT, P, NQ * AW), F16)
        rcnt_d = dram("rcnt", (N,))
        push_d = dram("pushed", (EP, 2 * HEADS))
        xe_d = dram("x3_of_edges", (EP, P))
        as_d = dram("src_and_edge_score", (EP, HEADS))
        at_d = dram("attention", (EP, HEADS))
        wl_d = dram("loop_weight", (EP, HEADS))

        wide = sb("wide", [P, 3, NA])
        wide_f = wide[:, :, :].rearrange("p a n -> p (a n)")
        rcnt = wide[:, 1, 0:N]
        nsum = wide[0:1 + HEADS, 0, :]
        rows = sb("rows", [P, RING, CH, ROW3])
        packed = [rows[:, i, :, :].rearrange("p c f -> p (c f)")[:, 0:CH * P].rearrange("p (c f) -> p c f", f=P)
                  for i in range(RING)]
        onehot = sb("onehot", [P, RING, CH, W])
        weighted = sb("weighted", [P, RING, CH, HEADS, W])
        idx = sb("idx", [P, RING, CH], I32)
        ea = sb("ea", [P, RING, CH, EF])
        prod = sb("prod", [P, RING, CH, HEADS, EF])
        one_ae = sb("one_ae", [P, RING, CH, 1 + HEADS])
        asum = sb("asum", [P, RING, CH, HEADS])
        att = sb("att", [P, RING, CH, HEADS])
        dst_rel = sb("dst_rel", [P, (NG + RING) * CH])
        dst_left = sb("dst_left", [P, NE])
        src_i = sb("src_i", [P, NE + RING * CH], I32)
        key = sb("key", [P, NE + CH])
        row = sb("row", [P, NE + CH])
        meta = sb("meta", [1, NIT, AH], I32)
        missing_i = sb("missing_i", [1, NG + 1], I32)
        base_f = sb("base_f", [1, NH])
        missing_f = sb("missing_f", [1, 1])
        iota_w = sb("iota_w", [P, W])
        iota_x = sb("iota_x", [P, W])
        wrap_x = sb("wrap_x", [P, W])
        onehot_x = sb("onehot_x", [P, CH, W])
        weighted_x = sb("weighted_x", [P, CH, HEADS, W])
        iota_k = sb("iota_k", [P, KW], F16)
        part_a = [wide_f[:, s * (NQ * AW // 2):(s + 1) * (NQ * AW // 2)].bitcast(F16).rearrange("p (q w) -> p q w", w=AW)
                  for s in range(2)]
        slices = sb("slices", [P, SL, TB, QS * AW], F16)
        slices_f = slices[:, :, :, :].rearrange("p s t w -> p (s t w)").bitcast(F32)

        def early(at, *shape):
            n = 1
            for size in shape[1:]:
                n *= size
            return slices_f[0:shape[0], at:at + n]

        zeros = early(0, P, EPP)
        att_b = early(EPP, P, 2, HEADS, P).rearrange("p (n h c) -> p n h c", n=2, c=P)
        w3, lin, w3T, we, ae_b = (early(EPP + (2 + n) * HEADS * P, EF if n > 2 else P, HEADS, P).rearrange("p (h c) -> p h c", c=P)
                                  for n in range(5))
        key_1h = early(0, P, 2, CW, KW).bitcast(F16).rearrange("p (n c k) -> p n c k", c=CW, k=KW)
        row_1h = early(2 * CW * KW, P, 2, CW, P).bitcast(F16).rearrange("p (n c k) -> p n c k", c=CW, k=P)
        table = slices[:, :, :, :].rearrange("p s t w -> p s (t w)").bitcast(F32)
        high_low = wide[:, 0, 0:NQ * P].bitcast(F16).rearrange("p (k q f) -> p k q f", k=2, f=P)
        scale = sb("scale", [P, 2])
        tmax = sb("tmax", [P, SL])
        pow2 = sb("pow2", [1, 2])
        ident = sb("ident", [P, P])
        ones = sb("ones", [P, P])
        fill_i, mark_i = (wide_f[0:1, (15 + n) * 1024:(15 + n) * 1024 + GE].bitcast(I32) for n in range(2))
        missed = sb("missed", [P, NG])
        xb = sb("xb", [TN, 2, TP, P])
        yb = sb("yb", [TN, 2, TP, ROW3])
        zb = sb("zb", [TN, 2, TP, P])
        rb = sb("rb", [TN, 2, TP, P])
        ub = sb("ub", [TN, 2, TP, P])
        xT = sb("xT", [P, 2, PN])
        aT = sb("aT", [P, 2, 3, PN])
        hT = sb("hT", [P, 2, H0, PN])
        st = sb("st", [TN, 2, TP, 6])
        mv = sb("mv", [TN, 2, TP, 2])
        rstd = sb("rstd", [TN, 2, TP])
        norm_eps = sb("norm_eps", [P, 1])
        w01 = sb("w01", [P, 2, H0 * P])
        w02 = sb("w02", [P, H0, P])
        w11 = sb("w11", [P, H1 * P])
        w12 = sb("w12", [P, H1, P])
        w21 = sb("w21", [P, 2, H1 * P])
        w22 = sb("w22", [P, H1, 2, P])
        fused3 = sb("fused3", [P, HEADS, P])
        v6 = sb("v6", [P, 2 * HEADS])
        we3 = sb("we3", [EF, HEADS])
        we_d = sb("we_d", [EF, HEADS, EF])
        we_b = sb("we_b", [P, HEADS, EF])
        col = sb("col", [P, 32])
        b01, b11, g11, e11, b12, g12, e12, b21, gatb = (0, 4, 6, 8, 10, 11, 12, 13, 15)
        eps1 = col[:, 20:21]
        row2 = sb("row2", [1, 4, P])
        ln_gb = sb("ln_gb", [TN, 2, P])
        bn1 = sb("bn1", [P, H1, NP, 6])
        bn2 = sb("bn2", [P, NP, 6])
        bnm = sb("bnm", [P, H1 + 1, 2])
        bns = sb("bns", [P, H1 + 1, 2])
        cntB = sb("cntB", [NT, 1 + HEADS, TN])
        endB = sb("endB", [NT, TN])
        begB = sb("begB", [NT, TN])
        rcB = sb("rcB", [NT, TN])
        meanB = sb("meanB", [NT, HEADS, TN])
        tri = sb("tri", [NT, NT])
        carB = sb("carB", [NT, 1])
        amean = sb("amean", [TN, NT, HEADS])
        beg_i = sb("beg_i", [TN, NT], I32)
        end_i = sb("end_i", [TN, NT], I32)
        push = sb("push", [TN, NT, 2 * HEADS])
        psum6 = sb("psum6", [TN, 2, TP, HEADS])
        wloop = sb("wloop", [TN, NT, HEADS])
        ends = sb("ends", [P, 2, 2, 2 * HEADS])
        goes = sb("goes", [2 * HEADS, 2, P])
        carry = sb("carry", [2 * HEADS, 2, P + 1])
        start = sb("start", [P, 16])
        allc = sb("allc", [P, 2])
        x_mark = sb("x_mark", [1, 1])
        totB = sb("totB", [NT, 1])

        ps = [ctx.enter_context(nc.psum_tensor(f"ps{i}", [P, 512], F32)) for i in range(8)]
        ps_t = [ps[0][:, PN * s:PN * s + PN] for s in range(2)]
        ps_h = [ps[1 + m][:, 0:PN] for m in range(4)]
        ps_y = [ps[5 + s][0:TN, 0:TP * P].rearrange("p (t f) -> p t f", t=TP) for s in range(2)]
        ps_b = [ps[5 + s][:, 0:PN] for s in range(2)]
        ps_z = [ps[5 + s][0:TN, 0:TP * 2 * P].rearrange("p (t k f) -> p t k f", t=TP, k=2) for s in range(2)]
        ps_a = [ps[4 + i][:, 0:HALF * HEADS * W] for i in range(RING)]
        ps_n = [ps[4 + i][0:1 + HEADS, 128:128 + HALF * W] for i in range(RING)]
        ps_k = [[ps[2 * s + k] for k in range(2)] for s in range(2)]
        ps_d = [ps[s][:, 0:TB * AW] for s in range(2)]
        ps_x = ps[0][:, 0:HEADS * W]
        ps_xn = ps[0][0:1 + HEADS, 128:128 + W]
        ps_m = ps[7]
        ps_v = [ps[7][0:TN, 16 * s:16 * s + TP * 2 * HEADS].rearrange("p (t k) -> p t k", t=TP) for s in range(2)]
        ps_l = [[ps[1 + 2 * s + k][0:TN, 0:HEADS * P] for k in range(TP)] for s in range(2)]

        filled = sem("filled")
        w_in = sem("w_in")
        consts = sem("consts")
        lists_in = sem("lists_in")
        we_in = sem("we_in")
        dve_step = sem("dve_step")
        prep_pe = sem("prep_pe")
        prep_dve = sem("prep_dve")
        rows_loaded = sems("rows_loaded", RING)
        rows_landed = sems("rows_landed", RING)
        idx_ready = sem("idx_ready")
        key_ready = sem("key_ready")
        key_summed = sem("key_summed")
        key_copied = sem("key_copied")
        adj_stored = sems("adj_stored", 2)
        slice_in = sems("slice_in", SL)
        table_zero = sem("table_zero")
        table_max = sem("table_max")
        scale_pe = sem("scale_pe")
        scaled = sem("scaled")
        high_ready = sem("high_ready")
        low_ready = sem("low_ready")
        slice_used = sem("slice_used")
        win_added = sem("win_added")
        x_loaded = sem("x_loaded")
        x_idx = sem("x_idx")
        x_rows = sem("x_rows")
        x_scored = sem("x_scored")
        x_prod = sem("x_prod")
        x_done = sem("x_done")
        ea_landed = sems("ea_landed", RING)
        att_landed = sems("att_landed", RING)
        xe_stored = sems("xe_stored", RING)
        as_stored = sems("as_stored", RING)
        onehot_ready = sem("onehot_ready")
        weighted_ready = sem("weighted_ready")
        scores_ready = sem("scores_ready")
        prod_ready = sem("prod_ready")
        node_sums = sem("node_sums")
        group_summed = sem("group_summed")
        psum_free = sem("psum_free")
        x_onehot = sem("x_onehot")
        x_summed = sem("x_summed")
        x_added = sem("x_added")
        asum_ready = sem("asum_ready")
        push_zeroed = sem("push_zeroed")
        pushed = sem("pushed")
        sums_out = sem("sums_out")
        sums_in = sem("sums_in")
        scan_in = sem("scan_in")
        scan_pe = sem("scan_pe")
        scan_dve = sem("scan_dve")
        scan_act = sem("scan_act")
        scan_out = sem("scan_out")
        wl_in = sem("wl_in")
        tail_in = sem("tail_in")
        ea_tail = sem("ea_tail")
        node_rc = sem("node_rc")
        node_dve = sem("node_dve")
        node_pe = sem("node_pe")
        dst_ready = sem("dst_ready")
        bn_var = sem("bn_var")
        bn_root = sem("bn_root")
        bn_ready = sem("bn_ready")
        x_iota = sem("x_iota")
        x_wrap = sem("x_wrap")
        scan_exp = sem("scan_exp")
        scan_done = sem("scan_done")

        root = sem("root")

        class Stage:

            def __init__(self, name, kinds):
                def of(kind):
                    return sem(f"{name}_{kind}") if kind in kinds.split() else None

                self.x = sems(f"{name}_x_landed", 2) if "x" in kinds.split() else None
                self.stored = sems(f"{name}_stored", 2) if "stored" in kinds.split() else None
                self.T = of("T")
                self.xT = of("xT")
                self.a = of("a")
                self.H = of("H")
                self.h = of("h")
                self.Y = of("Y")
                self.step = of("step")
                self.done = of("done")

        d0 = Stage("d0", "x stored T xT H h Y step done")
        d1a = Stage("d1a", "x T a H h done")
        d1b = Stage("d1b", "xT h Y done")
        d1c = Stage("d1c", "x stored xT Y step done")
        d2a = Stage("d2a", "x stored T xT a H h Y done")
        d2b = Stage("d2b", "x stored T xT a H h Y step done")
        d3 = Stage("d3", "x stored T xT a Y step done")

        L0, G1, C3 = range(3)
        LEAD = 2
        SUMMED = lambda a: a * NG
        ONEHOTS = lambda a: a * (NG + LEAD)
        FREED = lambda a: HALF * (RING + a * NG)
        LANDED = lambda k: 16 * NIT * CH * k
        IDX = lambda k: k * (RING + NG)

        def arrived(a, i, u):
            if a == G1:
                return rows_landed[i], LANDED(0) + 16 * CH * (u + 1)
            return rows_loaded[i], 16 * ((NIT if a == C3 else 0) + u + 1)

        def pairs(eng, body):
            body(0, 0, 0, True)
            body(1, 0, 1, True)
            with eng.Fori(1, NP // 2) as u:
                body(2 * u, u, 0, False)
                body(2 * u + 1, u, 1, False)
            body(NP - 1, NP // 2, 0, False)

        def tiles_of(a, q, width=P):
            return a.rearrange("(q t p) f -> p q t f", t=TP, p=TN)[:, bass.ds(q, 1), :, 0:width]

        def blk(a, q):
            return a[:, bass.ds(PN * q, PN)]

        def group_of(a, g):
            return a.rearrange("(g h p c) f -> p g h c f", h=HALF, p=P, c=CW)[:, bass.ds(g, 1), :, :, :]

        def slot_of(a):
            return a.rearrange("p (i h c) f -> p i h c f", h=HALF, c=CW)

        def batch_pair(t, s):
            return adj_d[bass.ds(TB * t, TB), :, QS * AW * s:QS * AW * (s + 1)].rearrange("b r w -> r b w")

        KEY_PARTS = ((0, -(-NQ // 2)), (-(-NQ // 2), NQ))

        def slices_in(s, k):
            return 16 * k * (NS + (2 if s == SL - 1 else 1))

        lists = [wide_f[0:HR, 1024 * n:1024 * n + HJ * HE].bitcast(I32).rearrange("r (j e) -> r j e", e=HE) for n in range(2)]
        lists_f = [wide_f[0:HR, 1024 * (2 + n):1024 * (2 + n) + HJ * HE].rearrange("r (j e) -> r j e", e=HE) for n in range(2)]
        tmp = [wide_f[:, 4096 + n * NE:4096 + (n + 1) * NE] for n in range(6)]

        def planes(at, n):
            return wide_f[:, at * EPP:(at + n) * EPP].rearrange("p (h j) -> p h j", j=EPP)

        PU = wide_f[:, 0:2 * HEADS * EPP]
        AL, XLP = planes(0, HEADS), planes(HEADS, HEADS)
        AS = wide_f[:, 2 * HEADS * EPP:3 * HEADS * EPP]
        EXP_ = planes(2 * HEADS, HEADS)
        FW, BW = planes(3 * HEADS, HEADS), planes(4 * HEADS, HEADS)
        FILLP = planes(3 * HEADS, 2 * HEADS)
        EX = wide_f[:, 3 * HEADS * EPP:4 * HEADS * EPP]
        XL = wide_f[:, 0:HEADS * EPP]
        DI = [wide_f[:, (5 * HEADS + n) * EPP:(5 * HEADS + n + 1) * EPP].bitcast(I32) for n in range(3)]
        CF, CB, NF, NB = (wide_f[:, (6 * HEADS + n) * EPP:(6 * HEADS + n + 1) * EPP] for n in range(4))
        SCANS = ((2 * HEADS, 1), (HEADS, 2), (HEADS, 2))
        STEPS3 = 1 + TP * HEADS + 6 + 3 + 5
        CONSTS = 16
        w_loads = Count()
        wloop_f = wloop[:, :, :].rearrange("p j h -> p (j h)")

        block = ctx.enter_context(nc.Block())

        @block.sync
        def _(sp):
            sp.wait_ge(consts, 3)
            sp.dma_start(src_d[0:E].unsqueeze(0), t["src"].unsqueeze(0)).then_inc(filled, 16)
            sp.dma_start(src_d[E:EP].unsqueeze(0), fill_i[:, 0:EP - E]).then_inc(filled, 16)
            sp.dma_start(dst_d[1:1 + E].unsqueeze(0), t["dst"].unsqueeze(0)).then_inc(filled, 16)
            sp.dma_start(dst_d[1 + E:2 + EP].unsqueeze(0), mark_i[:, 1:2 + EP - E]).then_inc(filled, 16)
            sp.dma_start(dst_d[0:1].unsqueeze(0), mark_i[:, 0:1]).then_inc(filled, 16)

            sp.wait_ge(filled, 80)
            for to, a in ((lists[0], dst_d[1:1 + EP]), (lists[1], src_d)):
                sp.dma_start(to, a.rearrange("(j r e) -> r j e", r=HR, e=HE)).then_inc(lists_in, 16)

            ea0 = t["edge_attr_128"]

            def load_edges(g, i):
                sp.dma_start(slot_of(packed[i]), group_of(ea0[0:FULL * GE, :], g)).then_inc(rows_loaded[i], 16)

            def load_tail(i, first_done, done):
                sp.dma_start(packed[i][:, 0:CW, :], ea0[FULL * GE:FULL * GE + HE, :].rearrange("(p c) f -> p c f", c=CW)
                             ).then_inc(first_done, 16)
                if first_done is not done:
                    sp.wait_ge(first_done, 16)
                sp.dma_start(packed[i][0:TAIL_P, CW:CH, :], ea0[E - TAIL:E, :].rearrange("(p c) f -> p c f", c=CW)
                             ).then_inc(done, 16)

            sp.wait_ge(consts, 4)
            for i in range(RING):
                load_edges(i, i)
            with sp.Fori(1, NIT - 1) as u:
                for i in range(RING):
                    sp.wait_ge(group_summed, RING * u + i - RING + 1)
                    load_edges(RING * u + i, i)
            for i in range(RING):
                g = NG - RING + i
                sp.wait_ge(group_summed, g - RING + 1)
                if g < FULL:
                    load_edges(g, i)
                else:
                    load_tail(i, tail_in, rows_loaded[i])

            miss = sp.alloc_register("sp_missing")
            turn = sp.alloc_register("sp_turn")
            sp.reg_mov(turn, 0)

            def missing_groups(load, last):
                sp.wait_ge(dst_ready, 1)
                sp.reg_load(miss, missing_i[0:1, NG:NG + 1])
                with sp.If(sp.snap(miss, min_val=0, max_val=EP) > 0):
                    def group(g, load):
                        sp.reg_load(miss, missing_i[0:1, bass.ds(g, 1)])
                        with sp.If(sp.snap(miss, min_val=0, max_val=GE) > 0):
                            sp.reg_add(turn, turn, 1)
                            sp.wait_ge(x_done, sp.snap(turn, min_val=1, max_val=2 * NG + 1))
                            load(g)
                    with sp.Fori(0, NG - 1) as g:
                        group(g, load)
                    group(NG - 1, last)

            ea16 = t["edge_attr_16"]

            def x_edges(g):
                for h in range(HALF):
                    sp.dma_start(slot_of(packed[0])[:, :, h, :, :], group_of(ea0[0:FULL * GE, :], g)[:, :, h, :, :]
                                 ).then_inc(x_loaded, 16)
                    sp.dma_start(slot_of(ea[:, 0, :, :])[:, :, h, :, :], group_of(ea16[0:FULL * GE, :], g)[:, :, h, :, :]
                                 ).then_inc(x_loaded, 16)

            def x_tail(g):
                load_tail(0, x_loaded, x_loaded)
                sp.dma_start(ea[:, 0, 0:CW, :], ea16[FULL * GE:FULL * GE + HE, :].rearrange("(p c) f -> p c f", c=CW)
                             ).then_inc(x_loaded, 16)
                sp.dma_start(ea[0:TAIL_P, 0, CW:CH, :], ea16[E - TAIL:E, :].rearrange("(p c) f -> p c f", c=CW)
                             ).then_inc(x_loaded, 16)

            def x_attention(g):
                sp.dma_start(slot_of(att[:, 0, :, :]), group_of(at_d, g)).then_inc(x_loaded, 16)

            sp.wait_ge(scores_ready, 1 + NG)
            missing_groups(x_edges, x_tail)

            def load_rows(s_, a):
                def body(q, u, s, first):
                    if not first:
                        sp.wait_ge(s_.done, q - 1)
                    sp.dma_start(xb[:, s:s + 1, :, :], tiles_of(a, q)).then_inc(s_.x[s], 16)
                pairs(sp, body)

            def stored(s_, n=1):
                sp.wait_ge(s_.stored[0], 16 * n * (NP // 2 + 1))
                sp.wait_ge(s_.stored[1], 16 * n * (NP // 2))

            sp.wait_ge(node_sums, 1)
            sp.dma_start(sums_d, nsum[:, 0:N]).then_inc(sums_out, 16)
            sp.wait_ge(sums_out, 16)
            sp.dma_start(cntB[:, :, :], sums_d.rearrange("k (j p) -> j k p", p=TN)).then_inc(sums_in, 16)
            load_rows(d0, t["x"])
            sp.wait_ge(d0.done, NP)
            stored(d0)
            load_rows(d1a, x1_d)
            sp.wait_ge(d1a.done, NP)
            load_rows(d1c, x1_d)
            sp.wait_ge(node_rc, 1)
            sp.dma_start(rcnt_d.rearrange("(j p) -> j p", p=TN), rcB[:, :]).then_inc(sums_out, 16)
            sp.wait_ge(sums_out, 32)
            sp.wait_ge(d1c.done, NP)
            sp.dma_start(rcnt, rcnt_d.unsqueeze(0).to_broadcast([P, N])).then_inc(sums_in, 16)
            stored(d1c)

            def load_dense(k, a):
                if k > 0:
                    sp.wait_ge(slice_used, SL * NS * k)
                for s in range(SL):
                    full = min((s + 1) * QS * P, N // P * P)
                    to = table[:, s, 0:full - s * QS * P].rearrange("p (q f) -> p q f", f=P)
                    sp.dma_start(to, a[s * QS * P:full, :].rearrange("(q r) f -> r q f", r=P)).then_inc(slice_in[s], 16)
                sp.wait_ge(table_zero, k + 1)
                sp.dma_start(table[0:N % P, SL - 1, (QS - 1) * P:QS * P], a[N // P * P:N, :]).then_inc(slice_in[SL - 1], 16)

                def load_slice(t, s):
                    sp.dma_start(slices[:, s, :, :], batch_pair(t, s)).then_inc(slice_in[s], 16)

                for s in range(SL):
                    sp.wait_ge(low_ready, SL * k + s + 1)
                    load_slice(0, s)
                with sp.Fori(1, NS) as t:
                    for s in range(SL):
                        sp.wait_ge(slice_used, SL * (NS * k + t - 1) + s + 1)
                        load_slice(t, s)

            for n in range(2):
                sp.wait_ge(adj_stored[n], 16 * NIT // 2)
            load_dense(0, x2_d)
            load_rows(d2a, x2_d)
            sp.wait_ge(d2a.done, NP)
            stored(d2a, 2)
            load_dense(1, z_d)
            load_rows(d2b, q_d)

            def store_xe(g, i):
                for h in range(HALF):
                    sp.dma_start(group_of(xe_d, g)[:, :, h, :, :], rows[:, i:i + 1, CW * h:CW * (h + 1), 0:P]).then_inc(xe_stored[i], 16)

            with sp.Fori(0, NIT) as u:
                for i in range(RING):
                    sp.wait_ge(asum_ready, RING * u + i + 1)
                    store_xe(RING * u + i, i)
            for i in range(RING):
                sp.wait_ge(xe_stored[i], 16 * HALF * NIT)
                sp.wait_ge(as_stored[i], 16 * NIT)

            sp.dma_start(AS, as_d.rearrange("(p j) h -> p (j h)", p=P)).then_inc(scan_in, 16)
            sp.wait_ge(pushed, 16 * NT)
            sp.dma_start(PU, push_d.rearrange("(p j) h -> p (j h)", p=P)).then_inc(scan_in, 16)
            for n in range(3):
                sp.dma_start(DI[n], dst_d[n:n + EP].rearrange("(p j) -> p j", p=P)).then_inc(scan_in, 16)
            sp.wait_ge(scan_done, 1)
            sp.dma_start(at_d.rearrange("(p j) h -> p (j h)", p=P), EX).then_inc(scan_out, 16)
            sp.dma_start(wl_d.rearrange("(p j) h -> p (j h)", p=P), XL).then_inc(scan_out, 16)
            sp.wait_ge(scan_out, 32)

            def load_c3(g, u, i):
                sp.dma_start(slot_of(packed[i]), group_of(xe_d, g)).then_inc(rows_loaded[i], 16)
                sp.dma_start(slot_of(att[:, i, :, :]), group_of(at_d, g)).then_inc(att_landed[i], 16)

            for i in range(RING):
                load_c3(i, 0, i)
            with sp.Fori(1, NIT) as u:
                for i in range(RING):
                    sp.wait_ge(group_summed, SUMMED(C3) + RING * u + i - RING + 1)
                    load_c3(RING * u + i, u, i)
            sp.wait_ge(psum_free, FREED(C3 + 1))
            missing_groups(x_attention, x_attention)
            load_rows(d3, t3_d)

        @block.gpsimd
        def _(pool):
            pool.memset(ident[:, :], 0.0).then_inc(consts, 1)
            pool.memset(fill_i, 0).then_inc(consts, 1)
            pool.memset(mark_i, NOWHERE).then_inc(consts, 1)
            pool.memset(rows[:, :, :, :], 0.0).then_inc(consts, 1)
            pool.memset(ones[:, :], 1.0).then_inc(consts, 1)
            pool.memset(tri[:, :], 1.0).then_inc(consts, 1)
            pool.iota(iota_w[:, :], pattern=[[1, W]], base=0, channel_multiplier=0,
                      allow_small_or_imprecise_dtypes=True).then_inc(consts, 1)
            pool.wait_ge(consts, 7)
            pool.affine_select(out=ident[:, :], in_=ident[:, :], compare_op=ALU.not_equal, fill=1.0, base=0,
                               pattern=[[-1, P]], channel_multiplier=1).then_inc(consts, 1)
            pool.affine_select(out=tri[:, :], in_=tri[:, :], compare_op=ALU.is_gt, fill=0.0, base=0,
                               pattern=[[1, NT]], channel_multiplier=-1).then_inc(consts, 1)
            pool.memset(one_ae[:, :, :, :], 1.0).then_inc(consts, 1)
            pool.memset(zeros, 0.0).then_inc(consts, 1)
            pool.memset(row2[:, :, :], 0.0).then_inc(consts, 1)
            pool.memset(wloop[:, :, :], 1.0).then_inc(consts, 1)
            pool.memset(yb[:, :, :, :], 0.0).then_inc(consts, 1)
            pool.memset(norm_eps[:, :], NORM_EPS).then_inc(consts, 1)
            pool.iota(iota_k[:, :], pattern=[[1, KW]], base=0, channel_multiplier=0,
                      allow_small_or_imprecise_dtypes=True).then_inc(consts, 1)

            def store_rows(s_, jobs):
                def body(q, u, s, first):
                    pool.wait_ge(s_.done, q + 1)
                    for buf, a, width in jobs:
                        pool.dma_start(tiles_of(a, q, width), buf[:, s:s + 1, :, 0:width]).then_inc(s_.stored[s], 16)
                pairs(pool, body)
                pool.wait_ge(s_.stored[0], 16 * len(jobs) * (NP // 2 + 1))
                pool.wait_ge(s_.stored[1], 16 * len(jobs) * (NP // 2))

            idx_next = pool.alloc_register("idx_next")
            pool.reg_mov(idx_next, 1)
            miss = pool.alloc_register("pool_missing")
            turn = pool.alloc_register("pool_turn")
            pool.reg_mov(turn, 1)

            def gather_chunk(i, c, table, width, done):
                pool.indirect_dma_start(out=packed[i][:, c, :] if width == P else rows[:, i, c, :], out_offset=None, in_=table,
                                        in_offset=bass.IndirectOffsetOnAxis(ap=idx[:, i, c:c + 1], axis=0)).then_inc(done, 16)

            def gather(table, width):
                with pool.Fori(0, NIT):
                    for i in range(RING):
                        pool.wait_ge(idx_ready, pool.snap(idx_next, min_val=1, max_val=1 << 20))
                        pool.reg_add(idx_next, idx_next, 1)
                        for c in range(CH):
                            gather_chunk(i, c, table, width, rows_landed[i])
                pool.reg_add(idx_next, idx_next, RING)

            def missing_groups(table, width=P):
                pool.wait_ge(dst_ready, 1)
                pool.reg_load(miss, missing_i[0:1, NG:NG + 1])
                with pool.If(pool.snap(miss, min_val=0, max_val=EP) > 0):
                    with pool.Fori(0, NG) as g:
                        pool.reg_load(miss, missing_i[0:1, bass.ds(g, 1)])
                        with pool.If(pool.snap(miss, min_val=0, max_val=GE) > 0):
                            pool.wait_ge(x_idx, pool.snap(turn, min_val=1, max_val=1 << 20))
                            pool.reg_add(turn, turn, 1)
                            for c in range(CH):
                                gather_chunk(0, c, table, width, x_rows)

            store_rows(d0, [(yb, x1_d, P)])
            gather(x1_d, P)
            missing_groups(x1_d)
            store_rows(d1c, [(yb, x2_d, P)])
            missing_groups(x2_d)
            store_rows(d2a, [(yb, z_d, P), (zb, q_d, P)])
            missing_groups(z_d)
            store_rows(d2b, [(yb, t3_d, ROW3)])

            pool.wait_ge(push_zeroed, 16 * 2 * HEADS)
            for j in range(NT):
                pool.indirect_dma_start(
                    out=push_d, out_offset=bass.IndirectOffsetOnAxis(ap=beg_i[:, j:j + 1], axis=0),
                    in_=push[:, j, :], in_offset=None, bounds_check=EP - 1, oob_is_err=False).then_inc(pushed, 16)

            gather(t3_d, ROW3)

            pool.wait_ge(scan_out, 32)
            for j in range(NT):
                pool.indirect_dma_start(
                    out=wloop[:, j, :], out_offset=None, in_=wl_d,
                    in_offset=bass.IndirectOffsetOnAxis(ap=end_i[:, j:j + 1], axis=0),
                    bounds_check=EP - 1, oob_is_err=False).then_inc(wl_in, 16)

            def weigh(u, i, first):
                g = RING * u + i
                pool.wait_ge(onehot_ready, ONEHOTS(C3) + g + 1)
                pool.wait_ge(att_landed[i], 16 * (u + 1))
                if not first:
                    pool.wait_ge(group_summed, SUMMED(C3) + g - RING + 1)
                pool.tensor_tensor(weighted[:, i, :, :, :],
                                   onehot[:, i, :, :].unsqueeze(2).to_broadcast([P, CH, HEADS, W]),
                                   att[:, i, :, :].unsqueeze(3).to_broadcast([P, CH, HEADS, W]),
                                   ALU.mult).then_inc(weighted_ready, 1)

            for i in range(RING):
                weigh(0, i, True)
            with pool.Fori(1, NIT) as u:
                for i in range(RING):
                    weigh(u, i, False)
            missing_groups(t3_d, ROW3)

            def store_out(q, u, s, first):
                pool.wait_ge(d3.done, q + 1)
                pool.dma_start(tiles_of(out, q), yb[:, s:s + 1, :, 0:P]).then_inc(d3.stored[s], 16)
            pairs(pool, store_out)
            pool.wait_ge(d3.stored[0], 16 * (NP // 2 + 1))
            pool.wait_ge(d3.stored[1], 16 * (NP // 2))

        @block.scalar
        def _(act):
            def load(dst, src):
                w_loads.up()
                act.dma_start(dst, src).then_inc(w_in, 16)

            def load_col(at, src, n):
                load(col[:, at:at + n], src.rearrange("(m p) -> p m", p=P))

            for to, a in ((we[:, :, :], t["L3_gnn_W_edge"].rearrange("k (h c) -> k h c", c=P)),
                          (ae_b[:, :, :].rearrange("p h c -> p (h c)"),
                           t["L3_gnn_att_edge"].rearrange("h c -> (h c)").unsqueeze(0).to_broadcast([EF, HEADS * P]))):
                act.dma_start(to, a).then_inc(we_in, 16)

            ea16 = t["edge_attr_16"]

            def load_ea(g, i):
                act.dma_start(slot_of(ea[:, i, :, :]), group_of(ea16[0:FULL * GE, :], g)).then_inc(ea_landed[i], 16)

            def load_ea_tail(i, n):
                act.dma_start(ea[:, i, 0:CW, :], ea16[FULL * GE:FULL * GE + HE, :].rearrange("(p c) k -> p c k", c=CW)
                              ).then_inc(ea_tail, 16)
                act.wait_ge(ea_tail, 16 * n)
                act.dma_start(ea[0:TAIL_P, i, CW:CH, :], ea16[E - TAIL:E, :].rearrange("(p c) k -> p c k", c=CW)
                              ).then_inc(ea_landed[i], 16)

            for i in range(RING):
                load_ea(i, i)
            with nc.allow_non_contiguous_dma(reason="biases by feature"):
                load(w01[:, :, :], t["L0_gnn_W1"].rearrange("(k p) m -> p k m", p=P))
                load(w02[:, :, :], t["L0_gnn_W2"].rearrange("(k p) m -> p k m", p=P))
                load_col(b01, t["L0_gnn_b1"], H0)
                act.wait_ge(consts, CONSTS)
                load(row2[:, 0, :], t["L0_gnn_b2"].unsqueeze(0))
                load(row2[:, 2, :], t["L2_gnn_b2"].unsqueeze(0))
                load(row2[:, 3, :], t["L3_gnn_lin_b"].unsqueeze(0))
                load(w11[:, :], t["L1_gnn_W1"])
                load(w12[:, :, :], t["L1_gnn_W2"].rearrange("(k p) m -> p k m", p=P))
                for at, name, n in ((b11, "L1_gnn_b1", H1), (g11, "L1_gnn_g1", H1), (e11, "L1_gnn_be1", H1),
                                    (b12, "L1_gnn_b2", 1), (g12, "L1_gnn_g2", 1), (e12, "L1_gnn_be2", 1),
                                    (b21, "L2_gnn_b1", H1), (gatb, "L3_gnn_gat_bias", HEADS)):
                    load_col(at, t[name], n)
                load(eps1, t["L1_gnn_eps"].to_broadcast([P, 1]))
                load(w21[:, 0, :], t["L2_gnn_W1_l"])
                load(w21[:, 1, :], t["L2_gnn_W1_r"])
                load(w22[:, :, 0, :], t["L2_gnn_W2_l"].rearrange("(k p) m -> p k m", p=P))
                load(w22[:, :, 1, :], t["L2_gnn_W2_r"].rearrange("(k p) m -> p k m", p=P))
                load(w3[:, :, :].rearrange("p h c -> p (h c)"), t["L3_gnn_W"])
                load(lin[:, :, :], t["L3_gnn_lin_W"].rearrange("(h p) m -> p h m", p=P))
                for n, name in enumerate(("L3_gnn_att_src", "L3_gnn_att_dst")):
                    load(att_b[:, n, :, :].rearrange("p h c -> p (h c)"),
                         t[name].rearrange("h c -> (h c)").unsqueeze(0).to_broadcast([P, HEADS * P]))
                for n, name in enumerate(("L3_gnn_ln_g", "L3_gnn_ln_b")):
                    load(ln_gb[:, n, :], t[name].unsqueeze(0).to_broadcast([TN, P]))
            for k in range(2 * HEADS):
                act.dma_start(push_d.rearrange("(p j) h -> p (j h)", p=P)[:, k * EPP:(k + 1) * EPP], zeros
                              ).then_inc(push_zeroed, 16)

            with act.Fori(1, NIT - 1) as u:
                for i in range(RING):
                    act.wait_ge(scores_ready, 1 + RING * u + i - RING + 1)
                    load_ea(RING * u + i, i)
            for i in range(RING):
                g = NG - RING + i
                act.wait_ge(scores_ready, 1 + g - RING + 1)
                if g < FULL:
                    load_ea(g, i)
                else:
                    load_ea_tail(i, 1)

            def deviations(s_, s, steps):
                act.wait_ge(s_.step, steps)
                act.activation(rstd[:, s, :], mv[:, s, :, 1], ACT.Sqrt, bias=norm_eps[0:TN, :]).then_inc(root, 1)

            def relu_rows(s_, n_h, bias, use_slot, before=None):
                def body(q, u, s, first):
                    act.wait_ge(s_.T, q + 1)
                    act.activation(xT[:, s, :], ps_t[s], ACT.Copy).then_inc(s_.xT, 1)
                    if before and not (first and s == 0):
                        before(q - 1, 1 - s)
                    if not first:
                        act.wait_ge(s_.Y, q - 1)
                    for m in range(n_h):
                        act.wait_ge(s_.H, n_h * q + m + 1)
                        act.activation(hT[:, s, m, :], ps_h[2 * s + m if use_slot else m], ACT.Relu,
                                       bias=col[:, bias + m:bias + m + 1]).then_inc(s_.h, 1)
                return body

            act.wait_ge(w_in, 16 * w_loads.n)

            def deviations0(q, s):
                deviations(d0, s, 6 * q + 5)
            pairs(act, relu_rows(d0, H0, b01, False, deviations0))
            deviations0(NP - 1, 0)

            def copy_batch(u, v, s, first):
                if not first:
                    act.wait_ge(adj_stored[s], 16 * v)
                for n in range(AH):
                    act.wait_ge(key_summed, 4 + AH * u + n + 1)
                    for k, (lo, hi) in enumerate(KEY_PARTS):
                        op = act.activation(part_a[s][:, lo:hi, W * n:W * (n + 1)],
                                            ps_k[n % 2][k][:, 0:(hi - lo) * W].rearrange("p (q w) -> p q w", w=W), ACT.Copy)
                    op.then_inc(key_copied, 1)
                act.wait_ge(key_copied, 2 + AH * (u + 1))
                act.dma_start(adj_d[bass.ds(u, 1), :, :].rearrange("b r w -> r b w"),
                              part_a[s].rearrange("p q w -> p (q w)").unsqueeze(1)).then_inc(adj_stored[s], 16)

            act.wait_ge(sums_out, 16)
            for n in range(2):
                copy_batch(n, 0, n, True)
            with act.Fori(1, NIT // 2) as v:
                for n in range(2):
                    copy_batch(2 * v + n, v, n, False)
            for n in range(2):
                act.wait_ge(adj_stored[n], 16 * NIT // 2)

            def hidden1(q, u, s, first):
                for m in range(H1):
                    act.wait_ge(d1a.H, H1 * q + m + 1)
                    act.activation(blk(wide[:, m, :], q), ps_h[2 * s + m], ACT.Identity,
                                   bias=col[:, b11 + m:b11 + m + 1]).then_inc(d1a.h, 1)
            pairs(act, hidden1)

            def norm1(q, u, s, first):
                if not first:
                    act.wait_ge(d1b.Y, q - 1)
                for m in range(H1):
                    act.activation(hT[:, s, m, :], blk(wide[:, m, :], q), ACT.Relu, bias=bns[:, m, 1:2],
                                   scale=bns[:, m, 0:1]).then_inc(d1b.h, 1)
            act.wait_ge(bn_var, 1)
            act.activation(bns[:, 0:H1, 1], bns[:, 0:H1, 1], ACT.Sqrt, bias=norm_eps[:, :]).then_inc(bn_root, 1)
            act.wait_ge(bn_ready, 1)
            pairs(act, norm1)

            def deviations1(q, s):
                deviations(d1c, s, 7 * q + 6)

            def norm2(q, u, s, first):
                if not first:
                    act.wait_ge(d1c.Y, q - 1)
                act.activation(xT[:, s, :], blk(wide[:, 0, :], q), ACT.Identity, bias=bns[:, H1, 1:2],
                               scale=bns[:, H1, 0:1]).then_inc(d1c.xT, 1)
                if not (first and s == 0):
                    deviations1(q - 1, 1 - s)
            act.wait_ge(bn_var, 2)
            act.activation(bns[:, H1, 1:2], bns[:, H1, 1:2], ACT.Sqrt, bias=norm_eps[:, :]).then_inc(bn_root, 1)
            act.wait_ge(bn_ready, 2)
            pairs(act, norm2)
            deviations1(NP - 1, 0)

            def high_parts(k):
                act.wait_ge(scaled, k + 1)
                for s in range(SL):
                    act.wait_ge(slice_in[s], slices_in(s, k) + (32 if s == SL - 1 else 16))
                    act.activation(high_low[:, 0, QS * s:QS * (s + 1), :].rearrange("p q f -> p (q f)"), table[:, s, 0:QS * P],
                                   ACT.Copy, scale=scale[:, 0:1]).then_inc(high_ready, 1)

            high_parts(0)
            pairs(act, relu_rows(d2a, H1, b21, True))

            high_parts(1)

            def x3T(q, u, s, first):
                deviations(d2b, s, 8 * q + 5)
                act.wait_ge(d2b.T, q + 1)
                act.activation(xT[:, s, :], ps_t[s], ACT.Copy).then_inc(d2b.xT, 1)
            pairs(act, x3T)

            for i in range(RING):
                load_ea(i, i)

            def store_as(g, i):
                act.wait_ge(asum_ready, g + 1)
                act.dma_start(group_of(as_d, g), slot_of(asum[:, i, :, :])).then_inc(as_stored[i], 16)

            with act.Fori(0, NIT - 2) as u:
                for i in range(RING):
                    store_as(RING * u + i, i)
                    load_ea(RING * (u + 1) + i, i)
            for i in range(RING):
                g = NG - 2 * RING + i
                store_as(g, i)
                if g + RING < FULL:
                    load_ea(g + RING, i)
                else:
                    load_ea_tail(i, 2)
            for i in range(RING):
                store_as(NG - RING + i, i)

            act.wait_ge(scan_exp, 1)
            act.activation(EXP_, EXP_, ACT.Exp).then_inc(scan_act, 1)
            act.wait_ge(scan_exp, 2)
            act.activation(XLP, XLP, ACT.Exp).then_inc(scan_act, 1)

            act.wait_ge(psum_free, FREED(C3 + 1))

            def deviations3(q, s):
                n = STEPS3 * q + 1 + TP * HEADS
                deviations(d3, s, n + 4)
                deviations(d3, s, n + 6 + 3 + 4)

            def operands3(q, u, s, first):
                act.wait_ge(d3.T, q + 1)
                if not first:
                    act.wait_ge(d3.Y, q - 1)
                act.activation(xT[:, s, :], ps_t[s], ACT.Copy).then_inc(d3.xT, 1)
                act.activation(aT[:, s, :, :], wide[:, :, bass.ds(PN * q, PN)], ACT.Copy).then_inc(d3.a, 1)
                if not (first and s == 0):
                    deviations3(q - 1, 1 - s)
            pairs(act, operands3)
            deviations3(NP - 1, 0)

        @block.tensor
        def _(pe):
            extra = pe.alloc_register("pe_extra")
            pe.reg_mov(extra, 0)
            miss = pe.alloc_register("pe_missing")
            turn = pe.alloc_register("pe_turn")
            pe.reg_mov(turn, 1)
            gathered = pe.alloc_register("pe_gathered")
            pe.reg_mov(gathered, 16 * CH)

            pe.wait_ge(consts, CONSTS)
            for n in range(2):
                pe.wait_ge(prep_dve, n + 1)
                for c in range(CW):
                    for j in range(HJ):
                        mm = pe.transpose(ps[2 * n + c][:, HR * j:HR * (j + 1)],
                                          lists_f[n][:, j, :].rearrange("r (p c) -> r c p", c=CW)[:, c, :], ident[0:HR, 0:HR])
                mm.then_inc(prep_pe, 1)
            pe.wait_ge(prep_dve, 3)
            pe.matmul(ps_m[:, 0:NH], ones[0:1, 0:P], base_f[:, :], start=True, stop=True).then_inc(prep_pe, 1)
            pe.wait_ge(prep_dve, 4)
            pe.matmul(ps[6][0:1, 0:NG], ones[:, 0:1], missed[:, :], start=True, stop=True).then_inc(prep_pe, 1)
            pe.wait_ge(prep_dve, 5)
            pe.matmul(ps_m[:, 0:HEADS * EF], ones[0:EF, 0:P], we_d[:, :, :].rearrange("k h e -> k (h e)"),
                      start=True, stop=True).then_inc(prep_pe, 1)
            pe.wait_ge(prep_dve, 6)
            pe.wait_ge(dst_ready, 1)

            def sums(a, sums_too=False, weigh=False, adjacency=False):
                width = HEADS * W if weigh else W

                def half(ha, n, h):
                    pe.wait_ge(key_ready, ha + 1)
                    pe.wait_ge(key_copied, ha + 1)
                    for k, (lo, hi) in enumerate(KEY_PARTS):
                        for c in range(CW):
                            mm = pe.matmul(ps_k[h][k][:, 0:(hi - lo) * W], row_1h[:, n, c, :], key_1h[:, n, c, lo * W:hi * W],
                                           start=(c == 0), stop=(c == CW - 1))
                    mm.then_inc(key_summed, 1)

                with pe.Fori(0, NIT) as u:
                    for i in range(RING):
                        g = RING * u + i
                        if adjacency:
                            for h in range(HALF):
                                half(HALF * g + h, (HALF * i + h) % 4, h)
                        if weigh:
                            pe.wait_ge(weighted_ready, g + 1)
                        else:
                            pe.wait_ge(onehot_ready, ONEHOTS(a) + g + 1)
                        if sums_too:
                            pe.wait_ge(scores_ready, 1 + g + 1)
                        pe.wait_ge(*arrived(a, i, u))
                        pe.wait_ge(psum_free, HALF * (SUMMED(a) + g + 1))
                        for h in range(HALF):
                            for c in range(CW):
                                n = CW * h + c
                                operand = weighted[:, i, n, :, :].rearrange("p h w -> p (h w)") if weigh else onehot[:, i, n, :]
                                mm = pe.matmul(ps_a[i][:, width * h:width * (h + 1)], packed[i][:, n, :], operand,
                                               start=(c == 0), stop=(c == CW - 1))
                            if sums_too:
                                for c in range(CW):
                                    n = CW * h + c
                                    mm = pe.matmul(ps_n[i][:, W * h:W * (h + 1)], one_ae[:, i, n, :], onehot[:, i, n, :],
                                                   start=(c == 0), stop=(c == CW - 1))
                        mm.then_inc(group_summed, 1)
                pe.wait_ge(psum_free, FREED(a + 1))
                if adjacency:
                    pe.wait_ge(key_copied, 2 + NH)

            def missing_groups(loaded=False, sums_too=False, weigh=False):
                pe.reg_load(miss, missing_i[0:1, NG:NG + 1])
                with pe.If(pe.snap(miss, min_val=0, max_val=EP) > 0):
                    with pe.Fori(0, NG) as g:
                        pe.reg_load(miss, missing_i[0:1, bass.ds(g, 1)])
                        with pe.If(pe.snap(miss, min_val=0, max_val=GE) > 0):
                            if loaded:
                                pe.wait_ge(x_scored, pe.snap(turn, min_val=1, max_val=1 << 20))
                                pe.reg_add(turn, turn, 1)
                            else:
                                pe.wait_ge(x_rows, pe.snap(gathered, min_val=1, max_val=1 << 20))
                                pe.reg_add(gathered, gathered, 16 * CH)
                            with pe.Fori(0, NK):
                                pe.reg_add(extra, extra, 1)
                                pe.wait_ge(x_onehot, pe.snap(extra, min_val=1, max_val=1 << 20))
                                for c in range(CH):
                                    operand = weighted_x[:, c, :, :].rearrange("p h w -> p (h w)") if weigh else onehot_x[:, c, :]
                                    mm = pe.matmul(ps_x[:, 0:HEADS * W if weigh else W], rows[:, 0, c, 0:P] if weigh else packed[0][:, c, :], operand,
                                                   start=(c == 0), stop=(c == CH - 1))
                                if sums_too:
                                    for c in range(CH):
                                        mm = pe.matmul(ps_xn, one_ae[:, 0, c, :], onehot_x[:, c, :], start=(c == 0), stop=(c == CH - 1))
                                mm.then_inc(x_summed, 1)

            def scale_products():
                pe.wait_ge(table_max, 1)
                pe.transpose(ps_m[0:1, 0:P], tmax[:, 0:1], ident[:, :]).then_inc(scale_pe, 1)
                pe.wait_ge(table_max, 2)
                pe.matmul(ps_m[:, P:P + 2], ones[0:1, 0:P], pow2[:, :], start=True, stop=True).then_inc(scale_pe, 1)

            def dense(k):
                pe.wait_ge(low_ready, SL * (k + 1))

                def dense_step(t, b, first):
                    if not first:
                        pe.wait_ge(win_added, TB * AH * (NS * k + t - 1))
                    for s in range(SL):
                        pe.wait_ge(slice_in[s], slices_in(s, k) + (32 if s == SL - 1 else 16) + 16 * (t + 1))
                        for q in range(QS):
                            for part in range(2):
                                mm = pe.matmul(ps_d[b], high_low[:, part, QS * s + q, :], slices[:, s, :, AW * q:AW * (q + 1)],
                                               start=(s == 0 and q == 0 and part == 0),
                                               stop=(s == SL - 1 and q == QS - 1 and part == 1))
                        mm.then_inc(slice_used, 1)

                for b in range(2):
                    dense_step(b, b, True)
                with pe.Fori(1, NS // 2) as v:
                    for b in range(2):
                        dense_step(2 * v + b, b, False)
                pe.wait_ge(win_added, TB * AH * NS * (k + 1))

            def transpose_rows(s_, q, u, s):
                pe.wait_ge(s_.x[s], 16 * (u + 1))
                for k in range(TP):
                    mm = pe.transpose(ps_t[s][:, TN * k:TN * (k + 1)], xb[:, s, k, :], ident[0:TN, 0:TN])
                mm.then_inc(s_.T, 1)

            sums(L0, sums_too=True)
            missing_groups(loaded=True, sums_too=True)
            pe.wait_ge(w_in, 16 * w_loads.n)

            def layer0(q, u, s, first):
                transpose_rows(d0, q, u, s)
                pe.wait_ge(d0.xT, q + 1)
                for m in range(H0):
                    if not (first and s == 0):
                        pe.wait_ge(d0.h, H0 * (q - 1) + m + 1)
                    pe.matmul(ps_h[m], w01[:, 0, m * P:(m + 1) * P], blk(wide[:, 2, :], q), start=True, stop=False)
                    pe.matmul(ps_h[m], w01[:, 1, m * P:(m + 1) * P], xT[:, s, :], start=False, stop=True).then_inc(d0.H, 1)
                pe.wait_ge(d0.h, H0 * (q + 1))
                if not first:
                    pe.wait_ge(d0.done, q - 1)
                for k in range(TP):
                    for m in range(H0):
                        pe.matmul(ps_y[s][:, k, :], hT[:, s, m, TN * k:TN * (k + 1)], w02[:, m, :], start=(m == 0), stop=False)
                    mm = pe.matmul(ps_y[s][:, k, :], ones[0:1, 0:TN], row2[:, 0, :], start=False, stop=True)
                mm.then_inc(d0.Y, 1)
            pairs(pe, layer0)

            pe.wait_ge(d0.done, NP)
            for h in range(HEADS):
                mm = pe.transpose(ps[6][:, h * P:(h + 1) * P], w3[:, h, :], ident[:, :])
            mm.then_inc(prep_pe, 1)
            pe.wait_ge(prep_dve, 7)
            for h in range(HEADS):
                mm = pe.matmul(ps[6][:, h * P:(h + 1) * P], w3T[:, h, :], lin[:, h, :], start=True, stop=True)
            mm.then_inc(prep_pe, 1)
            for h in range(HEADS):
                mm = pe.matmul(ps_m[0:1, 256:256 + P], col[:, gatb + h:gatb + h + 1], lin[:, h, :],
                               start=(h == 0), stop=(h == HEADS - 1))
            mm.then_inc(prep_pe, 1)
            pe.wait_ge(prep_dve, 9)

            sums(G1, adjacency=True)
            missing_groups()

            def layer1(q, u, s, first):
                transpose_rows(d1a, q, u, s)
                pe.wait_ge(d1a.a, q + 1)
                if not first:
                    pe.wait_ge(d1a.h, H1 * (q - 1))
                for m in range(H1):
                    pe.matmul(ps_h[2 * s + m], w11[:, m * P:(m + 1) * P], aT[:, s, 0, :], start=True, stop=True).then_inc(d1a.H, 1)
            pairs(pe, layer1)

            def layer1b(q, u, s, first):
                pe.wait_ge(d1b.h, H1 * (q + 1))
                if not first:
                    pe.wait_ge(d1b.xT, q - 1)
                for m in range(H1):
                    mm = pe.matmul(ps_b[s], w12[:, m, :], hT[:, s, m, :], start=(m == 0), stop=(m == H1 - 1))
                mm.then_inc(d1b.Y, 1)
            pairs(pe, layer1b)

            def layer1c(q, u, s, first):
                pe.wait_ge(d1c.xT, q + 1)
                if not first:
                    pe.wait_ge(d1c.done, q - 1)
                for k in range(TP):
                    mm = pe.transpose(ps_y[s][:, k, :], xT[:, s, TN * k:TN * (k + 1)], ident[:, :])
                mm.then_inc(d1c.Y, 1)
            pairs(pe, layer1c)

            pe.wait_ge(node_dve, 1)
            pe.matmul(ps_m[0:NT, 0:1], tri[:, :], totB[:, :], start=True, stop=True).then_inc(node_pe, 1)
            pe.wait_ge(node_dve, 2)
            for n, a in enumerate((begB[:, :], endB[:, :], *(meanB[:, h, :] for h in range(HEADS)))):
                mm = pe.transpose(ps_m[0:TN, 64 + n * NT:64 + (n + 1) * NT], a, ident[0:NT, 0:NT])
            mm.then_inc(node_pe, 1)
            pe.wait_ge(node_dve, 3)

            dense(0)
            missing_groups()

            def layer2(q, u, s, first):
                transpose_rows(d2a, q, u, s)
                pe.wait_ge(d2a.xT, q + 1)
                pe.wait_ge(d2a.a, q + 1)
                if not first:
                    pe.wait_ge(d2a.h, H1 * (q - 1))
                for m in range(H1):
                    pe.matmul(ps_h[2 * s + m], w21[:, 0, m * P:(m + 1) * P], aT[:, s, 0, :], start=True, stop=False)
                    pe.matmul(ps_h[2 * s + m], w21[:, 1, m * P:(m + 1) * P], xT[:, s, :], start=False, stop=True).then_inc(d2a.H, 1)
                pe.wait_ge(d2a.h, H1 * (q + 1))
                if not first:
                    pe.wait_ge(d2a.done, q - 1)
                for k in range(TP):
                    to = ps_z[s][:, k, :, :].rearrange("p k f -> p (k f)")
                    for m in range(H1):
                        pe.matmul(to, hT[:, s, m, TN * k:TN * (k + 1)], w22[:, m, :, :].rearrange("p k f -> p (k f)"),
                                  start=(m == 0), stop=False)
                    mm = pe.matmul(to, ones[0:1, 0:TN], row2[:, 1:3, :].rearrange("p k f -> p (k f)"), start=False, stop=True)
                mm.then_inc(d2a.Y, 1)
            pairs(pe, layer2)
            pe.wait_ge(d2a.done, NP)

            scale_products()
            dense(1)
            missing_groups()

            def layer2b(q, u, s, first):
                pe.wait_ge(d2b.a, q + 1)
                if not first:
                    pe.wait_ge(d2b.done, q - 1)
                for k in range(TP):
                    mm = pe.transpose(ps_y[s][:, k, :], aT[:, s, 0, TN * k:TN * (k + 1)], ident[:, :])
                mm.then_inc(d2b.Y, 1)
                pe.wait_ge(d2b.h, q + 1)
                for k in range(TP):
                    mm = pe.transpose(ps_t[s][:, TN * k:TN * (k + 1)], yb[:, s, k, 0:P], ident[0:TN, 0:TN])
                mm.then_inc(d2b.T, 1)
                pe.wait_ge(d2b.xT, q + 1)
                for k in range(TP):
                    mm = pe.matmul(ps_v[s][:, k, :], xT[:, s, TN * k:TN * (k + 1)], v6[:, :], start=True, stop=True)
                mm.then_inc(d2b.H, 1)
            pairs(pe, layer2b)

            for k, (n, dirs) in enumerate(SCANS):
                pe.wait_ge(scan_dve, 2 * k + 1)
                for d in range(dirs):
                    pe.transpose(ps_m[0:n, 2 * d * P:(2 * d + 1) * P], ends[:, d, 0, 0:n], ident[:, :])
                    mm = pe.transpose(ps_m[0:n, (2 * d + 1) * P:(2 * d + 2) * P], ends[:, d, 1, 0:n], ident[:, :])
                mm.then_inc(scan_pe, 1)
                pe.wait_ge(scan_dve, 2 * k + 2)
                for d in range(dirs):
                    mm = pe.transpose(ps[6][:, 8 * d:8 * d + n], carry[0:n, d, d:d + P], ident[0:n, 0:n])
                mm.then_inc(scan_pe, 1)

            sums(C3, weigh=True)
            missing_groups(weigh=True)

            def layer3(q, u, s, first):
                transpose_rows(d3, q, u, s)
                pe.wait_ge(d3.xT, q + 1)
                pe.wait_ge(d3.a, q + 1)
                if not first:
                    pe.wait_ge(d3.step, STEPS3 * (q - 2) + 1 + TP * HEADS)
                for k in range(TP):
                    pe.matmul(ps_l[s][k], xT[:, s, TN * k:TN * (k + 1)], fused3[:, :, :].rearrange("p h f -> p (h f)"),
                              start=True, stop=True)
                    for h in range(HEADS):
                        pe.matmul(ps_y[s][:, k, :], aT[:, s, h, TN * k:TN * (k + 1)], fused3[:, h, :], start=(h == 0), stop=False)
                    mm = pe.matmul(ps_y[s][:, k, :], ones[0:1, 0:TN], row2[:, 3, :], start=False, stop=True)
                mm.then_inc(d3.Y, 1)
            pairs(pe, layer3)

        @block.vector
        def _(v):
            extra = v.alloc_register("dve_extra")
            v.reg_mov(extra, 0)
            miss = v.alloc_register("dve_missing")
            prods = v.alloc_register("dve_prods")
            v.reg_mov(prods, 0)
            loads = v.alloc_register("dve_loads")
            v.reg_mov(loads, 0)
            norms = v.alloc_register("dve_norms")
            v.reg_mov(norms, 0)
            regs = [v.alloc_register(f"dve_base{n}") for n in range(TB * AH)]
            meta_f = meta[:, :, :].rearrange("a n k -> a (n k)")
            step = Count()

            v.memset(prod[:, :, :, :, :], 0.0).then_inc(scores_ready, 1)
            v.memset(x_mark[:, :], 0.0).then_inc(x_done, 1)
            for n in range(RING):
                v.memset(src_i[:, NE + CH * n:NE + CH * (n + 1)], 0).then_inc(key_summed, 1)
            for n in range(2):
                v.memset(key[:, NE + CW * n:NE + CW * (n + 1)], -1.0).then_inc(key_copied, 1)
            v.memset(row[:, NE:NE + CH], 0.0).then_inc(dve_step, step.up())
            for n in range(RING * HALF):
                v.memset(dst_rel[:, NE + CW * n:NE + CW * (n + 1)], -1.0).then_inc(psum_free, 1)

            v.wait_ge(lists_in, 32)
            for n in range(2):
                v.tensor_copy(lists_f[n], lists[n]).then_inc(prep_dve, 1)
            dst_f, src_f, kept, lost, block, block_i = tmp
            by_chunk = lambda a: a.rearrange("p (h c) -> p h c", c=CW)
            v.wait_ge(prep_pe, 1)
            for c in range(CW):
                v.tensor_copy(by_chunk(dst_f)[:, :, c], ps[c][:, 0:NH]).then_inc(dve_step, step.up())
            v.wait_ge(dve_step, step.n)
            v.tensor_copy(base_f[:, :], by_chunk(dst_f)[0:1, :, 0]).then_inc(prep_dve, 1)
            v.tensor_copy(meta_f[:, :], by_chunk(dst_f)[0:1, :, 0]).then_inc(dve_step, step.up())
            v.wait_ge(prep_pe, 2)
            for c in range(CW):
                v.tensor_copy(by_chunk(src_f)[:, :, c], ps[2 + c][:, 0:NH]).then_inc(dve_step, step.up())
                v.tensor_copy(by_chunk(src_i[:, 0:NE])[:, :, c], ps[2 + c][:, 0:NH]).then_inc(dve_step, step.up())
            v.wait_ge(prep_pe, 3)
            v.tensor_tensor(by_chunk(dst_rel[:, 0:NE]), by_chunk(dst_f), ps_m[:, 0:NH].unsqueeze(2).to_broadcast([P, NH, CW]),
                            ALU.subtract).then_inc(dve_step, step.up())
            v.wait_ge(dve_step, step.n)
            v.tensor_scalar(kept, dst_rel[:, 0:NE], 0.0, float(W - 1), ALU.max, ALU.min).then_inc(dve_step, step.up())
            v.tensor_scalar(block_i.bitcast(I32), src_i[:, 0:NE], 7, None, ALU.arith_shift_right).then_inc(dve_step, step.up())
            v.wait_ge(dve_step, step.n)
            v.tensor_tensor(lost, kept, dst_rel[:, 0:NE], ALU.not_equal).then_inc(dve_step, step.up())
            v.tensor_copy(block, block_i.bitcast(I32)).then_inc(dve_step, step.up())
            v.wait_ge(dve_step, step.n)
            v.tensor_tensor(kept, kept, dst_rel[:, 0:NE], ALU.is_equal).then_inc(dve_step, step.up())
            v.scalar_tensor_tensor(row[:, 0:NE], block, float(-P), src_f, ALU.mult, ALU.add).then_inc(dve_step, step.up())
            v.scalar_tensor_tensor(block, block, float(W), dst_rel[:, 0:NE], ALU.mult, ALU.add).then_inc(dve_step, step.up())
            v.scalar_tensor_tensor(dst_left[:, :], dst_f, 1.0, lost, ALU.add, ALU.mult).then_inc(dve_step, step.up())
            v.scalar_tensor_tensor(lost, dst_f, float(N), lost, ALU.is_lt, ALU.mult).then_inc(dve_step, step.up())
            v.wait_ge(dve_step, step.n)
            v.scalar_tensor_tensor(key[:, 0:NE], block, 1.0, kept, ALU.add, ALU.mult).then_inc(dve_step, step.up())
            v.tensor_scalar(dst_left[:, :], dst_left[:, :], -1.0, None, ALU.add).then_inc(dve_step, step.up())
            v.tensor_reduce(missed[:, :], lost.rearrange("p (g k) -> p g k", k=CH), AX.X, ALU.add).then_inc(prep_dve, 1)
            v.wait_ge(dve_step, step.n)
            v.tensor_scalar(key[:, 0:NE], key[:, 0:NE], -1.0, None, ALU.add).then_inc(dve_step, step.up())
            v.wait_ge(prep_pe, 4)
            v.tensor_copy(missing_i[:, 0:NG], ps[6][0:1, 0:NG]).then_inc(dve_step, step.up())
            v.tensor_reduce(missing_f[:, :], ps[6][0:1, 0:NG], AX.X, ALU.add).then_inc(dve_step, step.up())
            part_e = hT[0:EF, 1, :, :].rearrange("p m n -> p (m n)")[:, 0:HEADS * P]
            v.wait_ge(we_in, 32)
            v.tensor_tensor(part_e, we[:, :, :].rearrange("p h c -> p (h c)"),
                            ae_b[:, :, :].rearrange("p h c -> p (h c)"), ALU.mult).then_inc(dve_step, step.up())
            v.wait_ge(dve_step, step.n)
            v.tensor_copy(missing_i[:, NG:NG + 1], missing_f[:, :]).then_inc(dve_step, step.up())
            v.tensor_reduce(we3[:, :], part_e.rearrange("p (h c) -> p h c", c=P), AX.X, ALU.add).then_inc(dve_step, step.up())
            v.wait_ge(dve_step, step.n)
            v.wait_ge(consts, CONSTS)
            v.tensor_tensor(we_d[:, :, :], ident[0:EF, 0:EF].unsqueeze(1).to_broadcast([EF, HEADS, EF]),
                            we3[:, :].unsqueeze(2).to_broadcast([EF, HEADS, EF]), ALU.mult).then_inc(prep_dve, 1)
            v.wait_ge(prep_pe, 5)
            v.tensor_copy(we_b[:, :, :], ps_m[:, 0:HEADS * EF].rearrange("p (h e) -> p h e", e=EF)).then_inc(prep_dve, 1)
            v.tensor_copy(iota_x[:, :], iota_w[:, :]).then_inc(x_iota, 1)
            v.wait_ge(prep_dve, 6)
            v.wait_ge(x_iota, 1)
            v.memset(x_mark[:, :], 0.0).then_inc(dst_ready, 1)

            def scores(k, u):
                n = NG * k + RING * u
                v.wait_ge(scores_ready, 1 + n)
                for i in range(RING):
                    v.wait_ge(ea_landed[i], 16 * (NIT * k + u + 1))
                    v.tensor_tensor(prod[:, i, :, :, :], ea[:, i, :, :].unsqueeze(2).to_broadcast([P, CH, HEADS, EF]),
                                    we_b[:, :, :].unsqueeze(1).to_broadcast([P, CH, HEADS, EF]), ALU.mult).then_inc(prod_ready, 1)
                for i in range(RING):
                    v.wait_ge(prod_ready, n + i + 1)
                    v.tensor_reduce(one_ae[:, i, :, 1:1 + HEADS], prod[:, i, :, :, :], AX.X, ALU.add).then_inc(scores_ready, 1)

            def sources(g, i):
                v.tensor_copy(idx[:, i, :], src_i[:, bass.ds(CH * g, CH)]).then_inc(idx_ready, 1)

            def sums(a, sums_too=False, weigh=False, adjacency=False):
                def make(g, i):
                    v.tensor_tensor(onehot[:, i, :, :],
                                    dst_rel[:, bass.ds(CH * g, CH)].unsqueeze(2).to_broadcast([P, CH, W]),
                                    iota_w[:, :].unsqueeze(1).to_broadcast([P, CH, W]), ALU.is_equal).then_inc(onehot_ready, 1)

                def keys(g, i):
                    for h in range(HALF):
                        n = (HALF * i + h) % 4
                        v.wait_ge(key_summed, HALF * g + h + 1)
                        for c in range(CW):
                            at = CH * g + CW * h + c
                            v.tensor_scalar(row_1h[:, n, c, :], iota_k[:, 0:P], row[:, bass.ds(at, 1)], None, ALU.is_equal)
                            op = v.tensor_scalar(key_1h[:, n, c, :], iota_k[:, :], key[:, bass.ds(at, 1)], None, ALU.is_equal)
                        op.then_inc(key_ready, 1)

                v.memset(wide[:, :, :] if weigh else wide[:, 2, :], 0.0).then_inc(dve_step, step.up())
                if sums_too:
                    v.memset(nsum, 0.0).then_inc(dve_step, step.up())
                for g in range(LEAD):
                    make(g, g)
                if adjacency:
                    for g in range(RING):
                        sources(g, g)
                    v.wait_ge(push_zeroed, 16 * 2 * HEADS)
                    keys(0, 0)
                v.wait_ge(dve_step, step.n)
                with v.Fori(0, NIT) as u:
                    v.reg_load(regs[0:AH], meta_f[0:1, bass.ds(AH * u, AH)])
                    bases = [v.snap(r, min_val=0, max_val=N - 1) for r in regs[0:AH]]
                    if sums_too:
                        scores(0, u)
                    for i in range(RING):
                        g = RING * u + i
                        make(g + LEAD, (i + LEAD) % RING)
                        if adjacency:
                            keys(g + 1, i + 1)
                        v.wait_ge(group_summed, SUMMED(a) + g + 1)
                        for h in range(HALF):
                            at = bass.ds(bases[HALF * i + h], W)
                            v.wait_ge(psum_free, FREED(a) + HALF * g + h)
                            if sums_too:
                                v.tensor_tensor(nsum[:, at], nsum[:, at], ps_n[i][:, W * h:W * (h + 1)], ALU.add)
                            if weigh:
                                acc = wide[:, :, at]
                                part = ps_a[i][:, HEADS * W * h:HEADS * W * (h + 1)].rearrange("p (h w) -> p h w", w=W)
                            else:
                                acc = wide[:, 2, at]
                                part = ps_a[i][:, W * h:W * (h + 1)]
                            v.tensor_tensor(acc, acc, part, ALU.add).then_inc(psum_free, 1)
                        if adjacency:
                            sources(g + RING, i)
                v.wait_ge(psum_free, FREED(a + 1))

            def missing_groups(loaded=0, sums_too=False, weigh=False):
                v.reg_load(miss, missing_i[0:1, NG:NG + 1])
                with v.If(v.snap(miss, min_val=0, max_val=EP) > 0):
                    with v.Fori(0, NG) as g:
                        v.reg_load(miss, missing_i[0:1, bass.ds(g, 1)])
                        with v.If(v.snap(miss, min_val=0, max_val=GE) > 0):
                            if loaded:
                                v.reg_add(loads, loads, 16 * loaded)
                                v.wait_ge(x_loaded, v.snap(loads, min_val=1, max_val=1 << 20))
                            if sums_too:
                                v.tensor_tensor(prod[:, 0, :, :, :], ea[:, 0, :, :].unsqueeze(2).to_broadcast([P, CH, HEADS, EF]),
                                                we_b[:, :, :].unsqueeze(1).to_broadcast([P, CH, HEADS, EF]), ALU.mult
                                                ).then_inc(x_prod, 1)
                                v.reg_add(prods, prods, 1)
                                v.wait_ge(x_prod, v.snap(prods, min_val=1, max_val=1 << 20))
                                v.tensor_reduce(one_ae[:, 0, :, 1:1 + HEADS], prod[:, 0, :, :, :], AX.X, ALU.add
                                                ).then_inc(x_scored, 1)
                            else:
                                v.tensor_copy(idx[:, 0, :], src_i[:, bass.ds(CH * g, CH)]).then_inc(x_idx, 1)
                            with v.Fori(0, NK) as k:
                                v.reg_add(extra, extra, 1)
                                n = v.snap(extra, min_val=1, max_val=1 << 20)
                                v.wait_ge(x_iota, n)
                                if weigh:
                                    for c in range(CH):
                                        for h in range(HEADS):
                                            op = v.tensor_scalar(weighted_x[:, c, h, :], iota_x[:, :],
                                                                 dst_left[:, bass.ds(CH * g + c, 1)], att[:, 0, c, h:h + 1],
                                                                 ALU.is_equal, ALU.mult)
                                    op.then_inc(x_onehot, 1)
                                else:
                                    v.tensor_tensor(onehot_x[:, :, :],
                                                    dst_left[:, bass.ds(CH * g, CH)].unsqueeze(2).to_broadcast([P, CH, W]),
                                                    iota_x[:, :].unsqueeze(1).to_broadcast([P, CH, W]), ALU.is_equal
                                                    ).then_inc(x_onehot, 1)
                                v.wait_ge(x_onehot, n)
                                v.tensor_scalar(wrap_x[:, :], iota_x[:, :], float((NK - 1) * W), float(-NK * W), ALU.is_ge, ALU.mult
                                                ).then_inc(x_wrap, 1)
                                v.wait_ge(x_wrap, n)
                                v.scalar_tensor_tensor(iota_x[:, :], iota_x[:, :], float(W), wrap_x[:, :], ALU.add, ALU.add
                                                       ).then_inc(x_iota, 1)
                                v.wait_ge(x_summed, n)
                                if sums_too:
                                    part = nsum[:, bass.ds(W * k, W)]
                                    v.tensor_tensor(part, part, ps_xn, ALU.add)
                                acc = wide[:, :, bass.ds(W * k, W)] if weigh else wide[:, 2, bass.ds(W * k, W)]
                                frm = ps_x.rearrange("p (h w) -> p h w", w=W) if weigh else ps_x[:, 0:W]
                                v.tensor_tensor(acc, acc, frm, ALU.add).then_inc(x_added, 1)
                                v.wait_ge(x_added, n)
                            if loaded:
                                v.memset(x_mark[:, :], 0.0).then_inc(x_done, 1)

            def table_parts(k):
                v.wait_ge(slice_used, SL * NS * k) if k else None
                v.memset(table[:, SL - 1, (QS - 1) * P:QS * P], 0.0).then_inc(table_zero, 1)

            def scale_parts():
                for s in range(SL):
                    v.wait_ge(slice_in[s], slices_in(s, 1) + (32 if s == SL - 1 else 16))
                    v.tensor_reduce(tmax[:, s:s + 1], table[:, s, 0:QS * P], AX.X, ALU.max, apply_absolute_value=True
                                    ).then_inc(dve_step, step.up())
                v.wait_ge(dve_step, step.n)
                v.tensor_reduce(scale[:, 0:1], tmax[:, :], AX.X, ALU.max).then_inc(dve_step, step.up())
                v.wait_ge(dve_step, step.n)
                v.tensor_copy(tmax[:, 0:1], scale[:, 0:1]).then_inc(table_max, 1)
                v.wait_ge(scale_pe, 1)
                v.tensor_reduce(pow2[:, 0:1], ps_m[0:1, 0:P], AX.X, ALU.max).then_inc(dve_step, step.up())
                v.wait_ge(dve_step, step.n)
                v.tensor_scalar(pow2[:, 0:1], pow2[:, 0:1], 2.0 ** -90, 2.0 ** 90, ALU.max, ALU.min).then_inc(dve_step, step.up())
                v.wait_ge(dve_step, step.n)
                v.tensor_scalar(pow2[:, 0:1].bitcast(I32), pow2[:, 0:1].bitcast(I32), 0x7F800000, None, ALU.bitwise_and
                                ).then_inc(dve_step, step.up())
                v.wait_ge(dve_step, step.n)
                v.tensor_scalar(pow2[:, 1:2], pow2[:, 0:1], 2.0 ** -14, None, ALU.mult).then_inc(dve_step, step.up())
                v.wait_ge(dve_step, step.n)
                v.reciprocal(pow2[:, 0:1], pow2[:, 1:2]).then_inc(table_max, 1)
                v.wait_ge(scale_pe, 2)
                v.tensor_copy(scale[:, :], ps_m[:, P:P + 2]).then_inc(scaled, 1)

            def dense(k):
                v.wait_ge(scaled, k + 1)
                for s in range(SL):
                    v.wait_ge(high_ready, SL * k + s + 1)
                    v.scalar_tensor_tensor(high_low[:, 1, QS * s:QS * (s + 1), :].rearrange("p q f -> p (q f)"),
                                           table[:, s, 0:QS * P], scale[:, 0:1],
                                           high_low[:, 0, QS * s:QS * (s + 1), :].rearrange("p q f -> p (q f)"),
                                           ALU.mult, ALU.subtract).then_inc(low_ready, 1)
                v.memset(wide[:, 2, :], 0.0).then_inc(dve_step, step.up())
                v.wait_ge(dve_step, step.n)

                def add_step(t, b, first):
                    v.reg_load(regs, meta_f[0:1, bass.ds(TB * AH * t, TB * AH)])
                    bases = [v.snap(r, min_val=0, max_val=N - 1) for r in regs]
                    v.wait_ge(slice_used, SL * (NS * k + t + 1))
                    for n in range(TB * AH):
                        before = TB * AH * (NS * k + t) + n
                        if not (first and b == 0 and n == 0 and k == 0):
                            v.wait_ge(win_added, before)
                        acc = wide[:, 2, bass.ds(bases[n], W)]
                        v.scalar_tensor_tensor(acc, ps_d[b][:, W * n:W * (n + 1)], scale[:, 1:2], acc, ALU.mult, ALU.add
                                               ).then_inc(win_added, 1)

                for b in range(2):
                    add_step(b, b, True)
                with v.Fori(1, NS // 2) as t:
                    for b in range(2):
                        add_step(2 * t + b, b, False)
                v.wait_ge(win_added, TB * AH * NS * (k + 1))

            def layer_norm(s_, s, n, r, o, last):
                for k in range(TP):
                    v.bn_stats(st[:, s, k, :], r[:, s, k, :]).then_inc(s_.step, 1)
                v.wait_ge(s_.step, n + 2)
                v.reg_add(norms, norms, 1)
                for k in range(TP):
                    v.bn_aggr(mv[:, s, k, :], st[:, s, k, :]).then_inc(s_.step, 1)
                v.wait_ge(root, v.snap(norms, min_val=1, max_val=1 << 20))
                v.reciprocal(rstd[:, s, :], rstd[:, s, :]).then_inc(s_.step, 1)
                v.wait_ge(s_.step, n + 5)
                for k in range(TP):
                    op = v.tensor_scalar(o[:, s, k, 0:P], r[:, s, k, :], mv[:, s, k, 0:1], rstd[:, s, k:k + 1],
                                         ALU.subtract, ALU.mult)
                op.then_inc(last, 1)

            sums(L0, sums_too=True)
            missing_groups(loaded=4, sums_too=True)
            v.memset(x_mark[:, :], 0.0).then_inc(node_sums, 1)

            def layer0(q, u, s, first):
                n = 6 * q
                v.wait_ge(d0.Y, q + 1)
                v.tensor_tensor(rb[:, s, :, :], ps_y[s], xb[:, s, :, :], ALU.add).then_inc(d0.step, 1)
                v.wait_ge(d0.step, n + 1)
                if not first:
                    v.wait_ge(d0.stored[s], 16 * u)
                layer_norm(d0, s, n + 1, rb, yb, d0.done)
            pairs(v, layer0)

            v.wait_ge(w_in, 16 * w_loads.n)
            hT_f = hT[:, 0, :, :].rearrange("p m n -> p (m n)")
            hw = HEADS * P
            part = [hT_f[:, 0:hw], hT_f[:, hw:2 * hw]]
            for n in range(2):
                v.tensor_tensor(part[n], w3[:, :, :].rearrange("p h c -> p (h c)"),
                                att_b[:, n, :, :].rearrange("p h c -> p (h c)"), ALU.mult).then_inc(dve_step, step.up())
            v.wait_ge(dve_step, step.n)
            for n in range(2):
                v.tensor_reduce(v6[:, HEADS * n:HEADS * (n + 1)], part[n].rearrange("p (h c) -> p h c", c=P), AX.X, ALU.add)
            v.tensor_scalar(eps1, eps1, 1.0, None, ALU.add).then_inc(dve_step, step.up())
            v.wait_ge(dve_step, step.n)
            v.wait_ge(prep_pe, 6)
            v.tensor_copy(w3T[:, :, :], ps[6][:, 0:hw].rearrange("p (h c) -> p h c", c=P)).then_inc(prep_dve, 1)
            v.wait_ge(prep_pe, 7)
            v.tensor_copy(fused3[:, :, :], ps[6][:, 0:hw].rearrange("p (h c) -> p h c", c=P)).then_inc(prep_dve, 1)
            v.wait_ge(prep_pe, 8)
            v.tensor_tensor(row2[:, 3, :], row2[:, 3, :], ps_m[0:1, 256:256 + P], ALU.add).then_inc(prep_dve, 1)
            v.wait_ge(prep_dve, 9)

            sums(G1, adjacency=True)
            missing_groups()

            def stats1(q):
                v.wait_ge(d1a.h, H1 * (q + 1))
                for m in range(H1):
                    op = v.bn_stats(bn1[:, m, bass.ds(q, 1), :], blk(wide[:, m, :], q))
                op.then_inc(d1a.done, 1)

            def layer1(q, u, s, first):
                v.wait_ge(d1a.T, q + 1)
                if not first:
                    v.wait_ge(d1a.H, H1 * (q - 1))
                v.scalar_tensor_tensor(aT[:, s, 0, :], ps_t[s], eps1, blk(wide[:, 2, :], q), ALU.mult, ALU.add
                                       ).then_inc(d1a.a, 1)
                if not (first and s == 0):
                    stats1(q - 1)
            pairs(v, layer1)
            stats1(NP - 1)
            v.wait_ge(d1a.done, NP)

            def norm(lo, hi, frm, g, e):
                for m in range(lo, hi):
                    v.bn_aggr(bnm[:, m, :], frm[m - lo]).then_inc(dve_step, step.up())
                v.wait_ge(dve_step, step.n)
                v.tensor_copy(bns[:, lo:hi, 1], bnm[:, lo:hi, 1]).then_inc(bn_var, 1)
                v.wait_ge(bn_root, 1 if lo == 0 else 2)
                v.reciprocal(bns[:, lo:hi, 0], bns[:, lo:hi, 1]).then_inc(dve_step, step.up())
                v.wait_ge(dve_step, step.n)
                v.tensor_tensor(bns[:, lo:hi, 0], bns[:, lo:hi, 0], col[:, g:g + hi - lo], ALU.mult).then_inc(dve_step, step.up())
                v.wait_ge(dve_step, step.n)
                v.tensor_tensor(bnm[:, lo:hi, 0], bnm[:, lo:hi, 0], bns[:, lo:hi, 0], ALU.mult).then_inc(dve_step, step.up())
                v.wait_ge(dve_step, step.n)
                v.tensor_tensor(bns[:, lo:hi, 1], col[:, e:e + hi - lo], bnm[:, lo:hi, 0], ALU.subtract).then_inc(bn_ready, 1)

            norm(0, H1, [bn1[:, m, :, :].rearrange("p q k -> p (q k)") for m in range(H1)], g11, e11)

            def stats2(q, u, s, first):
                v.wait_ge(d1b.Y, q + 1)
                v.tensor_scalar(blk(wide[:, 0, :], q), ps_b[s], col[:, b12:b12 + 1], None, ALU.add).then_inc(d1b.xT, 1)
                v.wait_ge(d1b.xT, q + 1)
                v.bn_stats(bn2[:, bass.ds(q, 1), :], blk(wide[:, 0, :], q)).then_inc(d1b.done, 1)
            pairs(v, stats2)
            v.wait_ge(d1b.done, NP)
            norm(H1, H1 + 1, [bn2[:, :, :].rearrange("p q k -> p (q k)")], g12, e12)

            def layer1c(q, u, s, first):
                n = 7 * q
                v.wait_ge(d1c.Y, q + 1)
                v.wait_ge(d1c.x[s], 16 * (u + 1))
                v.tensor_tensor(rb[:, s, :, :], ps_y[s], xb[:, s, :, :], ALU.add).then_inc(d1c.step, 1)
                v.wait_ge(d1c.step, n + 1)
                v.scalar_tensor_tensor(ub[:, s, :, :], rb[:, s, :, :], 0.0, xb[:, s, :, :], ALU.max, ALU.add).then_inc(d1c.step, 1)
                v.wait_ge(d1c.step, n + 2)
                if not first:
                    v.wait_ge(d1c.stored[s], 16 * u)
                layer_norm(d1c, s, n + 2, ub, yb, d1c.done)
            pairs(v, layer1c)

            v.wait_ge(sums_in, 16)
            cnt = cntB[:, 0, :]
            v.tensor_tensor_scan(endB[:, :], ones[0:NT, 0:TN], cnt, 0.0, ALU.mult, ALU.add).then_inc(dve_step, step.up())
            v.tensor_scalar(rcB[:, :], cnt, 1.0, None, ALU.max).then_inc(dve_step, step.up())
            v.wait_ge(dve_step, step.n)
            v.tensor_copy(totB[:, :], endB[:, TN - 1:TN]).then_inc(node_dve, 1)
            v.reciprocal(rcB[:, :], rcB[:, :]).then_inc(node_rc, 1)
            v.wait_ge(node_rc, 1)
            v.tensor_tensor(meanB[:, :, :], cntB[:, 1:1 + HEADS, :], rcB[:, :].unsqueeze(1).to_broadcast([NT, HEADS, TN]),
                            ALU.mult).then_inc(dve_step, step.up())
            v.tensor_scalar(begB[:, :], cnt, 0.0, float(4 * EP), ALU.is_equal, ALU.mult).then_inc(dve_step, step.up())
            v.wait_ge(node_pe, 1)
            v.tensor_copy(carB[:, :], ps_m[0:NT, 0:1]).then_inc(dve_step, step.up())
            v.wait_ge(dve_step, step.n)
            v.scalar_tensor_tensor(endB[:, :], endB[:, :], carB[:, 0:1], begB[:, :], ALU.add, ALU.add).then_inc(dve_step, step.up())
            v.wait_ge(dve_step, step.n)
            v.tensor_tensor(begB[:, :], endB[:, :], cnt, ALU.subtract).then_inc(dve_step, step.up())
            v.wait_ge(dve_step, step.n)
            v.tensor_scalar(endB[:, :], endB[:, :], -1.0, None, ALU.add).then_inc(node_dve, 1)
            v.wait_ge(node_pe, 2)
            v.tensor_copy(beg_i[:, :], ps_m[0:TN, 64:64 + NT])
            v.tensor_copy(end_i[:, :], ps_m[0:TN, 64 + NT:64 + 2 * NT])
            v.tensor_copy(amean[:, :, :], ps_m[0:TN, 64 + 2 * NT:64 + (2 + HEADS) * NT].rearrange("p (h j) -> p j h", h=HEADS)
                          ).then_inc(node_dve, 1)
            v.wait_ge(node_dve, 3)

            table_parts(0)
            v.memset(scale[:, 0:1], 2.0 ** 10)
            v.memset(scale[:, 1:2], 2.0 ** -10).then_inc(scaled, 1)
            dense(0)
            missing_groups()
            v.wait_ge(sums_in, 32)

            def mean(s_, q, s):
                v.tensor_tensor(aT[:, s, 0, :], blk(wide[:, 2, :], q), blk(rcnt, q), ALU.mult).then_inc(s_.a, 1)

            def rest2(q, u, s, first):
                v.wait_ge(d2a.Y, q + 1)
                if not first:
                    v.wait_ge(d2a.stored[s], 32 * u)
                v.tensor_copy(yb[:, s, :, 0:P], ps_z[s][:, :, 0, :])
                v.tensor_tensor(zb[:, s, :, :], ps_z[s][:, :, 1, :], xb[:, s, :, :], ALU.add).then_inc(d2a.done, 1)

            def layer2(q, u, s, first):
                if not first:
                    v.wait_ge(d2a.H, H1 * (q - 1))
                mean(d2a, q, s)
                rest2(q, u, s, first)
            pairs(v, layer2)

            table_parts(1)
            scale_parts()
            dense(1)
            missing_groups()

            def scores2(q, u, s):
                n = 8 * q + 6
                v.wait_ge(d2b.H, q + 1)
                pj = push[:, bass.ds(TP * q, TP), :]
                v.tensor_copy(yb[:, s, :, P:P + HEADS], ps_v[s][:, :, 0:HEADS])
                v.tensor_copy(pj[:, :, 0:HEADS], ps_v[s][:, :, HEADS:2 * HEADS])
                v.tensor_tensor(psum6[:, s, :, :], ps_v[s][:, :, 0:HEADS], amean[:, bass.ds(TP * q, TP), :], ALU.add
                                ).then_inc(d2b.step, 1)
                v.wait_ge(d2b.step, n + 1)
                v.tensor_tensor(psum6[:, s, :, :], psum6[:, s, :, :], ps_v[s][:, :, HEADS:2 * HEADS], ALU.add).then_inc(d2b.step, 1)
                v.wait_ge(d2b.step, n + 2)
                v.scalar_tensor_tensor(pj[:, :, HEADS:2 * HEADS], psum6[:, s, :, :], SLOPE, psum6[:, s, :, :],
                                       ALU.mult, ALU.max).then_inc(d2b.done, 1)

            def layer2b(q, u, s, first):
                n = 8 * q
                if not first:
                    v.wait_ge(d2b.Y, q - 1)
                mean(d2b, q, s)
                v.wait_ge(d2b.Y, q + 1)
                v.wait_ge(d2b.x[s], 16 * (u + 1))
                v.tensor_tensor(rb[:, s, :, :], ps_y[s], xb[:, s, :, :], ALU.add).then_inc(d2b.step, 1)
                v.wait_ge(d2b.step, n + 1)
                if not first:
                    v.wait_ge(d2b.stored[s], 16 * u)
                layer_norm(d2b, s, n + 1, rb, yb, d2b.h)
                scores2(q, u, s)
            pairs(v, layer2b)

            def edge_scores(g, u, i, first):
                v.wait_ge(scores_ready, 1 + NG + g + 1)
                v.wait_ge(rows_landed[i], LANDED(1) + 16 * CH * (u + 1))
                if not first:
                    v.wait_ge(as_stored[i], 16 * u)
                v.tensor_tensor(asum[:, i, :, :], rows[:, i, :, P:P + HEADS], one_ae[:, i, :, 1:1 + HEADS], ALU.add
                                ).then_inc(asum_ready, 1)
                if not (first and i == 0):
                    v.wait_ge(xe_stored[(i - 1) % RING], 16 * HALF * (u + (1 if i > 0 else 0)))
                    sources(g - 1 + RING, (i - 1) % RING)

            for i in range(RING):
                sources(i, i)
            scores(1, 0)
            for i in range(RING):
                edge_scores(i, 0, i, True)
            with v.Fori(1, NIT) as u:
                scores(1, u)
                for i in range(RING):
                    edge_scores(RING * u + i, u, i, False)

            v.wait_ge(scan_in, 16 * 5)
            v.tensor_tensor(CF, DI[1], DI[0], ALU.is_equal).then_inc(dve_step, step.up())
            v.tensor_tensor(CB, DI[1], DI[2], ALU.is_equal).then_inc(dve_step, step.up())
            v.wait_ge(dve_step, step.n)
            v.tensor_scalar(NF, CF, -1.0, BIG, ALU.add, ALU.mult).then_inc(dve_step, step.up())
            v.tensor_scalar(NB, CB, -1.0, BIG, ALU.add, ALU.mult).then_inc(dve_step, step.up())
            v.tensor_reduce(allc[:, 0:1], CF, AX.X, ALU.min).then_inc(dve_step, step.up())
            v.tensor_reduce(allc[:, 1:2], CB, AX.X, ALU.min).then_inc(dve_step, step.up())
            v.wait_ge(dve_step, step.n)
            edge_by_edge = lambda a, n: a.rearrange("p (j h) -> p h j", h=n)

            def scan(k, values, to, take_max):
                n, dirs = SCANS[k]
                nothing = -BIG if take_max else 0.0
                op0, op1 = (ALU.add, ALU.max) if take_max else (ALU.mult, ALU.add)
                goes_on = ((NF, NB) if take_max else (CF, CB))
                way = (slice(None, None, 1), slice(None, None, -1))

                def run(start):
                    for d in range(dirs):
                        for h in range(n):
                            v.tensor_tensor_scan(to[d][:, h, :][:, way[d]], goes_on[d][:, way[d]], values[:, h, :][:, way[d]],
                                                 start(d, h), op0, op1).then_inc(dve_step, step.up())
                    v.wait_ge(dve_step, step.n)

                run(lambda d, h: nothing)
                for d in range(dirs):
                    last = EPP - 1 if d == 0 else 0
                    v.tensor_copy(ends[:, d, 0, 0:n], to[d][:, :, last])
                    op = v.tensor_copy(ends[:, d, 1, 0:n], allc[:, d:d + 1].to_broadcast([P, n]))
                op.then_inc(scan_dve, 1)
                v.memset(carry[:, :, :], nothing).then_inc(dve_step, step.up())
                v.wait_ge(scan_pe, 2 * k + 1)
                for d in range(dirs):
                    flags = ps_m[0:n, (2 * d + 1) * P:(2 * d + 2) * P]
                    if take_max:
                        op = v.tensor_scalar(goes[0:n, d, :], flags, -1.0, BIG, ALU.add, ALU.mult)
                    else:
                        op = v.tensor_copy(goes[0:n, d, :], flags)
                    op.then_inc(dve_step, step.up())
                v.wait_ge(dve_step, step.n)
                for d in range(dirs):
                    op = v.tensor_tensor_scan(carry[0:n, d, 1 - d:1 - d + P][:, way[d]], goes[0:n, d, :][:, way[d]],
                                              ps_m[0:n, 2 * d * P:(2 * d + 1) * P][:, way[d]], nothing, op0, op1)
                op.then_inc(scan_dve, 1)
                v.wait_ge(scan_pe, 2 * k + 2)
                for d in range(dirs):
                    v.tensor_copy(start[:, 8 * d:8 * d + n], ps[6][:, 8 * d:8 * d + n]).then_inc(dve_step, step.up())
                v.wait_ge(dve_step, step.n)
                run(lambda d, h: start[:, 8 * d + h:8 * d + h + 1])

            scan(0, edge_by_edge(PU, 2 * HEADS), (FILLP,), False)
            v.tensor_tensor(AL, FILLP[:, 0:HEADS, :], edge_by_edge(AS, HEADS), ALU.add).then_inc(dve_step, step.up())
            v.tensor_copy(XLP, FILLP[:, HEADS:2 * HEADS, :]).then_inc(dve_step, step.up())
            v.wait_ge(dve_step, step.n)
            v.scalar_tensor_tensor(AL, AL, SLOPE, AL, ALU.mult, ALU.max).then_inc(dve_step, step.up())
            v.wait_ge(dve_step, step.n)
            scan(1, AL, (FW, BW), True)
            v.tensor_tensor(FW, FW, BW, ALU.max).then_inc(dve_step, step.up())
            v.wait_ge(dve_step, step.n)
            v.tensor_tensor(FW, FW, XLP, ALU.max).then_inc(dve_step, step.up())
            v.wait_ge(dve_step, step.n)
            v.tensor_tensor(EXP_, AL, FW, ALU.subtract).then_inc(scan_exp, 1)
            v.tensor_tensor(XLP, XLP, FW, ALU.subtract).then_inc(scan_exp, 1)
            v.wait_ge(scan_act, 2)
            v.wait_ge(scan_exp, 2)
            scan(2, EXP_, (FW, BW), False)
            v.tensor_tensor(FW, FW, BW, ALU.add).then_inc(dve_step, step.up())
            v.wait_ge(dve_step, step.n)
            v.tensor_tensor(FW, FW, EXP_, ALU.subtract).then_inc(dve_step, step.up())
            v.wait_ge(dve_step, step.n)
            v.tensor_tensor(FW, FW, XLP, ALU.add).then_inc(dve_step, step.up())
            v.wait_ge(dve_step, step.n)
            v.reciprocal(BW, FW).then_inc(dve_step, step.up())
            v.wait_ge(dve_step, step.n)
            v.tensor_tensor(edge_by_edge(EX, HEADS), EXP_, BW, ALU.mult)
            v.tensor_tensor(edge_by_edge(XL, HEADS), XLP, BW, ALU.mult).then_inc(scan_done, 1)
            v.wait_ge(scan_out, 32)

            sums(C3, weigh=True)
            missing_groups(loaded=1, weigh=True)
            v.wait_ge(wl_in, 16 * NT)

            def layer3(q, u, s, first):
                n = STEPS3 * q
                v.wait_ge(d3.Y, q + 1)
                v.tensor_tensor(rb[:, s, :, :], ps_y[s], xb[:, s, :, :], ALU.add).then_inc(d3.step, 1)
                for h in range(HEADS):
                    v.wait_ge(d3.step, n + 1 + TP * h)
                    for k in range(TP):
                        v.scalar_tensor_tensor(rb[:, s, k, :], ps_l[s][k][:, h * P:(h + 1) * P],
                                               wloop_f[:, bass.ds(HEADS * (TP * q + k) + h, 1)], rb[:, s, k, :],
                                               ALU.mult, ALU.add).then_inc(d3.step, 1)
                n = n + 1 + TP * HEADS
                v.wait_ge(d3.step, n)
                layer_norm(d3, s, n, rb, ub, d3.step)
                n = n + 6
                v.wait_ge(d3.step, n)
                gb = [ln_gb[:, k, :].unsqueeze(1).to_broadcast([TN, TP, P]) for k in range(2)]
                v.tensor_tensor(ub[:, s, :, :], ub[:, s, :, :], gb[0], ALU.mult).then_inc(d3.step, 1)
                v.wait_ge(d3.step, n + 1)
                v.tensor_tensor(ub[:, s, :, :], ub[:, s, :, :], gb[1], ALU.add).then_inc(d3.step, 1)
                v.wait_ge(d3.step, n + 2)
                v.tensor_tensor(ub[:, s, :, :], ub[:, s, :, :], xb[:, s, :, :], ALU.add).then_inc(d3.step, 1)
                v.wait_ge(d3.step, n + 3)
                if not first:
                    v.wait_ge(d3.stored[s], 16 * u)
                layer_norm(d3, s, n + 3, ub, yb, d3.done)
            pairs(v, layer3)


_INS = ["x", "src", "dst", "edge_attr_128", "edge_attr_16", "L0_gnn_W1", "L0_gnn_b1", "L0_gnn_W2", "L0_gnn_b2",
        "L1_gnn_eps", "L1_gnn_W1", "L1_gnn_b1", "L1_gnn_g1", "L1_gnn_be1", "L1_gnn_W2", "L1_gnn_b2", "L1_gnn_g2",
        "L1_gnn_be2", "L2_gnn_W1_l", "L2_gnn_W1_r", "L2_gnn_b1", "L2_gnn_W2_l", "L2_gnn_W2_r", "L2_gnn_b2",
        "L3_gnn_W", "L3_gnn_W_edge", "L3_gnn_att_src", "L3_gnn_att_dst", "L3_gnn_att_edge", "L3_gnn_gat_bias",
        "L3_gnn_lin_W", "L3_gnn_lin_b", "L3_gnn_ln_g", "L3_gnn_ln_b"]


def kernel(**inputs):
    import numpy as _np
    import concourse.bacc as _bacc
    from concourse import mybir as _mybir
    from concourse.bass_utils import run_bass_kernel_spmd as _run

    nc = _bacc.Bacc("TRN2", target_bir_lowering=False, num_devices=1)
    arrays, args = {}, {}
    for name in _INS:
        a = _np.ascontiguousarray(inputs[name])
        if _np.ndim(inputs[name]) == 0:
            a = a.reshape(1, 1)
        arrays[f"in_{name}"] = a
        args[name] = nc.dram_tensor(f"in_{name}", a.shape, _mybir.dt.from_np(a.dtype), kind="ExternalInput").ap()
    shape = inputs["x"].shape
    out = nc.dram_tensor("out", shape, F32, kind="ExternalOutput").ap()
    gnn_stack(nc, args, out)
    r = _run(nc, [arrays], core_ids=[0])
    return r.results[0]["out"]
```

```python
from contextlib import ExitStack

import concourse.bass as bass
from concourse import mybir

F32 = mybir.dt.float32
I32 = mybir.dt.int32
F16 = mybir.dt.float16
BF16 = mybir.dt.bfloat16
ALU = mybir.AluOpType
ACT = mybir.ActivationFunctionType
AX = mybir.AxisListType

P = 128
CH = 4
HALF = 2
CW = CH // HALF
GE = P * CH
HE = GE // HALF
RING = 4
W = 19
HEADS = 3
EF = 16
NSUM = 1 + 3 * EF
ROW3 = 132
NORM_EPS = 1e-5
SLOPE = 0.2
BIG = 1e30
NOWHERE = 20000


class Count:

    def __init__(self):
        self.n = 0

    def up(self):
        self.n += 1
        return 1


def gnn_stack(nc, t, out):
    N = t["x"].shape[0]
    E = t["src"].shape[0]
    H0 = t["L0_gnn_W1"].shape[1] // P
    H1 = t["L1_gnn_W1"].shape[1] // P
    NG = -(-E // (GE * RING)) * RING
    NIT = NG // RING
    EP = NG * GE
    NK = -(-N // W)
    NA = max(N + W, NK * W, -(-N // P) * P)
    TN = 125
    TP = 2
    PN = TN * TP
    NT = N // TN
    NP = N // PN
    EPP = EP // P
    FULL = E // GE
    TAIL = E - FULL * GE - HE
    TAIL_P = TAIL // CW
    NH = NG * HALF
    NE = NG * CH
    NQ = -(-N // P)
    KW = NQ * W
    AH = RING * HALF
    AW = AH * W
    TB = 2
    NS = NIT // TB
    QS = 7
    SL = NQ // QS
    HR = 104
    HJ = NH // HR
    assert N % PN == 0 and NP % 2 == 1 and FULL == NG - 1 and 0 < TAIL < HE and TAIL % CW == 0
    assert NA < 8192 and N < NOWHERE and NIT % 4 == 0 and NQ == SL * QS and NH == HR * HJ
    assert TB * AW <= 512 and HJ * HR <= 512 and HE <= 2048

    ctx = ExitStack()
    with ctx:
        def sb(name, shape, dt=F32):
            return ctx.enter_context(nc.sbuf_tensor(name, shape, dt))

        def sem(name):
            return ctx.enter_context(nc.semaphore(name))

        def sems(name, n):
            return [sem(f"{name}{i}") for i in range(n)]

        def dram(name, shape, dt=F32):
            return nc.dram_tensor(name, shape, dt, kind="Internal").ap()

        src_d = dram("src_filled", (EP,), I32)
        dst_d = dram("dst_filled", (EP + 2,), I32)
        x1_d = dram("x1_rows", (N, P))
        x2_d = dram("x2_rows", (N, P))
        z_d = dram("z_rows", (N, P))
        q_d = dram("q_rows", (N, P))
        t3_d = dram("x3_rows", (N, ROW3))
        sums_d = dram("node_sums", (1 + HEADS, N))
        adj_d = dram("adjacency", (NIT, P, NQ * AW), F16)
        rcnt_d = dram("rcnt", (N,))
        push_d = dram("pushed", (EP, 2 * HEADS))
        xe_d = dram("x3_of_edges", (EP, P))
        as_d = dram("src_and_edge_score", (EP, HEADS))
        at_d = dram("attention", (EP, HEADS))
        wl_d = dram("loop_weight", (EP, HEADS))

        wide = sb("wide", [P, 3, NA])
        wide_f = wide[:, :, :].rearrange("p a n -> p (a n)")
        rcnt = wide[:, 1, 0:N]
        nsum = wide[0:NSUM, 1, :]
        rows = sb("rows", [P, RING, CH, ROW3])
        packed = [rows[:, i, :, :].rearrange("p c f -> p (c f)")[:, 0:CH * P].rearrange("p (c f) -> p c f", f=P)
                  for i in range(RING)]
        onehot = sb("onehot", [P, RING, CH, W])
        weighted = sb("weighted", [P, RING, CH, HEADS, W])
        idx = sb("idx", [P, RING, CH], I32)
        ea = sb("ea", [P, RING, CH, EF])
        prod = sb("prod", [P, RING, CH, HEADS, EF])
        e_score = sb("e_score", [P, RING, CH, HEADS])
        one_ea = sb("one_ea", [P, CH, 1 + EF])
        parts = sb("parts", [P, 2, RING * CH, NSUM], BF16)
        left = sb("left", [P, RING * CH, EF])
        onehot_b = sb("onehot_b", [P, RING, CH, W], BF16)
        asum = sb("asum", [P, RING, CH, HEADS])
        att = sb("att", [P, RING, CH, HEADS])
        dst_rel = sb("dst_rel", [P, (NG + RING) * CH])
        dst_left = sb("dst_left", [P, NE])
        src_i = sb("src_i", [P, NE + RING * CH], I32)
        key = sb("key", [P, NE + CH])
        row = sb("row", [P, NE + CH], F16)
        meta = sb("meta", [1, NIT, AH], I32)
        missing_i = sb("missing_i", [1, NG + 1], I32)
        base_f = sb("base_f", [1, NH])
        missing_f = sb("missing_f", [1, 1])
        iota_w = sb("iota_w", [P, W])
        iota_x = sb("iota_x", [P, W])
        wrap_x = sb("wrap_x", [P, W])
        onehot_x = sb("onehot_x", [P, CH, W])
        weighted_x = sb("weighted_x", [P, CH, HEADS, W])
        iota_k = sb("iota_k", [P, KW], F16)
        slices = sb("slices", [P, SL, TB, QS * AW], F16)
        slices_f = slices[:, :, :, :].rearrange("p s t w -> p (s t w)").bitcast(F32)

        def early(at, *shape):
            n = 1
            for size in shape[1:]:
                n *= size
            return slices_f[0:shape[0], at:at + n]

        zeros = early(SL * TB * QS * AW // 2 - EPP, P, EPP)
        att_b = early(EPP, P, 2, HEADS, P).rearrange("p (n h c) -> p n h c", n=2, c=P)
        w3, lin, w3T, we, ae_b = (early(EPP + (2 + n) * HEADS * P, EF if n > 2 else P, HEADS, P).rearrange("p (h c) -> p h c", c=P)
                                  for n in range(5))
        row_1h = early(0, P, 2, CW, P).bitcast(F16).rearrange("p (n c k) -> p n c k", c=CW, k=P)
        key_1h = 2 * CW * P
        part_a = [a.bitcast(F16).rearrange("p (q w) -> p q w", w=AW)
                  for a in (wide_f[:, 0:NQ * AW // 2], early(key_1h + CW * KW, P, NQ * AW // 2))]
        key_1h = early(key_1h, P, CW, KW)
        table = slices[:, :, :, :].rearrange("p s t w -> p s (t w)").bitcast(F32)
        high_low = wide[:, 0, 0:NQ * P].bitcast(F16).rearrange("p (k q f) -> p k q f", k=2, f=P)
        scale = sb("scale", [P, 2])
        tmax = sb("tmax", [P, SL])
        pow2 = sb("pow2", [1, 2])
        ident = sb("ident", [P, P])
        ones = sb("ones", [P, P])
        fill_i, mark_i = (wide_f[0:1, (15 + n) * 1024:(15 + n) * 1024 + GE].bitcast(I32) for n in range(2))
        missed = sb("missed", [P, NG])
        xb = sb("xb", [TN, 2, TP, P])
        yb = sb("yb", [TN, 2, TP, ROW3])
        zb = sb("zb", [TN, 2, TP, P])
        rb = sb("rb", [TN, 2, TP, P])
        ub = sb("ub", [TN, 2, TP, P])
        xa = ub
        xT = sb("xT", [P, 2, PN])
        aT = sb("aT", [P, 2, 3, PN])
        hT = sb("hT", [P, 2, H0, PN])
        hT_f = hT[:, :, :, :].rearrange("p s m n -> p (s m n)")
        key_1h = [a[:, n * CW * KW // 2:(n + 1) * CW * KW // 2].bitcast(F16).rearrange("p (c k) -> p c k", k=KW)
                  for a in (key_1h, hT_f) for n in range(2)]
        st = sb("st", [TN, 2, TP, 6])
        mv = sb("mv", [TN, 2, TP, 2])
        rstd = sb("rstd", [TN, 2, TP])
        norm_eps = sb("norm_eps", [P, 1])
        w01 = sb("w01", [P, 2, H0 * P])
        w02 = sb("w02", [P, H0, P])
        w11 = sb("w11", [P, H1 * P])
        w12 = sb("w12", [P, H1, P])
        w21 = sb("w21", [P, 2, H1 * P])
        w22 = sb("w22", [P, H1, 2, P])
        fused3 = sb("fused3", [P, HEADS, P])
        v6 = sb("v6", [P, 2 * HEADS])
        we3 = sb("we3", [EF, HEADS])
        to_scores = sb("to_scores", [NSUM, 1 + HEADS])
        we_d = sb("we_d", [EF, HEADS, EF])
        we_b = sb("we_b", [P, HEADS, EF])
        col = sb("col", [P, 32])
        b01, b11, g11, e11, b12, g12, e12, b21, gatb = (0, 4, 6, 8, 10, 11, 12, 13, 15)
        eps1 = col[:, 20:21]
        row2 = sb("row2", [1, 4, P])
        ln_gb = sb("ln_gb", [TN, 2, P])
        bn1 = sb("bn1", [P, H1, NP, 6])
        bn2 = sb("bn2", [P, NP, 6])
        bnm = sb("bnm", [P, H1 + 1, 2])
        bns = sb("bns", [P, H1 + 1, 2])
        cntB = sb("cntB", [NT, 1 + HEADS, TN])
        endB = sb("endB", [NT, TN])
        begB = sb("begB", [NT, TN])
        rcB = sb("rcB", [NT, TN])
        meanB = sb("meanB", [NT, HEADS, TN])
        tri = sb("tri", [NT, NT])
        carB = sb("carB", [NT, 1])
        amean = sb("amean", [TN, NT, HEADS])
        beg_i = sb("beg_i", [TN, NT], I32)
        end_i = sb("end_i", [TN, NT], I32)
        push = sb("push", [TN, NT, 2 * HEADS])
        psum6 = sb("psum6", [TN, 2, TP, HEADS])
        wloop = sb("wloop", [TN, NT, HEADS])
        ends = sb("ends", [P, 2, 2, 2 * HEADS])
        goes = sb("goes", [2 * HEADS, 2, P])
        carry = sb("carry", [2 * HEADS, 2, P + 1])
        start = sb("start", [P, 16])
        allc = sb("allc", [P, 2])
        x_mark = sb("x_mark", [1, 2])
        totB = sb("totB", [NT, 1])

        ps = [ctx.enter_context(nc.psum_tensor(f"ps{i}", [P, 512], F32)) for i in range(8)]
        ps_t = [ps[7 * s][:, 0:PN] for s in range(2)]
        ps_h = [ps[1 + m][:, 0:PN] for m in range(4)]
        ps_y = [ps[5 + s][0:TN, 0:TP * P].rearrange("p (t f) -> p t f", t=TP) for s in range(2)]
        ps_b = [ps[5 + s][:, 0:PN] for s in range(2)]
        ps_z = [ps[5 + s][0:TN, 0:TP * 2 * P].rearrange("p (t k f) -> p t k f", t=TP, k=2) for s in range(2)]
        ps_a = [ps[4 + i][:, 128:128 + HALF * HEADS * W] for i in range(RING)]
        ps_n = [ps[4 + i][0:NSUM, 0:HALF * W] for i in range(RING)]
        ps_k = [[ps[2 * s + k] for k in range(2)] for s in range(2)]
        ps_d = [ps[s][:, 0:TB * AW] for s in range(2)]
        ps_x = ps[0][:, 0:HEADS * W]
        ps_xn = ps[0][0:1 + EF, 256:256 + W]
        ps_m = ps[7]
        ps_v = [ps[1 + s][0:TN, 0:TP * 2 * HEADS].rearrange("p (t k) -> p t k", t=TP) for s in range(2)]
        ps_l = [[ps[1 + 2 * s + k][0:TN, 0:HEADS * P] for k in range(TP)] for s in range(2)]

        filled = sem("filled")
        w_in = sem("w_in")
        consts = sem("consts")
        lists_in = sem("lists_in")
        we_in = sem("we_in")
        dve_step = sem("dve_step")
        prep_pe = sem("prep_pe")
        prep_dve = sem("prep_dve")
        rows_loaded = sems("rows_loaded", RING)
        rows_landed = sems("rows_landed", RING)
        idx_ready = sem("idx_ready")
        key_ready = sem("key_ready")
        key_summed = sem("key_summed")
        key_copied = sem("key_copied")
        adj_stored = sems("adj_stored", 2)
        slice_in = sems("slice_in", SL)
        table_zero = sem("table_zero")
        table_max = sem("table_max")
        scale_pe = sem("scale_pe")
        scaled = sem("scaled")
        high_ready = sem("high_ready")
        low_ready = sem("low_ready")
        slice_used = sem("slice_used")
        win_added = sem("win_added")
        x_loaded = sem("x_loaded")
        x_idx = sem("x_idx")
        x_rows = sem("x_rows")
        x_scored = sem("x_scored")
        ea_in = sem("ea_in")
        x_done = sem("x_done")
        ea_landed = sems("ea_landed", RING)
        att_landed = sems("att_landed", RING)
        xe_stored = sems("xe_stored", RING)
        as_stored = sems("as_stored", RING)
        onehot_ready = sem("onehot_ready")
        weighted_ready = sem("weighted_ready")
        scores_ready = sem("scores_ready")
        parts_ready = sem("parts_ready")
        onehot_b_ready = sem("onehot_b_ready")
        prod_ready = sem("prod_ready")
        node_sums = sem("node_sums")
        sums_pe = sem("sums_pe")
        ps_zero = sem("ps_zero")
        group_summed = sem("group_summed")
        psum_free = sem("psum_free")
        x_onehot = sem("x_onehot")
        x_summed = sem("x_summed")
        x_added = sem("x_added")
        asum_ready = sem("asum_ready")
        push_zeroed = sem("push_zeroed")
        pushed = sem("pushed")
        sums_out = sem("sums_out")
        sums_in = sem("sums_in")
        scan_in = sem("scan_in")
        scan_pe = sem("scan_pe")
        scan_dve = sem("scan_dve")
        scan_act = sem("scan_act")
        scan_out = sem("scan_out")
        wl_in = sem("wl_in")
        tail_in = sem("tail_in")
        ea_tail = sem("ea_tail")
        node_rc = sem("node_rc")
        node_dve = sem("node_dve")
        node_pe = sem("node_pe")
        dst_ready = sem("dst_ready")
        bn_var = sem("bn_var")
        bn_root = sem("bn_root")
        bn_ready = sem("bn_ready")
        x_iota = sem("x_iota")
        x_wrap = sem("x_wrap")
        scan_exp = sem("scan_exp")
        scan_done = sem("scan_done")

        root = sem("root")

        xa_landed = sems("xa_landed", 2)
        pair_landed = sems("pair_landed", 2)
        pair_stored = sems("pair_stored", 2)
        pair_counts = [[0, 0], [0, 0]]

        class Stage:

            def __init__(self, name, kinds, loads=0, stores=0):
                def of(kind):
                    return sem(f"{name}_{kind}") if kind in kinds.split() else None

                self.landed0 = list(pair_counts[0])
                self.stored0 = list(pair_counts[1])
                self.stores = stores
                for s in range(2):
                    pair_counts[0][s] += 16 * loads * ((NP + 1 - s) // 2)
                    pair_counts[1][s] += 16 * stores * ((NP + 1 - s) // 2)
                self.T = of("T")
                self.xT = of("xT")
                self.a = of("a")
                self.H = of("H")
                self.h = of("h")
                self.Y = of("Y")
                self.step = of("step")
                self.done = of("done")

            def landed(self, s, u):
                return pair_landed[s], self.landed0[s] + 16 * (u + 1)

            def stored(self, s, n):
                return pair_stored[s], self.stored0[s] + 16 * self.stores * n

        d0 = Stage("d0", "T xT H h Y step done", loads=1, stores=1)
        d1a = Stage("d1a", "T a H h done", loads=1)
        d1b = Stage("d1b", "xT h Y done")
        d1c = Stage("d1c", "xT Y step done", loads=1, stores=1)
        d2a = Stage("d2a", "T xT a H h Y done", loads=1, stores=2)
        d2b = Stage("d2b", "T xT a H h Y step done", loads=1, stores=1)
        d3 = Stage("d3", "T xT a Y step done", loads=1, stores=1)

        L0, C3 = range(2)
        LEAD = 3
        SUMMED = lambda a: a * NG
        ONEHOTS = lambda a: a * (NG + LEAD)
        FREED = lambda a: HALF * (RING + a * NG)
        PIECES = -(-N // 512)
        SCALED = (1, 1, 2)

        def arrived(a, i, u):
            return rows_loaded[i], 16 * ((NIT if a == C3 else 0) + u + 1)

        def steps2b(q):
            return 0 if isinstance(q, int) and q == 0 else 8 * q - 2

        def pairs(eng, body, peeled=2):
            for q in range(peeled):
                body(q, q // 2, q % 2, q < 2)
            with eng.Fori(peeled // 2, NP // 2) as u:
                body(2 * u, u, 0, False)
                body(2 * u + 1, u, 1, False)
            body(NP - 1, NP // 2, 0, False)

        def xa_in(s_, s, u):
            return xa_landed[s], (16 * ((NP + 1 - s) // 2) if s_ is d2a else 0) + 16 * (u + 1)

        def is_last(q):
            return isinstance(q, int) and q == NP - 1

        def tiles_of(a, q, width=P):
            return a.rearrange("(q t p) f -> p q t f", t=TP, p=TN)[:, bass.ds(q, 1), :, 0:width]

        def blk(a, q):
            return a[:, bass.ds(PN * q, PN)]

        def group_of(a, g):
            return a.rearrange("(g h p c) f -> p g h c f", h=HALF, p=P, c=CW)[:, bass.ds(g, 1), :, :, :]

        def slot_of(a):
            return a.rearrange("p (i h c) f -> p i h c f", h=HALF, c=CW)

        def batch_pair(t, s):
            return adj_d[bass.ds(TB * t, TB), :, QS * AW * s:QS * AW * (s + 1)].rearrange("b r w -> r b w")

        KEY_PARTS = ((0, -(-NQ // 2)), (-(-NQ // 2), NQ))

        def slices_in(s, k):
            return 16 * k * (NS + (2 if s == SL - 1 else 1))

        lists = [wide_f[0:HR, 1024 * n:1024 * n + HJ * HE].bitcast(I32).rearrange("r (j e) -> r j e", e=HE) for n in range(2)]
        lists_f = [wide_f[0:HR, 1024 * (2 + n):1024 * (2 + n) + HJ * HE].rearrange("r (j e) -> r j e", e=HE) for n in range(2)]
        tmp = [wide_f[:, 4096 + n * NE:4096 + (n + 1) * NE] for n in range(6)]

        def planes(at, n):
            return wide_f[:, at * EPP:(at + n) * EPP].rearrange("p (h j) -> p h j", j=EPP)

        PU = wide_f[:, 0:2 * HEADS * EPP]
        AL, XLP = planes(0, HEADS), planes(HEADS, HEADS)
        AS = wide_f[:, 2 * HEADS * EPP:3 * HEADS * EPP]
        EXP_ = planes(2 * HEADS, HEADS)
        FW, BW = planes(3 * HEADS, HEADS), planes(4 * HEADS, HEADS)
        FILLP = planes(3 * HEADS, 2 * HEADS)
        EX = wide_f[:, 3 * HEADS * EPP:4 * HEADS * EPP]
        XL = wide_f[:, 0:HEADS * EPP]
        DI = [wide_f[:, (5 * HEADS + n) * EPP:(5 * HEADS + n + 1) * EPP].bitcast(I32) for n in range(3)]
        CF, CB, NF, NB = (wide_f[:, (6 * HEADS + n) * EPP:(6 * HEADS + n + 1) * EPP] for n in range(4))
        SCANS = ((2 * HEADS, 1), (HEADS, 2), (HEADS, 2))
        STEPS3 = 1 + TP * HEADS + 6 + 3 + 5
        CONSTS = 19
        w_loads = Count()
        wloop_f = wloop[:, :, :].rearrange("p j h -> p (j h)")

        block = ctx.enter_context(nc.Block())

        @block.sync
        def _(sp):
            sp.wait_ge(consts, 3)
            sp.dma_start(src_d[0:E].unsqueeze(0), t["src"].unsqueeze(0)).then_inc(filled, 16)
            sp.dma_start(src_d[E:EP].unsqueeze(0), fill_i[:, 0:EP - E]).then_inc(filled, 16)
            sp.dma_start(dst_d[1:1 + E].unsqueeze(0), t["dst"].unsqueeze(0)).then_inc(filled, 16)
            sp.dma_start(dst_d[1 + E:2 + EP].unsqueeze(0), mark_i[:, 1:2 + EP - E]).then_inc(filled, 16)
            sp.dma_start(dst_d[0:1].unsqueeze(0), mark_i[:, 0:1]).then_inc(filled, 16)

            sp.wait_ge(filled, 80)
            for to, a in ((lists[0], dst_d[1:1 + EP]), (lists[1], src_d)):
                sp.dma_start(to, a.rearrange("(j r e) -> r j e", r=HR, e=HE)).then_inc(lists_in, 16)

            ea0 = t["edge_attr_128"]
            ea16 = t["edge_attr_16"]

            def load_ea(g, i):
                sp.dma_start(slot_of(ea[:, i, :, :]), group_of(ea16[0:FULL * GE, :], g)).then_inc(ea_in, 16)

            def load_ea_tail(i, n):
                sp.dma_start(ea[:, i, 0:CW, :], ea16[FULL * GE:FULL * GE + HE, :].rearrange("(p c) k -> p c k", c=CW)
                              ).then_inc(ea_tail, 16)
                sp.wait_ge(ea_tail, 16 * n)
                sp.dma_start(ea[0:TAIL_P, i, CW:CH, :], ea16[E - TAIL:E, :].rearrange("(p c) k -> p c k", c=CW)
                              ).then_inc(ea_in, 16)

            def load_edges(g, i):
                sp.dma_start(slot_of(packed[i]), group_of(ea0[0:FULL * GE, :], g)).then_inc(rows_loaded[i], 16)

            def load_tail(i, first_done, done):
                sp.dma_start(packed[i][:, 0:CW, :], ea0[FULL * GE:FULL * GE + HE, :].rearrange("(p c) f -> p c f", c=CW)
                             ).then_inc(first_done, 16)
                if first_done is not done:
                    sp.wait_ge(first_done, 16)
                sp.dma_start(packed[i][0:TAIL_P, CW:CH, :], ea0[E - TAIL:E, :].rearrange("(p c) f -> p c f", c=CW)
                             ).then_inc(done, 16)

            for i in range(RING):
                load_ea(i, i)
            sp.wait_ge(consts, 4)

            def next_ea(u):
                sp.wait_ge(parts_ready, 5 * u + 2)
                for i in range(RING):
                    if isinstance(u, int) and RING * (u + 1) + i == FULL:
                        load_ea_tail(i, 1)
                    else:
                        load_ea(RING * (u + 1) + i, i)

            for i in range(RING):
                load_edges(i, i)
            next_ea(0)
            with sp.Fori(1, NIT - 2) as u:
                for i in range(RING):
                    sp.wait_ge(group_summed, RING * u + i - RING + 1)
                    load_edges(RING * u + i, i)
                    if i == 2:
                        next_ea(u)
            for g in range(NG - 2 * RING, NG):
                i = g % RING
                sp.wait_ge(group_summed, g - RING + 1)
                if g < FULL:
                    load_edges(g, i)
                else:
                    load_tail(i, tail_in, rows_loaded[i])
                if g == NG - RING - 2:
                    next_ea(NIT - 2)

            miss = sp.alloc_register("sp_missing")
            turn = sp.alloc_register("sp_turn")
            sp.reg_mov(turn, 0)

            def missing_groups(load, last):
                sp.wait_ge(dst_ready, 1)
                sp.reg_load(miss, missing_i[0:1, NG:NG + 1])
                with sp.If(sp.snap(miss, min_val=0, max_val=EP) > 0):
                    def group(g, load):
                        sp.reg_load(miss, missing_i[0:1, bass.ds(g, 1)])
                        with sp.If(sp.snap(miss, min_val=0, max_val=GE) > 0):
                            sp.reg_add(turn, turn, 1)
                            sp.wait_ge(x_done, sp.snap(turn, min_val=1, max_val=2 * NG + 1))
                            load(g)
                    with sp.Fori(0, NG - 1) as g:
                        group(g, load)
                    group(NG - 1, last)

            def x_edges(g):
                for h in range(HALF):
                    sp.dma_start(slot_of(packed[0])[:, :, h, :, :], group_of(ea0[0:FULL * GE, :], g)[:, :, h, :, :]
                                 ).then_inc(x_loaded, 16)
                    sp.dma_start(slot_of(ea[:, 0, :, :])[:, :, h, :, :], group_of(ea16[0:FULL * GE, :], g)[:, :, h, :, :]
                                 ).then_inc(x_loaded, 16)

            def x_tail(g):
                load_tail(0, x_loaded, x_loaded)
                sp.dma_start(ea[:, 0, 0:CW, :], ea16[FULL * GE:FULL * GE + HE, :].rearrange("(p c) f -> p c f", c=CW)
                             ).then_inc(x_loaded, 16)
                sp.dma_start(ea[0:TAIL_P, 0, CW:CH, :], ea16[E - TAIL:E, :].rearrange("(p c) f -> p c f", c=CW)
                             ).then_inc(x_loaded, 16)

            def x_attention(g):
                sp.dma_start(slot_of(att[:, 0, :, :]), group_of(at_d, g)).then_inc(x_loaded, 16)

            sp.wait_ge(parts_ready, 5 * NIT)
            sp.wait_ge(group_summed, SUMMED(L0 + 1))
            missing_groups(x_edges, x_tail)

            def load_rows(s_, a, free=None):
                def body(q, u, s, first):
                    if not first:
                        sp.wait_ge(free or s_.done, q - 1)
                    sp.dma_start(xb[:, s:s + 1, :, :], tiles_of(a, q)).then_inc(pair_landed[s], 16)
                pairs(sp, body)

            def load_rows_twice(s_, a):
                def body(q, u, s, first):
                    if not is_last(q):
                        if not (first and s == 0):
                            sp.wait_ge(s_.T, q)
                        sp.dma_start(xa[:, 1 - s:2 - s, :, :], tiles_of(a, q + 1)).then_inc(xa_landed[1 - s], 16)
                    if not first:
                        sp.wait_ge(s_.done, q - 1)
                    sp.dma_start(xb[:, s:s + 1, :, :], tiles_of(a, q)).then_inc(pair_landed[s], 16)
                sp.dma_start(xa[:, 0:1, :, :], tiles_of(a, 0)).then_inc(xa_landed[0], 16)
                pairs(sp, body)

            def stored(s_):
                for s in range(2):
                    sp.wait_ge(*s_.stored(s, (NP + 1 - s) // 2))

            def load_dense(k, a):
                if k > 0:
                    sp.wait_ge(slice_used, SL * NS * k)
                for s in range(SL):
                    full = min((s + 1) * QS * P, N // P * P)
                    to = table[:, s, 0:full - s * QS * P].rearrange("p (q f) -> p q f", f=P)
                    sp.dma_start(to, a[s * QS * P:full, :].rearrange("(q r) f -> r q f", r=P)).then_inc(slice_in[s], 16)
                sp.wait_ge(table_zero, k + 1)
                sp.dma_start(table[0:N % P, SL - 1, (QS - 1) * P:QS * P], a[N // P * P:N, :]).then_inc(slice_in[SL - 1], 16)

                def load_slice(t, s):
                    sp.dma_start(slices[:, s, :, :], batch_pair(t, s)).then_inc(slice_in[s], 16)

                for s in range(SL):
                    sp.wait_ge(low_ready, SL * k + s + 1)
                    load_slice(0, s)
                with sp.Fori(1, NS) as t:
                    for s in range(SL):
                        sp.wait_ge(slice_used, SL * (NS * k + t - 1) + s + 1)
                        load_slice(t, s)

            load_rows_twice(d0, t["x"])
            sp.wait_ge(d0.done, NP)
            stored(d0)
            for n in range(2):
                sp.wait_ge(adj_stored[n], 16 * NIT // 2)
            sp.wait_ge(prep_dve, 9)
            sp.wait_ge(push_zeroed, 16 * 2 * HEADS)
            load_dense(0, x1_d)
            sp.wait_ge(node_sums, 1 + PIECES)
            sp.dma_start(sums_d, nsum[0:1 + HEADS, 0:N]).then_inc(sums_out, 16)
            load_rows(d1a, x1_d, d1a.T)
            sp.wait_ge(sums_out, 16)
            sp.dma_start(cntB[:, :, :], sums_d.rearrange("k (j p) -> j k p", p=TN)).then_inc(sums_in, 16)
            sp.wait_ge(d1a.done, NP)
            load_rows(d1c, x1_d)
            sp.wait_ge(node_rc, 1)
            sp.dma_start(rcnt_d.rearrange("(j p) -> j p", p=TN), rcB[:, :]).then_inc(sums_out, 16)
            sp.wait_ge(sums_out, 32)
            sp.wait_ge(d1c.done, NP)
            sp.dma_start(rcnt, rcnt_d.unsqueeze(0).to_broadcast([P, N])).then_inc(sums_in, 16)
            stored(d1c)

            load_dense(1, x2_d)

            load_rows_twice(d2a, x2_d)
            sp.wait_ge(d2a.done, NP)
            stored(d2a)
            load_dense(2, z_d)
            load_rows(d2b, q_d, d2b.h)

            def store_xe(g, i):
                for h in range(HALF):
                    sp.dma_start(group_of(xe_d, g)[:, :, h, :, :], rows[:, i:i + 1, CW * h:CW * (h + 1), 0:P]).then_inc(xe_stored[i], 16)

            for n in range(3):
                sp.wait_ge(d2b.done, NP)
                sp.dma_start(DI[n], dst_d[n:n + EP].rearrange("(p j) -> p j", p=P)).then_inc(scan_in, 16)
            sp.wait_ge(pushed, 16 * NT)
            sp.dma_start(PU, push_d.rearrange("(p j) h -> p (j h)", p=P)).then_inc(scan_in, 16)

            with sp.Fori(0, NIT) as u:
                for i in range(RING):
                    sp.wait_ge(asum_ready, RING * u + i + 1)
                    store_xe(RING * u + i, i)
            for i in range(RING):
                sp.wait_ge(xe_stored[i], 16 * HALF * NIT)
                sp.wait_ge(as_stored[i], 16 * NIT)
            sp.dma_start(AS, as_d.rearrange("(p j) h -> p (j h)", p=P)).then_inc(scan_in, 16)
            sp.wait_ge(scan_done, 1)
            sp.dma_start(at_d.rearrange("(p j) h -> p (j h)", p=P), EX).then_inc(scan_out, 16)
            sp.dma_start(wl_d.rearrange("(p j) h -> p (j h)", p=P), XL).then_inc(scan_out, 16)
            sp.wait_ge(scan_out, 32)

            def load_c3(g, u, i):
                sp.dma_start(slot_of(packed[i]), group_of(xe_d, g)).then_inc(rows_loaded[i], 16)
                sp.dma_start(slot_of(att[:, i, :, :]), group_of(at_d, g)).then_inc(att_landed[i], 16)

            for i in range(RING):
                load_c3(i, 0, i)
            with sp.Fori(1, NIT) as u:
                for i in range(RING):
                    sp.wait_ge(group_summed, SUMMED(C3) + RING * u + i - RING + 1)
                    load_c3(RING * u + i, u, i)
            sp.wait_ge(psum_free, FREED(C3 + 1))
            missing_groups(x_attention, x_attention)
            load_rows(d3, t3_d)

        @block.gpsimd
        def _(pool):
            pool.memset(ident[:, :], 0.0).then_inc(consts, 1)
            pool.memset(fill_i, 0).then_inc(consts, 1)
            pool.memset(mark_i, NOWHERE).then_inc(consts, 1)
            pool.memset(rows[:, :, :, :], 0.0).then_inc(consts, 1)
            pool.memset(ones[:, :], 1.0).then_inc(consts, 1)
            pool.memset(tri[:, :], 1.0).then_inc(consts, 1)
            pool.memset(to_scores[:, :], 0.0).then_inc(consts, 1)
            pool.iota(iota_w[:, :], pattern=[[1, W]], base=0, channel_multiplier=0,
                      allow_small_or_imprecise_dtypes=True).then_inc(consts, 1)
            pool.wait_ge(consts, 8)
            pool.affine_select(out=ident[:, :], in_=ident[:, :], compare_op=ALU.not_equal, fill=1.0, base=0,
                               pattern=[[-1, P]], channel_multiplier=1).then_inc(consts, 1)
            pool.affine_select(out=tri[:, :], in_=tri[:, :], compare_op=ALU.is_gt, fill=0.0, base=0,
                               pattern=[[1, NT]], channel_multiplier=-1).then_inc(consts, 1)
            pool.memset(one_ea[:, :, :], 1.0).then_inc(consts, 1)
            pool.memset(to_scores[0:1, 0:1], 1.0).then_inc(consts, 1)
            pool.memset(parts[:, :, :, :], 1.0).then_inc(consts, 1)
            pool.memset(zeros, 0.0).then_inc(consts, 1)
            pool.memset(row2[:, :, :], 0.0).then_inc(consts, 1)
            pool.memset(wloop[:, :, :], 1.0).then_inc(consts, 1)
            pool.memset(yb[:, :, :, :], 0.0).then_inc(consts, 1)
            pool.memset(norm_eps[:, :], NORM_EPS).then_inc(consts, 1)
            pool.iota(iota_k[:, :], pattern=[[1, KW]], base=0, channel_multiplier=0,
                      allow_small_or_imprecise_dtypes=True).then_inc(consts, 1)

            def stored(s_):
                for s in range(2):
                    pool.wait_ge(*s_.stored(s, (NP + 1 - s) // 2))

            def store_rows(s_, jobs):
                def body(q, u, s, first):
                    pool.wait_ge(s_.done, q + 1)
                    for buf, a, width in jobs:
                        pool.dma_start(tiles_of(a, q, width), buf[:, s:s + 1, :, 0:width]).then_inc(pair_stored[s], 16)
                pairs(pool, body)
                stored(s_)

            idx_next = pool.alloc_register("idx_next")
            pool.reg_mov(idx_next, 1)
            miss = pool.alloc_register("pool_missing")
            turn = pool.alloc_register("pool_turn")
            pool.reg_mov(turn, 1)

            def gather_chunk(i, c, table, width, done):
                pool.indirect_dma_start(out=packed[i][:, c, :] if width == P else rows[:, i, c, :], out_offset=None, in_=table,
                                        in_offset=bass.IndirectOffsetOnAxis(ap=idx[:, i, c:c + 1], axis=0)).then_inc(done, 16)

            def gather(table, width):
                with pool.Fori(0, NIT):
                    for i in range(RING):
                        pool.wait_ge(idx_ready, pool.snap(idx_next, min_val=1, max_val=1 << 20))
                        pool.reg_add(idx_next, idx_next, 1)
                        for c in range(CH):
                            gather_chunk(i, c, table, width, rows_landed[i])
                pool.reg_add(idx_next, idx_next, RING)

            def missing_groups(table, width=P):
                pool.wait_ge(dst_ready, 1)
                pool.reg_load(miss, missing_i[0:1, NG:NG + 1])
                with pool.If(pool.snap(miss, min_val=0, max_val=EP) > 0):
                    with pool.Fori(0, NG) as g:
                        pool.reg_load(miss, missing_i[0:1, bass.ds(g, 1)])
                        with pool.If(pool.snap(miss, min_val=0, max_val=GE) > 0):
                            pool.wait_ge(x_idx, pool.snap(turn, min_val=1, max_val=1 << 20))
                            pool.reg_add(turn, turn, 1)
                            for c in range(CH):
                                gather_chunk(0, c, table, width, x_rows)

            onehots = pool.alloc_register("pool_onehots")
            pool.reg_mov(onehots, RING + 1)
            features = pool.alloc_register("pool_features")
            pool.reg_mov(features, 16 * RING * 3)
            summed = pool.alloc_register("pool_summed")
            pool.reg_mov(summed, 1)
            splits = pool.alloc_register("pool_splits")
            pool.reg_mov(splits, 1)

            def after_split():
                pool.wait_ge(parts_ready, pool.snap(splits, min_val=1, max_val=5 * NIT))
                pool.reg_add(splits, splits, 1)

            def onehots_b(u=None):
                for i in range(RING):
                    if u is None:
                        pool.wait_ge(group_summed, pool.snap(summed, min_val=1, max_val=NG))
                        pool.reg_add(summed, summed, 1)
                        pool.wait_ge(onehot_ready, pool.snap(onehots, min_val=1, max_val=NG))
                        pool.reg_add(onehots, onehots, 1)
                    else:
                        if u:
                            pool.wait_ge(group_summed, RING * (u - 1) + i + 1)
                        pool.wait_ge(onehot_ready, RING * u + i + 1)
                    pool.tensor_copy(onehot_b[:, i, :, :], onehot[:, i, :, :]).then_inc(onehot_b_ready, 1)

            def split(u, s):
                whole = ea[:, :, :, :].rearrange("p i c f -> p (i c) f")
                part = [parts[:, s, :, 1 + EF * n:1 + EF * (n + 1)] for n in range(3)]
                if isinstance(u, int):
                    pool.wait_ge(ea_in, 16 * RING * (u + 1))
                else:
                    pool.wait_ge(ea_in, pool.snap(features, min_val=1, max_val=16 * NG))
                    pool.reg_add(features, features, 16 * RING)
                for n in range(3):
                    if n:
                        after_split()
                        pool.tensor_tensor(left[:, :, :], whole if n == 1 else left[:, :, :], part[n - 1], ALU.subtract).then_inc(parts_ready, 1)
                    if not (isinstance(u, int) and u + n == 0):
                        after_split()
                    pool.tensor_copy(part[n], left[:, :, :] if n else whole).then_inc(parts_ready, 1)

            pool.wait_ge(consts, CONSTS)
            split(0, 0)
            onehots_b(0)
            split(1, 1)
            with pool.Fori(0, NIT // 2 - 1) as k:
                for s in range(2):
                    onehots_b()
                    split(2 * k + 2 + s, s)
            onehots_b(NIT - 1)

            store_rows(d0, [(yb, x1_d, P)])
            missing_groups(x1_d)
            store_rows(d1c, [(yb, x2_d, P)])
            missing_groups(x2_d)
            store_rows(d2a, [(yb, z_d, P), (zb, q_d, P)])
            missing_groups(z_d)
            pool.wait_ge(push_zeroed, 16 * 2 * HEADS)
            for q in range(NP):
                pool.wait_ge(d2b.done, q + 1)
                pool.dma_start(tiles_of(t3_d, q, ROW3), yb[:, q % 2:q % 2 + 1, :, 0:ROW3]).then_inc(pair_stored[q % 2], 16)
                for j in range(TP * q, TP * (q + 1)):
                    pool.indirect_dma_start(
                        out=push_d, out_offset=bass.IndirectOffsetOnAxis(ap=beg_i[:, j:j + 1], axis=0),
                        in_=push[:, j, :], in_offset=None, bounds_check=EP - 1, oob_is_err=False).then_inc(pushed, 16)
            stored(d2b)

            gather(t3_d, ROW3)

            pool.wait_ge(scan_out, 32)
            for j in range(NT):
                pool.indirect_dma_start(
                    out=wloop[:, j, :], out_offset=None, in_=wl_d,
                    in_offset=bass.IndirectOffsetOnAxis(ap=end_i[:, j:j + 1], axis=0),
                    bounds_check=EP - 1, oob_is_err=False).then_inc(wl_in, 16)

            missing_groups(t3_d, ROW3)

            def store_out(q, u, s, first):
                pool.wait_ge(d3.done, q + 1)
                pool.dma_start(tiles_of(out, q), yb[:, s:s + 1, :, 0:P]).then_inc(pair_stored[s], 16)
            pairs(pool, store_out)
            stored(d3)

        @block.scalar
        def _(act):
            def load(dst, src):
                w_loads.up()
                act.dma_start(dst, src).then_inc(w_in, 16)

            def load_col(at, src, n):
                load(col[:, at:at + n], src.rearrange("(m p) -> p m", p=P))

            for to, a in ((we[:, :, :], t["L3_gnn_W_edge"].rearrange("k (h c) -> k h c", c=P)),
                          (ae_b[:, :, :].rearrange("p h c -> p (h c)"),
                           t["L3_gnn_att_edge"].rearrange("h c -> (h c)").unsqueeze(0).to_broadcast([EF, HEADS * P]))):
                act.dma_start(to, a).then_inc(we_in, 16)

            with nc.allow_non_contiguous_dma(reason="biases by feature"):
                load(w01[:, :, :], t["L0_gnn_W1"].rearrange("(k p) m -> p k m", p=P))
                load(w02[:, :, :], t["L0_gnn_W2"].rearrange("(k p) m -> p k m", p=P))
                load_col(b01, t["L0_gnn_b1"], H0)
                act.wait_ge(consts, CONSTS)
                load(row2[:, 0, :], t["L0_gnn_b2"].unsqueeze(0))
                load(row2[:, 2, :], t["L2_gnn_b2"].unsqueeze(0))
                load(row2[:, 3, :], t["L3_gnn_lin_b"].unsqueeze(0))
                load(w11[:, :], t["L1_gnn_W1"])
                load(w12[:, :, :], t["L1_gnn_W2"].rearrange("(k p) m -> p k m", p=P))
                for at, name, n in ((b11, "L1_gnn_b1", H1), (g11, "L1_gnn_g1", H1), (e11, "L1_gnn_be1", H1),
                                    (b12, "L1_gnn_b2", 1), (g12, "L1_gnn_g2", 1), (e12, "L1_gnn_be2", 1),
                                    (b21, "L2_gnn_b1", H1), (gatb, "L3_gnn_gat_bias", HEADS)):
                    load_col(at, t[name], n)
                load(eps1, t["L1_gnn_eps"].to_broadcast([P, 1]))
                load(w21[:, 0, :], t["L2_gnn_W1_l"])
                load(w21[:, 1, :], t["L2_gnn_W1_r"])
                load(w22[:, :, 0, :], t["L2_gnn_W2_l"].rearrange("(k p) m -> p k m", p=P))
                load(w22[:, :, 1, :], t["L2_gnn_W2_r"].rearrange("(k p) m -> p k m", p=P))
                for n, name in enumerate(("L3_gnn_ln_g", "L3_gnn_ln_b")):
                    load(ln_gb[:, n, :], t[name].unsqueeze(0).to_broadcast([TN, P]))
            for k in range(2 * HEADS):
                act.dma_start(push_d.rearrange("(p j) h -> p (j h)", p=P)[:, k * EPP:(k + 1) * EPP], zeros
                              ).then_inc(push_zeroed, 16)

            def copy_batch(u, v, s, first):
                if not first:
                    act.wait_ge(adj_stored[s], 16 * v)
                for n in range(AH):
                    act.wait_ge(key_summed, 4 + AH * u + n + 1)
                    for k, (lo, hi) in enumerate(KEY_PARTS):
                        op = act.activation(part_a[s][:, lo:hi, W * n:W * (n + 1)],
                                            ps_k[n % 2][k][:, 0:(hi - lo) * W].rearrange("p (q w) -> p q w", w=W), ACT.Copy)
                    op.then_inc(key_copied, 1)
                act.wait_ge(key_copied, 2 + AH * (u + 1))
                act.dma_start(adj_d[bass.ds(u, 1), :, :].rearrange("b r w -> r b w"),
                              part_a[s].rearrange("p q w -> p (q w)").unsqueeze(1)).then_inc(adj_stored[s], 16)

            act.wait_ge(dst_ready, 1)
            for n in range(3):
                act.dma_start(to_scores[1 + EF * n:1 + EF * (n + 1), 1:1 + HEADS], we3[:, :]).then_inc(we_in, 16)
            for n in range(2):
                copy_batch(n, 0, n, True)
            with act.Fori(1, NIT // 2 - 1) as v:
                for n in range(2):
                    copy_batch(2 * v + n, v, n, False)
            for n in range(2):
                copy_batch(NIT - 2 + n, NIT // 2 - 1, n, False)
            for n in range(2):
                act.wait_ge(adj_stored[n], 16 * NIT // 2)
            act.wait_ge(key_ready, NH + HALF)
            load(w3[:, :, :].rearrange("p h c -> p (h c)"), t["L3_gnn_W"])
            load(lin[:, :, :], t["L3_gnn_lin_W"].rearrange("(h p) m -> p h m", p=P))
            for n, name in enumerate(("L3_gnn_att_src", "L3_gnn_att_dst")):
                load(att_b[:, n, :, :].rearrange("p h c -> p (h c)"),
                     t[name].rearrange("h c -> (h c)").unsqueeze(0).to_broadcast([P, HEADS * P]))

            def deviations(s_, s, steps):
                act.wait_ge(s_.step, steps)
                act.activation(rstd[:, s, :], mv[:, s, :, 1], ACT.Sqrt, bias=norm_eps[0:TN, :]).then_inc(root, 1)

            def rows_T(s_, n_h, q, s):
                act.wait_ge(s_.T, q + 1)
                if not (isinstance(q, int) and q < 2):
                    act.wait_ge(s_.H, n_h * (q - 1))
                act.activation(xT[:, s, :], ps_t[s], ACT.Copy).then_inc(s_.xT, 1)

            def hidden0(q, u, s, first):
                if not is_last(q):
                    rows_T(d0, H0, q + 1, 1 - s)
                if not first:
                    deviations0(q - 2, s)
                    act.wait_ge(d0.Y, q - 1)
                for m in range(H0):
                    act.wait_ge(d0.H, H0 * q + m + 1)
                    act.activation(hT[:, s, m, :], ps_h[m], ACT.Relu, bias=col[:, b01 + m:b01 + m + 1]).then_inc(d0.h, 1)

            act.wait_ge(w_in, 16 * w_loads.n)

            def deviations0(q, s):
                deviations(d0, s, 6 * q + 5)
            rows_T(d0, H0, 0, 0)
            pairs(act, hidden0)
            deviations0(NP - 2, 1)
            deviations0(NP - 1, 0)

            def high_parts(k):
                act.wait_ge(scaled, SCALED[k])
                for s in range(SL):
                    act.wait_ge(slice_in[s], slices_in(s, k) + (32 if s == SL - 1 else 16))
                    act.activation(high_low[:, 0, QS * s:QS * (s + 1), :].rearrange("p q f -> p (q f)"), table[:, s, 0:QS * P],
                                   ACT.Copy, scale=scale[:, 0:1]).then_inc(high_ready, 1)

            high_parts(0)

            def hidden1(q, u, s, first):
                for m in range(H1):
                    act.wait_ge(d1a.H, H1 * q + m + 1)
                    act.activation(blk(wide[:, m, :], q), ps_h[2 * s + m], ACT.Identity,
                                   bias=col[:, b11 + m:b11 + m + 1]).then_inc(d1a.h, 1)
            act.wait_ge(sums_out, 16)
            pairs(act, hidden1)

            def norm1(q, u, s, first):
                if not first:
                    act.wait_ge(d1b.Y, q - 1)
                for m in range(H1):
                    act.activation(hT[:, s, m, :], blk(wide[:, m, :], q), ACT.Relu, bias=bns[:, m, 1:2],
                                   scale=bns[:, m, 0:1]).then_inc(d1b.h, 1)
            act.wait_ge(bn_var, 1)
            act.activation(bns[:, 0:H1, 1], bns[:, 0:H1, 1], ACT.Sqrt, bias=norm_eps[:, :]).then_inc(bn_root, 1)
            act.wait_ge(bn_ready, 1)
            pairs(act, norm1)

            def deviations1(q, s):
                deviations(d1c, s, 7 * q + 6)

            def norm2(q, u, s, first):
                if not first:
                    act.wait_ge(d1c.Y, q - 1)
                act.activation(xT[:, s, :], blk(wide[:, 0, :], q), ACT.Identity, bias=bns[:, H1, 1:2],
                               scale=bns[:, H1, 0:1]).then_inc(d1c.xT, 1)
                if not (first and s == 0):
                    deviations1(q - 1, 1 - s)
            act.wait_ge(bn_var, 2)
            act.activation(bns[:, H1, 1:2], bns[:, H1, 1:2], ACT.Sqrt, bias=norm_eps[:, :]).then_inc(bn_root, 1)
            act.wait_ge(bn_ready, 2)
            pairs(act, norm2)
            deviations1(NP - 1, 0)

            high_parts(1)
            def hidden2(q, u, s, first):
                if not is_last(q):
                    rows_T(d2a, H1, q + 1, 1 - s)
                if not first:
                    act.wait_ge(d2a.Y, q - 1)
                for m in range(H1):
                    act.wait_ge(d2a.H, H1 * q + m + 1)
                    act.activation(hT[:, s, m, :], ps_h[2 * s + m], ACT.Relu,
                                   bias=col[:, b21 + m:b21 + m + 1]).then_inc(d2a.h, 1)
            rows_T(d2a, H1, 0, 0)
            pairs(act, hidden2)

            high_parts(2)

            def x3T(q, u, s, first):
                deviations(d2b, s, steps2b(q) + 5)
                act.wait_ge(d2b.T, q + 1)
                act.activation(xT[:, s, :], ps_t[s], ACT.Copy).then_inc(d2b.xT, 1)
            pairs(act, x3T)

            ea16 = t["edge_attr_16"]

            def load_ea(g, i):
                act.dma_start(slot_of(ea[:, i, :, :]), group_of(ea16[0:FULL * GE, :], g)).then_inc(ea_landed[i], 16)

            def load_ea_tail(i, n):
                act.dma_start(ea[:, i, 0:CW, :], ea16[FULL * GE:FULL * GE + HE, :].rearrange("(p c) k -> p c k", c=CW)
                              ).then_inc(ea_tail, 16)
                act.wait_ge(ea_tail, 16 * n)
                act.dma_start(ea[0:TAIL_P, i, CW:CH, :], ea16[E - TAIL:E, :].rearrange("(p c) k -> p c k", c=CW)
                              ).then_inc(ea_landed[i], 16)

            for i in range(RING):
                load_ea(i, i)

            def store_as(g, i):
                act.wait_ge(asum_ready, g + 1)
                act.dma_start(group_of(as_d, g), slot_of(asum[:, i, :, :])).then_inc(as_stored[i], 16)

            with act.Fori(0, NIT - 2) as u:
                for i in range(RING):
                    store_as(RING * u + i, i)
                    load_ea(RING * (u + 1) + i, i)
            for i in range(RING):
                g = NG - 2 * RING + i
                store_as(g, i)
                if g + RING < FULL:
                    load_ea(g + RING, i)
                else:
                    load_ea_tail(i, 2)
            for i in range(RING):
                store_as(NG - RING + i, i)

            act.wait_ge(scan_exp, 1)
            act.activation(EXP_, EXP_, ACT.Exp).then_inc(scan_act, 1)
            act.wait_ge(scan_exp, 2)
            act.activation(XLP, XLP, ACT.Exp).then_inc(scan_act, 1)

            act.wait_ge(psum_free, FREED(C3 + 1))

            def deviations3(q, s):
                n = STEPS3 * q + 1 + TP * HEADS
                deviations(d3, s, n + 4)
                deviations(d3, s, n + 6 + 3 + 4)

            def operands3(q, u, s, first):
                act.wait_ge(d3.T, q + 1)
                if not first:
                    act.wait_ge(d3.Y, q - 1)
                act.activation(xT[:, s, :], ps_t[s], ACT.Copy).then_inc(d3.xT, 1)
                act.activation(aT[:, s, :, :], wide[:, :, bass.ds(PN * q, PN)], ACT.Copy).then_inc(d3.a, 1)
                if not (first and s == 0):
                    deviations3(q - 1, 1 - s)
            pairs(act, operands3)
            deviations3(NP - 1, 0)

        @block.tensor
        def _(pe):
            extra = pe.alloc_register("pe_extra")
            pe.reg_mov(extra, 1)
            miss = pe.alloc_register("pe_missing")
            turn = pe.alloc_register("pe_turn")
            pe.reg_mov(turn, 1)
            gathered = pe.alloc_register("pe_gathered")
            pe.reg_mov(gathered, 16 * CH)

            pe.wait_ge(consts, CONSTS)
            for n in range(2):
                pe.wait_ge(prep_dve, n + 1)
                for c in range(CW):
                    for j in range(HJ):
                        mm = pe.transpose(ps[2 * n + c][:, HR * j:HR * (j + 1)],
                                          lists_f[n][:, j, :].rearrange("r (p c) -> r c p", c=CW)[:, c, :], ident[0:HR, 0:HR])
                mm.then_inc(prep_pe, 1)
            pe.wait_ge(prep_dve, 3)
            pe.matmul(ps_m[:, 0:NH], ones[0:1, 0:P], base_f[:, :], start=True, stop=True).then_inc(prep_pe, 1)
            pe.wait_ge(prep_dve, 4)
            pe.matmul(ps[6][0:1, 0:NG], ones[:, 0:1], missed[:, :], start=True, stop=True).then_inc(prep_pe, 1)
            pe.wait_ge(prep_dve, 5)
            pe.matmul(ps_m[:, 0:HEADS * EF], ones[0:EF, 0:P], we_d[:, :, :].rearrange("k h e -> k (h e)"),
                      start=True, stop=True).then_inc(prep_pe, 1)
            pe.wait_ge(prep_dve, 6)
            pe.wait_ge(dst_ready, 1)

            def sums(a, sums_too=False, weigh=False, adjacency=False):
                width = HEADS * W if weigh else W

                def half(ha, n, h):
                    pe.wait_ge(key_ready, ha + 1)
                    pe.wait_ge(key_copied, ha + 1)
                    for k, (lo, hi) in enumerate(KEY_PARTS):
                        for c in range(CW):
                            mm = pe.matmul(ps_k[h][k][:, 0:(hi - lo) * W], row_1h[:, n, c, :], key_1h[n][:, c, lo * W:hi * W],
                                           start=(c == 0), stop=(c == CW - 1))
                    mm.then_inc(key_summed, 1)

                def iteration(u, s):
                    for i in range(RING):
                        g = RING * u + i
                        if adjacency:
                            for h in range(HALF):
                                half(HALF * g + h, (HALF * i + h) % 4, h)
                        if weigh:
                            pe.wait_ge(weighted_ready, g + 1)
                        else:
                            pe.wait_ge(onehot_ready, ONEHOTS(a) + g + 1)
                        if sums_too:
                            pe.wait_ge(ps_zero, RING)
                            pe.wait_ge(parts_ready, 5 * (u + 1))
                            pe.wait_ge(onehot_b_ready, g + 1)
                        pe.wait_ge(*arrived(a, i, u))
                        pe.wait_ge(psum_free, HALF * (SUMMED(a) + g + 1))
                        for h in range(HALF):
                            for c in range(CW):
                                n = CW * h + c
                                operand = weighted[:, i, n, :, :].rearrange("p h w -> p (h w)") if weigh else onehot[:, i, n, :]
                                mm = pe.matmul(ps_a[i][:, width * h:width * (h + 1)], packed[i][:, n, :], operand,
                                               start=(c == 0), stop=(c == CW - 1))
                            if sums_too:
                                for c in range(CW):
                                    n = CW * h + c
                                    mm = pe.matmul(ps_n[i][:, W * h:W * (h + 1)], parts[:, s, CH * i + n, :], onehot_b[:, i, n, :],
                                                   start=(c == 0), stop=(c == CW - 1))
                        mm.then_inc(group_summed, 1)

                steps = 2 if sums_too else 1
                with pe.Fori(0, NIT // steps) as k:
                    for s in range(steps):
                        iteration(steps * k + s, s)
                pe.wait_ge(psum_free, FREED(a + 1))
                if adjacency:
                    pe.wait_ge(key_copied, 2 + NH)

            def missing_groups(loaded=False, sums_too=False, weigh=False):
                pe.reg_load(miss, missing_i[0:1, NG:NG + 1])
                with pe.If(pe.snap(miss, min_val=0, max_val=EP) > 0):
                    with pe.Fori(0, NG) as g:
                        pe.reg_load(miss, missing_i[0:1, bass.ds(g, 1)])
                        with pe.If(pe.snap(miss, min_val=0, max_val=GE) > 0):
                            if loaded:
                                pe.wait_ge(x_scored, pe.snap(turn, min_val=1, max_val=1 << 20))
                                pe.reg_add(turn, turn, 1)
                            else:
                                pe.wait_ge(x_rows, pe.snap(gathered, min_val=1, max_val=1 << 20))
                                pe.reg_add(gathered, gathered, 16 * CH)
                            with pe.Fori(0, NK):
                                pe.wait_ge(x_onehot, pe.snap(extra, min_val=1, max_val=1 << 20))
                                for c in range(CH):
                                    operand = weighted_x[:, c, :, :].rearrange("p h w -> p (h w)") if weigh else onehot_x[:, c, :]
                                    mm = pe.matmul(ps_x[:, 0:HEADS * W if weigh else W], rows[:, 0, c, 0:P] if weigh else packed[0][:, c, :], operand,
                                                   start=(c == 0), stop=(c == CH - 1))
                                if sums_too:
                                    for c in range(CH):
                                        mm = pe.matmul(ps_xn, one_ea[:, c, :], onehot_x[:, c, :], start=(c == 0), stop=(c == CH - 1))
                                mm.then_inc(x_summed, 1)
                                pe.wait_ge(x_added, pe.snap(extra, min_val=1, max_val=1 << 20))
                                pe.reg_add(extra, extra, 1)

            def scale_products():
                pe.wait_ge(table_max, 1)
                pe.transpose(ps_m[0:1, 0:P], tmax[:, 0:1], ident[:, :]).then_inc(scale_pe, 1)
                pe.wait_ge(table_max, 2)
                pe.matmul(ps_m[:, P:P + 2], ones[0:1, 0:P], pow2[:, :], start=True, stop=True).then_inc(scale_pe, 1)

            def dense(k):
                pe.wait_ge(low_ready, SL * (k + 1))

                def dense_step(t, b, first):
                    if not first:
                        pe.wait_ge(win_added, TB * AH * (NS * k + t - 1))
                    for s in range(SL):
                        pe.wait_ge(slice_in[s], slices_in(s, k) + (32 if s == SL - 1 else 16) + 16 * (t + 1))
                        for q in range(QS):
                            for part in range(2):
                                mm = pe.matmul(ps_d[b], high_low[:, part, QS * s + q, :], slices[:, s, :, AW * q:AW * (q + 1)],
                                               start=(s == 0 and q == 0 and part == 0),
                                               stop=(s == SL - 1 and q == QS - 1 and part == 1))
                        mm.then_inc(slice_used, 1)

                for b in range(2):
                    dense_step(b, b, True)
                with pe.Fori(1, NS // 2) as v:
                    for b in range(2):
                        dense_step(2 * v + b, b, False)
                pe.wait_ge(win_added, TB * AH * NS * (k + 1))

            def transpose_rows(s_, q, u, s, buf=xb):
                pe.wait_ge(*(xa_in(s_, s, u) if buf is xa else s_.landed(s, u)))
                for k in range(TP):
                    mm = pe.transpose(ps_t[s][:, TN * k:TN * (k + 1)], buf[:, s, k, :], ident[0:TN, 0:TN])
                mm.then_inc(s_.T, 1)

            sums(L0, sums_too=True, adjacency=True)
            missing_groups(loaded=True, sums_too=True)
            pe.wait_ge(w_in, 16 * w_loads.n)

            def second0(q, s):
                pe.wait_ge(d0.h, H0 * (q + 1))
                if not (isinstance(q, int) and q < 2):
                    pe.wait_ge(d0.done, q - 1)
                for k in range(TP):
                    for m in range(H0):
                        pe.matmul(ps_y[s][:, k, :], hT[:, s, m, TN * k:TN * (k + 1)], w02[:, m, :], start=(m == 0), stop=False)
                    mm = pe.matmul(ps_y[s][:, k, :], ones[0:1, 0:TN], row2[:, 0, :], start=False, stop=True)
                mm.then_inc(d0.Y, 1)

            def layer0(q, u, s, first):
                if not is_last(q):
                    transpose_rows(d0, q + 1, u + s, 1 - s, xa)
                pe.wait_ge(d0.xT, q + 1)
                for m in range(H0):
                    if not (first and s == 0):
                        pe.wait_ge(d0.h, H0 * (q - 1) + m + 1)
                    pe.matmul(ps_h[m], w01[:, 0, m * P:(m + 1) * P], blk(wide[:, 2, :], q), start=True, stop=False)
                    pe.matmul(ps_h[m], w01[:, 1, m * P:(m + 1) * P], xT[:, s, :], start=False, stop=True).then_inc(d0.H, 1)
                if not (first and s == 0):
                    second0(q - 1, 1 - s)
            transpose_rows(d0, 0, 0, 0, xa)
            pairs(pe, layer0, 4)
            second0(NP - 1, (NP - 1) % 2)

            pe.wait_ge(d0.done, NP)
            pe.wait_ge(we_in, 32 + 48)
            for k in range(PIECES):
                if k >= 2:
                    pe.wait_ge(node_sums, 1 + k - 1)
                at = slice(512 * k, min(512 * (k + 1), N))
                pe.matmul(ps[1 + k % 2][0:1 + HEADS, 0:at.stop - at.start], to_scores[:, :], nsum[:, at], start=True, stop=True
                          ).then_inc(sums_pe, 1)
            for h in range(HEADS):
                mm = pe.transpose(ps[6][:, h * P:(h + 1) * P], w3[:, h, :], ident[:, :])
            mm.then_inc(prep_pe, 1)
            pe.wait_ge(prep_dve, 7)
            for h in range(HEADS):
                mm = pe.matmul(ps[6][:, h * P:(h + 1) * P], w3T[:, h, :], lin[:, h, :], start=True, stop=True)
            mm.then_inc(prep_pe, 1)
            for h in range(HEADS):
                mm = pe.matmul(ps_m[0:1, 256:256 + P], col[:, gatb + h:gatb + h + 1], lin[:, h, :],
                               start=(h == 0), stop=(h == HEADS - 1))
            mm.then_inc(prep_pe, 1)
            pe.wait_ge(prep_dve, 9)

            dense(0)
            missing_groups()

            def layer1(q, u, s, first):
                if not is_last(q):
                    transpose_rows(d1a, q + 1, u + s, 1 - s)
                pe.wait_ge(d1a.a, q + 1)
                if not first:
                    pe.wait_ge(d1a.h, H1 * (q - 1))
                for m in range(H1):
                    pe.matmul(ps_h[2 * s + m], w11[:, m * P:(m + 1) * P], aT[:, s, 0, :], start=True, stop=True).then_inc(d1a.H, 1)
            transpose_rows(d1a, 0, 0, 0)
            pairs(pe, layer1)

            def layer1b(q, u, s, first):
                pe.wait_ge(d1b.h, H1 * (q + 1))
                if not first:
                    pe.wait_ge(d1b.xT, q - 1)
                for m in range(H1):
                    mm = pe.matmul(ps_b[s], w12[:, m, :], hT[:, s, m, :], start=(m == 0), stop=(m == H1 - 1))
                mm.then_inc(d1b.Y, 1)
            pairs(pe, layer1b)

            def layer1c(q, u, s, first):
                pe.wait_ge(d1c.xT, q + 1)
                if not first:
                    pe.wait_ge(d1c.done, q - 1)
                for k in range(TP):
                    mm = pe.transpose(ps_y[s][:, k, :], xT[:, s, TN * k:TN * (k + 1)], ident[:, :])
                mm.then_inc(d1c.Y, 1)
            pairs(pe, layer1c)

            pe.wait_ge(node_dve, 1)
            pe.matmul(ps_m[0:NT, 0:1], tri[:, :], totB[:, :], start=True, stop=True).then_inc(node_pe, 1)
            pe.wait_ge(node_dve, 2)
            for n, a in enumerate((begB[:, :], endB[:, :], *(meanB[:, h, :] for h in range(HEADS)))):
                mm = pe.transpose(ps_m[0:TN, 64 + n * NT:64 + (n + 1) * NT], a, ident[0:NT, 0:NT])
            mm.then_inc(node_pe, 1)
            pe.wait_ge(node_dve, 3)

            dense(1)
            missing_groups()

            def second2(q, s):
                pe.wait_ge(d2a.h, H1 * (q + 1))
                if not (isinstance(q, int) and q < 2):
                    pe.wait_ge(d2a.done, q - 1)
                for k in range(TP):
                    to = ps_z[s][:, k, :, :].rearrange("p k f -> p (k f)")
                    for m in range(H1):
                        pe.matmul(to, hT[:, s, m, TN * k:TN * (k + 1)], w22[:, m, :, :].rearrange("p k f -> p (k f)"),
                                  start=(m == 0), stop=False)
                    mm = pe.matmul(to, ones[0:1, 0:TN], row2[:, 1:3, :].rearrange("p k f -> p (k f)"), start=False, stop=True)
                mm.then_inc(d2a.Y, 1)

            def layer2(q, u, s, first):
                if not is_last(q):
                    transpose_rows(d2a, q + 1, u + s, 1 - s, xa)
                pe.wait_ge(d2a.xT, q + 1)
                pe.wait_ge(d2a.a, q + 1)
                if not first:
                    pe.wait_ge(d2a.h, H1 * (q - 1))
                for m in range(H1):
                    pe.matmul(ps_h[2 * s + m], w21[:, 0, m * P:(m + 1) * P], aT[:, s, 0, :], start=True, stop=False)
                    pe.matmul(ps_h[2 * s + m], w21[:, 1, m * P:(m + 1) * P], xT[:, s, :], start=False, stop=True).then_inc(d2a.H, 1)
                if not (first and s == 0):
                    second2(q - 1, 1 - s)
            transpose_rows(d2a, 0, 0, 0, xa)
            pairs(pe, layer2, 4)
            second2(NP - 1, (NP - 1) % 2)
            pe.wait_ge(d2a.done, NP)

            scale_products()
            dense(2)
            missing_groups()

            def mean_rows(q, s):
                pe.wait_ge(d2b.a, q + 1)
                if not (isinstance(q, int) and q < 2):
                    pe.wait_ge(d2b.step, steps2b(q - 2) + 1)
                for k in range(TP):
                    mm = pe.transpose(ps_y[s][:, k, :], aT[:, s, 0, TN * k:TN * (k + 1)], ident[:, :])
                mm.then_inc(d2b.Y, 1)

            def layer2b(q, u, s, first):
                if not (isinstance(q, int) and q == NP - 1):
                    mean_rows(q + 1, 1 - s)
                pe.wait_ge(d2b.h, q + 1)
                for k in range(TP):
                    mm = pe.transpose(ps_t[s][:, TN * k:TN * (k + 1)], yb[:, s, k, 0:P], ident[0:TN, 0:TN])
                mm.then_inc(d2b.T, 1)
                pe.wait_ge(d2b.xT, q + 1)
                if not first:
                    pe.wait_ge(d2b.done, q - 1)
                for k in range(TP):
                    mm = pe.matmul(ps_v[s][:, k, :], xT[:, s, TN * k:TN * (k + 1)], v6[:, :], start=True, stop=True)
                mm.then_inc(d2b.H, 1)
            mean_rows(0, 0)
            pairs(pe, layer2b)

            for k, (n, dirs) in enumerate(SCANS):
                pe.wait_ge(scan_dve, 2 * k + 1)
                for d in range(dirs):
                    pe.transpose(ps_m[0:n, 2 * d * P:(2 * d + 1) * P], ends[:, d, 0, 0:n], ident[:, :])
                    mm = pe.transpose(ps_m[0:n, (2 * d + 1) * P:(2 * d + 2) * P], ends[:, d, 1, 0:n], ident[:, :])
                mm.then_inc(scan_pe, 1)
                pe.wait_ge(scan_dve, 2 * k + 2)
                for d in range(dirs):
                    mm = pe.transpose(ps[6][:, 8 * d:8 * d + n], carry[0:n, d, d:d + P], ident[0:n, 0:n])
                mm.then_inc(scan_pe, 1)

            sums(C3, weigh=True)
            missing_groups(weigh=True)

            def layer3(q, u, s, first):
                transpose_rows(d3, q, u, s)
                pe.wait_ge(d3.xT, q + 1)
                pe.wait_ge(d3.a, q + 1)
                if not first:
                    pe.wait_ge(d3.step, STEPS3 * (q - 2) + 1 + TP * HEADS)
                for k in range(TP):
                    pe.matmul(ps_l[s][k], xT[:, s, TN * k:TN * (k + 1)], fused3[:, :, :].rearrange("p h f -> p (h f)"),
                              start=True, stop=True)
                    for h in range(HEADS):
                        pe.matmul(ps_y[s][:, k, :], aT[:, s, h, TN * k:TN * (k + 1)], fused3[:, h, :], start=(h == 0), stop=False)
                    mm = pe.matmul(ps_y[s][:, k, :], ones[0:1, 0:TN], row2[:, 3, :], start=False, stop=True)
                mm.then_inc(d3.Y, 1)
            pairs(pe, layer3)

        @block.vector
        def _(v):
            extra = v.alloc_register("dve_extra")
            v.reg_mov(extra, 0)
            miss = v.alloc_register("dve_missing")
            loads = v.alloc_register("dve_loads")
            v.reg_mov(loads, 0)
            norms = v.alloc_register("dve_norms")
            v.reg_mov(norms, 0)
            regs = [v.alloc_register(f"dve_base{n}") for n in range(TB * AH)]
            meta_f = meta[:, :, :].rearrange("a n k -> a (n k)")
            step = Count()

            v.memset(prod[:, :, :, :, :], 0.0).then_inc(scores_ready, 1)
            v.memset(x_mark[:, 0:1], 0.0).then_inc(x_done, 1)
            for n in range(RING):
                v.memset(src_i[:, NE + CH * n:NE + CH * (n + 1)], 0).then_inc(key_summed, 1)
            for n in range(2):
                v.memset(key[:, NE + CW * n:NE + CW * (n + 1)], -1.0).then_inc(key_copied, 1)
            v.memset(row[:, NE:NE + CH], 0.0).then_inc(dve_step, step.up())
            for n in range(RING * HALF):
                v.memset(dst_rel[:, NE + CW * n:NE + CW * (n + 1)], -1.0).then_inc(psum_free, 1)

            v.wait_ge(lists_in, 32)
            for n in range(2):
                v.tensor_copy(lists_f[n], lists[n]).then_inc(prep_dve, 1)
            dst_f, src_f, kept, lost, block, block_i = tmp
            by_chunk = lambda a: a.rearrange("p (h c) -> p h c", c=CW)
            v.wait_ge(prep_pe, 1)
            for c in range(CW):
                v.tensor_copy(by_chunk(dst_f)[:, :, c], ps[c][:, 0:NH]).then_inc(dve_step, step.up())
            v.wait_ge(dve_step, step.n)
            v.tensor_copy(base_f[:, :], by_chunk(dst_f)[0:1, :, 0]).then_inc(prep_dve, 1)
            v.tensor_copy(meta_f[:, :], by_chunk(dst_f)[0:1, :, 0]).then_inc(dve_step, step.up())
            v.wait_ge(prep_pe, 2)
            for c in range(CW):
                v.tensor_copy(by_chunk(src_f)[:, :, c], ps[2 + c][:, 0:NH]).then_inc(dve_step, step.up())
                v.tensor_copy(by_chunk(src_i[:, 0:NE])[:, :, c], ps[2 + c][:, 0:NH]).then_inc(dve_step, step.up())
            v.wait_ge(prep_pe, 3)
            v.tensor_tensor(by_chunk(dst_rel[:, 0:NE]), by_chunk(dst_f), ps_m[:, 0:NH].unsqueeze(2).to_broadcast([P, NH, CW]),
                            ALU.subtract).then_inc(dve_step, step.up())
            v.wait_ge(dve_step, step.n)
            v.tensor_scalar(kept, dst_rel[:, 0:NE], 0.0, float(W - 1), ALU.max, ALU.min).then_inc(dve_step, step.up())
            v.tensor_scalar(block_i.bitcast(I32), src_i[:, 0:NE], 7, None, ALU.arith_shift_right).then_inc(dve_step, step.up())
            v.wait_ge(dve_step, step.n)
            v.tensor_tensor(lost, kept, dst_rel[:, 0:NE], ALU.not_equal).then_inc(dve_step, step.up())
            v.tensor_copy(block, block_i.bitcast(I32)).then_inc(dve_step, step.up())
            v.wait_ge(dve_step, step.n)
            v.tensor_tensor(kept, kept, dst_rel[:, 0:NE], ALU.is_equal).then_inc(dve_step, step.up())
            v.scalar_tensor_tensor(row[:, 0:NE], block, float(-P), src_f, ALU.mult, ALU.add).then_inc(dve_step, step.up())
            v.scalar_tensor_tensor(block, block, float(W), dst_rel[:, 0:NE], ALU.mult, ALU.add).then_inc(dve_step, step.up())
            v.scalar_tensor_tensor(dst_left[:, :], dst_f, 1.0, lost, ALU.add, ALU.mult).then_inc(dve_step, step.up())
            v.scalar_tensor_tensor(lost, dst_f, float(N), lost, ALU.is_lt, ALU.mult).then_inc(dve_step, step.up())
            v.wait_ge(dve_step, step.n)
            v.scalar_tensor_tensor(key[:, 0:NE], block, 1.0, kept, ALU.add, ALU.mult).then_inc(dve_step, step.up())
            v.tensor_scalar(dst_left[:, :], dst_left[:, :], -1.0, None, ALU.add).then_inc(dve_step, step.up())
            v.tensor_reduce(missed[:, :], lost.rearrange("p (g k) -> p g k", k=CH), AX.X, ALU.add).then_inc(prep_dve, 1)
            v.wait_ge(dve_step, step.n)
            v.tensor_scalar(key[:, 0:NE], key[:, 0:NE], -1.0, None, ALU.add).then_inc(dve_step, step.up())
            v.wait_ge(prep_pe, 4)
            v.tensor_copy(missing_i[:, 0:NG], ps[6][0:1, 0:NG]).then_inc(dve_step, step.up())
            v.tensor_reduce(missing_f[:, :], ps[6][0:1, 0:NG], AX.X, ALU.add).then_inc(dve_step, step.up())
            part_e = hT[0:EF, 1, :, :].rearrange("p m n -> p (m n)")[:, 0:HEADS * P]
            v.wait_ge(we_in, 32)
            v.tensor_tensor(part_e, we[:, :, :].rearrange("p h c -> p (h c)"),
                            ae_b[:, :, :].rearrange("p h c -> p (h c)"), ALU.mult).then_inc(dve_step, step.up())
            v.wait_ge(dve_step, step.n)
            v.tensor_copy(missing_i[:, NG:NG + 1], missing_f[:, :]).then_inc(dve_step, step.up())
            v.tensor_reduce(we3[:, :], part_e.rearrange("p (h c) -> p h c", c=P), AX.X, ALU.add).then_inc(dve_step, step.up())
            v.wait_ge(dve_step, step.n)
            v.wait_ge(consts, CONSTS)
            v.tensor_tensor(we_d[:, :, :], ident[0:EF, 0:EF].unsqueeze(1).to_broadcast([EF, HEADS, EF]),
                            we3[:, :].unsqueeze(2).to_broadcast([EF, HEADS, EF]), ALU.mult).then_inc(prep_dve, 1)
            v.wait_ge(prep_pe, 5)
            v.tensor_copy(we_b[:, :, :], ps_m[:, 0:HEADS * EF].rearrange("p (h e) -> p h e", e=EF)).then_inc(prep_dve, 1)
            v.tensor_copy(iota_x[:, :], iota_w[:, :]).then_inc(x_iota, 1)
            v.wait_ge(prep_dve, 6)
            v.wait_ge(x_iota, 1)
            v.memset(x_mark[:, 0:1], 0.0).then_inc(dst_ready, 1)

            def scores(u):
                n = RING * u
                v.wait_ge(scores_ready, 1 + n)
                for i in range(RING):
                    v.wait_ge(ea_landed[i], 16 * (u + 1))
                    v.tensor_tensor(prod[:, i, :, :, :], ea[:, i, :, :].unsqueeze(2).to_broadcast([P, CH, HEADS, EF]),
                                    we_b[:, :, :].unsqueeze(1).to_broadcast([P, CH, HEADS, EF]), ALU.mult).then_inc(prod_ready, 1)
                for i in range(RING):
                    v.wait_ge(prod_ready, n + i + 1)
                    v.tensor_reduce(e_score[:, i, :, :], prod[:, i, :, :, :], AX.X, ALU.add).then_inc(scores_ready, 1)

            def sources(g, i):
                v.tensor_copy(idx[:, i, :], src_i[:, bass.ds(CH * g, CH)]).then_inc(idx_ready, 1)

            def sums(a, sums_too=False, weigh=False, adjacency=False):
                def make(g, i):
                    v.tensor_tensor(onehot[:, i, :, :],
                                    dst_rel[:, bass.ds(CH * g, CH)].unsqueeze(2).to_broadcast([P, CH, W]),
                                    iota_w[:, :].unsqueeze(1).to_broadcast([P, CH, W]), ALU.is_equal).then_inc(onehot_ready, 1)

                def keys(g, i):
                    n = HALF * i % 4
                    v.wait_ge(key_summed, HALF * (g + 1))
                    v.tensor_tensor(row_1h[:, n:n + HALF, :, :].rearrange("p n c k -> p (n c) k"),
                                    iota_k[:, 0:P].unsqueeze(1).to_broadcast([P, CH, P]),
                                    row[:, bass.ds(CH * g, CH)].unsqueeze(2).to_broadcast([P, CH, P]), ALU.is_equal)
                    for h in range(HALF):
                        for c in range(CW):
                            op = v.tensor_scalar(key_1h[n + h][:, c, :], iota_k[:, :], key[:, bass.ds(CH * g + CW * h + c, 1)],
                                                 None, ALU.is_equal)
                        op.then_inc(key_ready, 1)

                def weights(g, u, i):
                    v.wait_ge(onehot_ready, ONEHOTS(a) + g + 1)
                    v.wait_ge(att_landed[i], 16 * (u + 1))
                    v.tensor_tensor(weighted[:, i, :, :, :],
                                    onehot[:, i, :, :].unsqueeze(2).to_broadcast([P, CH, HEADS, W]),
                                    att[:, i, :, :].unsqueeze(3).to_broadcast([P, CH, HEADS, W]),
                                    ALU.mult).then_inc(weighted_ready, 1)

                v.memset(wide[:, :, :] if weigh else wide[:, 2, :], 0.0).then_inc(dve_step, step.up())
                if sums_too:
                    v.memset(wide[:, 1, :], 0.0).then_inc(dve_step, step.up())
                    for i in range(RING):
                        v.memset(ps[4 + i][:, 0:HALF * W], 0.0).then_inc(ps_zero, 1)
                for g in range(LEAD):
                    make(g, g)
                if adjacency:
                    keys(0, 0)
                if weigh:
                    for g in range(2):
                        weights(g, 0, g)
                v.wait_ge(dve_step, step.n)

                def iteration(u, bases, last):
                    for i in range(RING):
                        g = RING * u + i
                        make(g + LEAD, (i + LEAD) % RING)
                        if adjacency:
                            keys(g + 1, i + 1)
                        if weigh and not (last and i + 2 >= RING):
                            weights(g + 2, u + (i + 2) // RING, (i + 2) % RING)
                        v.wait_ge(group_summed, SUMMED(a) + g + 1)
                        for h in range(HALF):
                            at = bass.ds(bases[HALF * i + h], W)
                            v.wait_ge(psum_free, FREED(a) + HALF * g + h)
                            if sums_too:
                                acc = wide[:, 1:3, at]
                                part = ps[4 + i][:, 0:2 * P].rearrange("p (k w) -> p k w", w=P)[:, :, W * h:W * (h + 1)]
                            elif weigh:
                                acc = wide[:, :, at]
                                part = ps_a[i][:, HEADS * W * h:HEADS * W * (h + 1)].rearrange("p (h w) -> p h w", w=W)
                            else:
                                acc = wide[:, 2, at]
                                part = ps_a[i][:, W * h:W * (h + 1)]
                            v.tensor_tensor(acc, acc, part, ALU.add).then_inc(psum_free, 1)

                def two_iterations(k, last):
                    v.reg_load(regs, meta_f[0:1, bass.ds(2 * AH * k, 2 * AH)])
                    bases = [v.snap(r, min_val=0, max_val=N - 1) for r in regs]
                    for n in range(2):
                        iteration(2 * k + n, bases[AH * n:AH * (n + 1)], last and n == 1)

                with v.Fori(0, NIT // 2 - 1) as k:
                    two_iterations(k, False)
                two_iterations(NIT // 2 - 1, True)
                v.wait_ge(psum_free, FREED(a + 1))

            def missing_groups(loaded=0, sums_too=False, weigh=False):
                v.reg_load(miss, missing_i[0:1, NG:NG + 1])
                with v.If(v.snap(miss, min_val=0, max_val=EP) > 0):
                    with v.Fori(0, NG) as g:
                        v.reg_load(miss, missing_i[0:1, bass.ds(g, 1)])
                        with v.If(v.snap(miss, min_val=0, max_val=GE) > 0):
                            if loaded:
                                v.reg_add(loads, loads, 16 * loaded)
                                v.wait_ge(x_loaded, v.snap(loads, min_val=1, max_val=1 << 20))
                            if sums_too:
                                v.tensor_copy(one_ea[:, :, 1:1 + EF], ea[:, 0, :, :]).then_inc(x_scored, 1)
                            else:
                                v.tensor_copy(idx[:, 0, :], src_i[:, bass.ds(CH * g, CH)]).then_inc(x_idx, 1)
                            with v.Fori(0, NK) as k:
                                v.reg_add(extra, extra, 1)
                                n = v.snap(extra, min_val=1, max_val=1 << 20)
                                v.wait_ge(x_iota, n)
                                if weigh:
                                    for c in range(CH):
                                        for h in range(HEADS):
                                            op = v.tensor_scalar(weighted_x[:, c, h, :], iota_x[:, :],
                                                                 dst_left[:, bass.ds(CH * g + c, 1)], att[:, 0, c, h:h + 1],
                                                                 ALU.is_equal, ALU.mult)
                                    op.then_inc(x_onehot, 1)
                                else:
                                    v.tensor_tensor(onehot_x[:, :, :],
                                                    dst_left[:, bass.ds(CH * g, CH)].unsqueeze(2).to_broadcast([P, CH, W]),
                                                    iota_x[:, :].unsqueeze(1).to_broadcast([P, CH, W]), ALU.is_equal
                                                    ).then_inc(x_onehot, 1)
                                v.wait_ge(x_onehot, n)
                                v.tensor_scalar(wrap_x[:, :], iota_x[:, :], float((NK - 1) * W), float(-NK * W), ALU.is_ge, ALU.mult
                                                ).then_inc(x_wrap, 1)
                                v.wait_ge(x_wrap, n)
                                v.scalar_tensor_tensor(iota_x[:, :], iota_x[:, :], float(W), wrap_x[:, :], ALU.add, ALU.add
                                                       ).then_inc(x_iota, 1)
                                v.wait_ge(x_summed, n)
                                if sums_too:
                                    part = nsum[0:1 + EF, bass.ds(W * k, W)]
                                    v.tensor_tensor(part, part, ps_xn, ALU.add)
                                acc = wide[:, :, bass.ds(W * k, W)] if weigh else wide[:, 2, bass.ds(W * k, W)]
                                frm = ps_x.rearrange("p (h w) -> p h w", w=W) if weigh else ps_x[:, 0:W]
                                v.tensor_tensor(acc, acc, frm, ALU.add).then_inc(x_added, 1)
                                v.wait_ge(x_added, n)
                            if loaded:
                                v.memset(x_mark[:, 0:1], 0.0).then_inc(x_done, 1)

            def table_parts(k):
                if k:
                    v.wait_ge(slice_used, SL * NS * k)
                v.memset(table[:, SL - 1, (QS - 1) * P:QS * P], 0.0).then_inc(table_zero, 1)

            def scale_parts():
                for s in range(SL):
                    v.wait_ge(slice_in[s], slices_in(s, 2) + (32 if s == SL - 1 else 16))
                    v.tensor_reduce(tmax[:, s:s + 1], table[:, s, 0:QS * P], AX.X, ALU.max, apply_absolute_value=True
                                    ).then_inc(dve_step, step.up())
                v.wait_ge(dve_step, step.n)
                v.tensor_reduce(scale[:, 0:1], tmax[:, :], AX.X, ALU.max).then_inc(dve_step, step.up())
                v.wait_ge(dve_step, step.n)
                v.tensor_copy(tmax[:, 0:1], scale[:, 0:1]).then_inc(table_max, 1)
                v.wait_ge(scale_pe, 1)
                v.tensor_reduce(pow2[:, 0:1], ps_m[0:1, 0:P], AX.X, ALU.max).then_inc(dve_step, step.up())
                v.wait_ge(dve_step, step.n)
                v.tensor_scalar(pow2[:, 0:1], pow2[:, 0:1], 2.0 ** -90, 2.0 ** 90, ALU.max, ALU.min).then_inc(dve_step, step.up())
                v.wait_ge(dve_step, step.n)
                v.tensor_scalar(pow2[:, 0:1].bitcast(I32), pow2[:, 0:1].bitcast(I32), 0x7F800000, None, ALU.bitwise_and
                                ).then_inc(dve_step, step.up())
                v.wait_ge(dve_step, step.n)
                v.tensor_scalar(pow2[:, 1:2], pow2[:, 0:1], 2.0 ** -14, None, ALU.mult).then_inc(dve_step, step.up())
                v.wait_ge(dve_step, step.n)
                v.reciprocal(pow2[:, 0:1], pow2[:, 1:2]).then_inc(table_max, 1)
                v.wait_ge(scale_pe, 2)
                v.tensor_copy(scale[:, :], ps_m[:, P:P + 2]).then_inc(scaled, 1)

            def dense(k):
                v.wait_ge(scaled, SCALED[k])
                for s in range(SL):
                    v.wait_ge(high_ready, SL * k + s + 1)
                    v.scalar_tensor_tensor(high_low[:, 1, QS * s:QS * (s + 1), :].rearrange("p q f -> p (q f)"),
                                           table[:, s, 0:QS * P], scale[:, 0:1],
                                           high_low[:, 0, QS * s:QS * (s + 1), :].rearrange("p q f -> p (q f)"),
                                           ALU.mult, ALU.subtract).then_inc(low_ready, 1)
                v.memset(wide[:, 2, :], 0.0).then_inc(dve_step, step.up())
                v.wait_ge(dve_step, step.n)

                def add_step(t, b, first):
                    v.reg_load(regs, meta_f[0:1, bass.ds(TB * AH * t, TB * AH)])
                    bases = [v.snap(r, min_val=0, max_val=N - 1) for r in regs]
                    v.wait_ge(slice_used, SL * (NS * k + t + 1))
                    for n in range(TB * AH):
                        before = TB * AH * (NS * k + t) + n
                        if not (first and b == 0 and n == 0 and k == 0):
                            v.wait_ge(win_added, before)
                        acc = wide[:, 2, bass.ds(bases[n], W)]
                        v.scalar_tensor_tensor(acc, ps_d[b][:, W * n:W * (n + 1)], scale[:, 1:2], acc, ALU.mult, ALU.add
                                               ).then_inc(win_added, 1)

                for b in range(2):
                    add_step(b, b, True)
                with v.Fori(1, NS // 2) as t:
                    for b in range(2):
                        add_step(2 * t + b, b, False)
                v.wait_ge(win_added, TB * AH * NS * (k + 1))

            def layer_norm(s_, s, n, r, o, last):
                for k in range(TP):
                    v.bn_stats(st[:, s, k, :], r[:, s, k, :]).then_inc(s_.step, 1)
                v.wait_ge(s_.step, n + 2)
                v.reg_add(norms, norms, 1)
                for k in range(TP):
                    v.bn_aggr(mv[:, s, k, :], st[:, s, k, :]).then_inc(s_.step, 1)
                v.wait_ge(root, v.snap(norms, min_val=1, max_val=1 << 20))
                v.reciprocal(rstd[:, s, :], rstd[:, s, :]).then_inc(s_.step, 1)
                v.wait_ge(s_.step, n + 5)
                for k in range(TP):
                    op = v.tensor_scalar(o[:, s, k, 0:P], r[:, s, k, :], mv[:, s, k, 0:1], rstd[:, s, k:k + 1],
                                         ALU.subtract, ALU.mult)
                op.then_inc(last, 1)

            sums(L0, sums_too=True, adjacency=True)
            missing_groups(loaded=4, sums_too=True)
            v.memset(x_mark[:, 1:2], 0.0).then_inc(node_sums, 1)

            def layer0(q, u, s, first):
                n = 6 * q
                v.wait_ge(d0.Y, q + 1)
                v.wait_ge(*d0.landed(s, u))
                v.tensor_tensor(rb[:, s, :, :], ps_y[s], xb[:, s, :, :], ALU.add).then_inc(d0.step, 1)
                v.wait_ge(d0.step, n + 1)
                if not first:
                    v.wait_ge(*d0.stored(s, u))
                layer_norm(d0, s, n + 1, rb, yb, d0.done)
            pairs(v, layer0)

            for k in range(PIECES):
                v.wait_ge(sums_pe, k + 1)
                at = slice(512 * k, min(512 * (k + 1), N))
                v.tensor_copy(nsum[0:1 + HEADS, at], ps[1 + k % 2][0:1 + HEADS, 0:at.stop - at.start]).then_inc(node_sums, 1)

            v.wait_ge(w_in, 16 * w_loads.n)
            hw = HEADS * P
            part = [hT_f[:, 0:hw], hT_f[:, hw:2 * hw]]
            for n in range(2):
                v.tensor_tensor(part[n], w3[:, :, :].rearrange("p h c -> p (h c)"),
                                att_b[:, n, :, :].rearrange("p h c -> p (h c)"), ALU.mult).then_inc(dve_step, step.up())
            v.wait_ge(dve_step, step.n)
            for n in range(2):
                v.tensor_reduce(v6[:, HEADS * n:HEADS * (n + 1)], part[n].rearrange("p (h c) -> p h c", c=P), AX.X, ALU.add)
            v.tensor_scalar(eps1, eps1, 1.0, None, ALU.add).then_inc(dve_step, step.up())
            v.wait_ge(dve_step, step.n)
            v.wait_ge(prep_pe, 6)
            v.tensor_copy(w3T[:, :, :], ps[6][:, 0:hw].rearrange("p (h c) -> p h c", c=P)).then_inc(prep_dve, 1)
            v.wait_ge(prep_pe, 7)
            v.tensor_copy(fused3[:, :, :], ps[6][:, 0:hw].rearrange("p (h c) -> p h c", c=P)).then_inc(prep_dve, 1)
            v.wait_ge(prep_pe, 8)
            v.tensor_tensor(row2[:, 3, :], row2[:, 3, :], ps_m[0:1, 256:256 + P], ALU.add).then_inc(prep_dve, 1)
            v.wait_ge(prep_dve, 9)

            v.wait_ge(push_zeroed, 16 * 2 * HEADS)
            table_parts(0)
            v.memset(scale[:, 0:1], 2.0 ** 10)
            v.memset(scale[:, 1:2], 2.0 ** -10).then_inc(scaled, 1)
            dense(0)
            missing_groups()

            def stats1(q):
                v.wait_ge(d1a.h, H1 * (q + 1))
                for m in range(H1):
                    op = v.bn_stats(bn1[:, m, bass.ds(q, 1), :], blk(wide[:, m, :], q))
                op.then_inc(d1a.done, 1)

            def layer1(q, u, s, first):
                v.wait_ge(d1a.T, q + 1)
                if not first:
                    v.wait_ge(d1a.H, H1 * (q - 1))
                v.scalar_tensor_tensor(aT[:, s, 0, :], ps_t[s], eps1, blk(wide[:, 2, :], q), ALU.mult, ALU.add
                                       ).then_inc(d1a.a, 1)
                if not (first and s == 0):
                    stats1(q - 1)
            pairs(v, layer1)
            stats1(NP - 1)
            v.wait_ge(d1a.done, NP)

            def norm(lo, hi, frm, g, e):
                for m in range(lo, hi):
                    v.bn_aggr(bnm[:, m, :], frm[m - lo]).then_inc(dve_step, step.up())
                v.wait_ge(dve_step, step.n)
                v.tensor_copy(bns[:, lo:hi, 1], bnm[:, lo:hi, 1]).then_inc(bn_var, 1)
                v.wait_ge(bn_root, 1 if lo == 0 else 2)
                v.reciprocal(bns[:, lo:hi, 0], bns[:, lo:hi, 1]).then_inc(dve_step, step.up())
                v.wait_ge(dve_step, step.n)
                v.tensor_tensor(bns[:, lo:hi, 0], bns[:, lo:hi, 0], col[:, g:g + hi - lo], ALU.mult).then_inc(dve_step, step.up())
                v.wait_ge(dve_step, step.n)
                v.tensor_tensor(bnm[:, lo:hi, 0], bnm[:, lo:hi, 0], bns[:, lo:hi, 0], ALU.mult).then_inc(dve_step, step.up())
                v.wait_ge(dve_step, step.n)
                v.tensor_tensor(bns[:, lo:hi, 1], col[:, e:e + hi - lo], bnm[:, lo:hi, 0], ALU.subtract).then_inc(bn_ready, 1)

            norm(0, H1, [bn1[:, m, :, :].rearrange("p q k -> p (q k)") for m in range(H1)], g11, e11)

            def stats2(q, u, s, first):
                v.wait_ge(d1b.Y, q + 1)
                v.tensor_scalar(blk(wide[:, 0, :], q), ps_b[s], col[:, b12:b12 + 1], None, ALU.add).then_inc(d1b.xT, 1)
                v.wait_ge(d1b.xT, q + 1)
                v.bn_stats(bn2[:, bass.ds(q, 1), :], blk(wide[:, 0, :], q)).then_inc(d1b.done, 1)
            pairs(v, stats2)
            v.wait_ge(d1b.done, NP)
            norm(H1, H1 + 1, [bn2[:, :, :].rearrange("p q k -> p (q k)")], g12, e12)

            def layer1c(q, u, s, first):
                n = 7 * q
                v.wait_ge(d1c.Y, q + 1)
                v.wait_ge(*d1c.landed(s, u))
                v.tensor_tensor(rb[:, s, :, :], ps_y[s], xb[:, s, :, :], ALU.add).then_inc(d1c.step, 1)
                v.wait_ge(d1c.step, n + 1)
                v.scalar_tensor_tensor(ub[:, s, :, :], rb[:, s, :, :], 0.0, xb[:, s, :, :], ALU.max, ALU.add).then_inc(d1c.step, 1)
                v.wait_ge(d1c.step, n + 2)
                if not first:
                    v.wait_ge(*d1c.stored(s, u))
                layer_norm(d1c, s, n + 2, ub, yb, d1c.done)
            pairs(v, layer1c)

            v.wait_ge(sums_in, 16)
            cnt = cntB[:, 0, :]
            v.tensor_tensor_scan(endB[:, :], ones[0:NT, 0:TN], cnt, 0.0, ALU.mult, ALU.add).then_inc(dve_step, step.up())
            v.tensor_scalar(rcB[:, :], cnt, 1.0, None, ALU.max).then_inc(dve_step, step.up())
            v.wait_ge(dve_step, step.n)
            v.tensor_copy(totB[:, :], endB[:, TN - 1:TN]).then_inc(node_dve, 1)
            v.reciprocal(rcB[:, :], rcB[:, :]).then_inc(node_rc, 1)
            v.wait_ge(node_rc, 1)
            v.tensor_tensor(meanB[:, :, :], cntB[:, 1:1 + HEADS, :], rcB[:, :].unsqueeze(1).to_broadcast([NT, HEADS, TN]),
                            ALU.mult).then_inc(dve_step, step.up())
            v.tensor_scalar(begB[:, :], cnt, 0.0, float(4 * EP), ALU.is_equal, ALU.mult).then_inc(dve_step, step.up())
            v.wait_ge(node_pe, 1)
            v.tensor_copy(carB[:, :], ps_m[0:NT, 0:1]).then_inc(dve_step, step.up())
            v.wait_ge(dve_step, step.n)
            v.scalar_tensor_tensor(endB[:, :], endB[:, :], carB[:, 0:1], begB[:, :], ALU.add, ALU.add).then_inc(dve_step, step.up())
            v.wait_ge(dve_step, step.n)
            v.tensor_tensor(begB[:, :], endB[:, :], cnt, ALU.subtract).then_inc(dve_step, step.up())
            v.wait_ge(dve_step, step.n)
            v.tensor_scalar(endB[:, :], endB[:, :], -1.0, None, ALU.add).then_inc(node_dve, 1)
            v.wait_ge(node_pe, 2)
            v.tensor_copy(beg_i[:, :], ps_m[0:TN, 64:64 + NT])
            v.tensor_copy(end_i[:, :], ps_m[0:TN, 64 + NT:64 + 2 * NT])
            v.tensor_copy(amean[:, :, :], ps_m[0:TN, 64 + 2 * NT:64 + (2 + HEADS) * NT].rearrange("p (h j) -> p j h", h=HEADS)
                          ).then_inc(node_dve, 1)
            v.wait_ge(node_dve, 3)

            table_parts(1)
            dense(1)
            missing_groups()
            v.wait_ge(sums_in, 32)

            def mean(s_, q, s):
                v.tensor_tensor(aT[:, s, 0, :], blk(wide[:, 2, :], q), blk(rcnt, q), ALU.mult).then_inc(s_.a, 1)

            def rest2(q, u, s, first):
                v.wait_ge(d2a.Y, q + 1)
                v.wait_ge(*d2a.landed(s, u))
                if not first:
                    v.wait_ge(*d2a.stored(s, u))
                v.tensor_copy(yb[:, s, :, 0:P], ps_z[s][:, :, 0, :])
                v.tensor_tensor(zb[:, s, :, :], ps_z[s][:, :, 1, :], xb[:, s, :, :], ALU.add).then_inc(d2a.done, 1)

            def layer2(q, u, s, first):
                if not is_last(q):
                    if not (first and s == 0):
                        v.wait_ge(d2a.H, H1 * q)
                    mean(d2a, q + 1, 1 - s)
                rest2(q, u, s, first)
            mean(d2a, 0, 0)
            pairs(v, layer2)

            table_parts(2)
            scale_parts()
            dense(2)
            missing_groups()

            def scores2(q, s):
                n = 8 * q + (6 if isinstance(q, int) and q == NP - 1 else 12)
                v.wait_ge(d2b.H, q + 1)
                pj = push[:, bass.ds(TP * q, TP), :]
                v.tensor_copy(yb[:, s, :, P:P + HEADS], ps_v[s][:, :, 0:HEADS])
                v.tensor_copy(pj[:, :, 0:HEADS], ps_v[s][:, :, HEADS:2 * HEADS])
                v.tensor_tensor(psum6[:, s, :, :], ps_v[s][:, :, 0:HEADS], amean[:, bass.ds(TP * q, TP), :], ALU.add
                                ).then_inc(d2b.step, 1)
                v.wait_ge(d2b.step, n + 1)
                v.tensor_tensor(psum6[:, s, :, :], psum6[:, s, :, :], ps_v[s][:, :, HEADS:2 * HEADS], ALU.add).then_inc(d2b.step, 1)
                v.wait_ge(d2b.step, n + 2)
                v.scalar_tensor_tensor(pj[:, :, HEADS:2 * HEADS], psum6[:, s, :, :], SLOPE, psum6[:, s, :, :],
                                       ALU.mult, ALU.max).then_inc(d2b.done, 1)

            def layer2b(q, u, s, first):
                n = steps2b(q)
                if not (isinstance(q, int) and q == NP - 1):
                    if not (first and s == 0):
                        v.wait_ge(d2b.Y, q)
                    mean(d2b, q + 1, 1 - s)
                v.wait_ge(d2b.Y, q + 1)
                v.wait_ge(*d2b.landed(s, u))
                v.tensor_tensor(rb[:, s, :, :], ps_y[s], xb[:, s, :, :], ALU.add).then_inc(d2b.step, 1)
                v.wait_ge(d2b.step, n + 1)
                if not first:
                    v.wait_ge(*d2b.stored(s, u))
                layer_norm(d2b, s, n + 1, rb, yb, d2b.h)
                if not (first and s == 0):
                    scores2(q - 1, 1 - s)
            mean(d2b, 0, 0)
            pairs(v, layer2b)
            scores2(NP - 1, (NP - 1) % 2)

            def edge_scores(g, u, i, first):
                v.wait_ge(scores_ready, 1 + g + 1)
                v.wait_ge(rows_landed[i], 16 * CH * (u + 1))
                if not first:
                    v.wait_ge(as_stored[i], 16 * u)
                v.tensor_tensor(asum[:, i, :, :], rows[:, i, :, P:P + HEADS], e_score[:, i, :, :], ALU.add
                                ).then_inc(asum_ready, 1)
                if not (first and i == 0):
                    v.wait_ge(xe_stored[(i - 1) % RING], 16 * HALF * (u + (1 if i > 0 else 0)))
                    sources(g - 1 + RING, (i - 1) % RING)

            for i in range(RING):
                sources(i, i)
            def iterations(lo, hi):
                with v.Fori(lo, hi) as u:
                    scores(u)
                    for i in range(RING):
                        edge_scores(RING * u + i, u, i, False)

            edge_by_edge = lambda a, n: a.rearrange("p (j h) -> p h j", h=n)
            nothing = lambda take_max: -BIG if take_max else 0.0
            operations = lambda take_max: (ALU.add, ALU.max) if take_max else (ALU.mult, ALU.add)
            ways = (slice(None, None, 1), slice(None, None, -1))

            def scan_run(k, values, to, take_max, initial):
                n, dirs = SCANS[k]
                goes_on = ((NF, NB) if take_max else (CF, CB))
                for d in range(dirs):
                    for h in range(n):
                        v.tensor_tensor_scan(to[d][:, h, :][:, ways[d]], goes_on[d][:, ways[d]], values[:, h, :][:, ways[d]],
                                             initial(d, h), *operations(take_max)).then_inc(dve_step, step.up())
                v.wait_ge(dve_step, step.n)

            def scan_first(k, values, to, take_max):
                n, dirs = SCANS[k]
                scan_run(k, values, to, take_max, lambda d, h: nothing(take_max))
                for d in range(dirs):
                    last = EPP - 1 if d == 0 else 0
                    v.tensor_copy(ends[:, d, 0, 0:n], to[d][:, :, last])
                    op = v.tensor_copy(ends[:, d, 1, 0:n], allc[:, d:d + 1].to_broadcast([P, n]))
                op.then_inc(scan_dve, 1)
                v.memset(carry[:, :, :], nothing(take_max)).then_inc(dve_step, step.up())

            def scan_carry(k, take_max):
                n, dirs = SCANS[k]
                v.wait_ge(scan_pe, 2 * k + 1)
                for d in range(dirs):
                    flags = ps_m[0:n, (2 * d + 1) * P:(2 * d + 2) * P]
                    if take_max:
                        op = v.tensor_scalar(goes[0:n, d, :], flags, -1.0, BIG, ALU.add, ALU.mult)
                    else:
                        op = v.tensor_copy(goes[0:n, d, :], flags)
                    op.then_inc(dve_step, step.up())
                v.wait_ge(dve_step, step.n)
                for d in range(dirs):
                    op = v.tensor_tensor_scan(carry[0:n, d, 1 - d:1 - d + P][:, ways[d]], goes[0:n, d, :][:, ways[d]],
                                              ps_m[0:n, 2 * d * P:(2 * d + 1) * P][:, ways[d]], nothing(take_max),
                                              *operations(take_max))
                op.then_inc(scan_dve, 1)

            def scan_again(k, values, to, take_max):
                n, dirs = SCANS[k]
                v.wait_ge(scan_pe, 2 * k + 2)
                for d in range(dirs):
                    v.tensor_copy(start[:, 8 * d:8 * d + n], ps[6][:, 8 * d:8 * d + n]).then_inc(dve_step, step.up())
                v.wait_ge(dve_step, step.n)
                scan_run(k, values, to, take_max, lambda d, h: start[:, 8 * d + h:8 * d + h + 1])

            def scan(k, values, to, take_max):
                scan_first(k, values, to, take_max)
                scan_carry(k, take_max)
                scan_again(k, values, to, take_max)

            pushed_values = (0, edge_by_edge(PU, 2 * HEADS), (FILLP,), False)
            scores(0)
            for i in range(RING):
                edge_scores(i, 0, i, True)
            iterations(1, NIT // 4)
            v.wait_ge(scan_in, 16 * 4)
            v.tensor_tensor(CF, DI[1], DI[0], ALU.is_equal).then_inc(dve_step, step.up())
            v.tensor_tensor(CB, DI[1], DI[2], ALU.is_equal).then_inc(dve_step, step.up())
            v.wait_ge(dve_step, step.n)
            v.tensor_scalar(NF, CF, -1.0, BIG, ALU.add, ALU.mult).then_inc(dve_step, step.up())
            v.tensor_scalar(NB, CB, -1.0, BIG, ALU.add, ALU.mult).then_inc(dve_step, step.up())
            v.tensor_reduce(allc[:, 0:1], CF, AX.X, ALU.min).then_inc(dve_step, step.up())
            v.tensor_reduce(allc[:, 1:2], CB, AX.X, ALU.min).then_inc(dve_step, step.up())
            v.wait_ge(dve_step, step.n)
            iterations(NIT // 4, NIT // 4 + 3)
            scan_first(*pushed_values)
            iterations(NIT // 4 + 3, NIT // 2)
            scan_carry(0, False)
            iterations(NIT // 2, NIT // 2 + 3)
            scan_again(*pushed_values)
            iterations(NIT // 2 + 3, NIT)

            v.wait_ge(scan_in, 16 * 5)
            v.tensor_tensor(AL, FILLP[:, 0:HEADS, :], edge_by_edge(AS, HEADS), ALU.add).then_inc(dve_step, step.up())
            v.tensor_copy(XLP, FILLP[:, HEADS:2 * HEADS, :]).then_inc(dve_step, step.up())
            v.wait_ge(dve_step, step.n)
            v.scalar_tensor_tensor(AL, AL, SLOPE, AL, ALU.mult, ALU.max).then_inc(dve_step, step.up())
            v.wait_ge(dve_step, step.n)
            scan(1, AL, (FW, BW), True)
            v.tensor_tensor(FW, FW, BW, ALU.max).then_inc(dve_step, step.up())
            v.wait_ge(dve_step, step.n)
            v.tensor_tensor(FW, FW, XLP, ALU.max).then_inc(dve_step, step.up())
            v.wait_ge(dve_step, step.n)
            v.tensor_tensor(EXP_, AL, FW, ALU.subtract).then_inc(scan_exp, 1)
            v.tensor_tensor(XLP, XLP, FW, ALU.subtract).then_inc(scan_exp, 1)
            v.wait_ge(scan_act, 2)
            v.wait_ge(scan_exp, 2)
            scan(2, EXP_, (FW, BW), False)
            v.tensor_tensor(FW, FW, BW, ALU.add).then_inc(dve_step, step.up())
            v.wait_ge(dve_step, step.n)
            v.tensor_tensor(FW, FW, EXP_, ALU.subtract).then_inc(dve_step, step.up())
            v.wait_ge(dve_step, step.n)
            v.tensor_tensor(FW, FW, XLP, ALU.add).then_inc(dve_step, step.up())
            v.wait_ge(dve_step, step.n)
            v.reciprocal(BW, FW).then_inc(dve_step, step.up())
            v.wait_ge(dve_step, step.n)
            v.tensor_tensor(edge_by_edge(EX, HEADS), EXP_, BW, ALU.mult)
            v.tensor_tensor(edge_by_edge(XL, HEADS), XLP, BW, ALU.mult).then_inc(scan_done, 1)
            v.wait_ge(scan_out, 32)

            sums(C3, weigh=True)
            missing_groups(loaded=1, weigh=True)
            v.wait_ge(wl_in, 16 * NT)

            def layer3(q, u, s, first):
                n = STEPS3 * q
                v.wait_ge(d3.Y, q + 1)
                v.tensor_tensor(rb[:, s, :, :], ps_y[s], xb[:, s, :, :], ALU.add).then_inc(d3.step, 1)
                for h in range(HEADS):
                    v.wait_ge(d3.step, n + 1 + TP * h)
                    for k in range(TP):
                        v.scalar_tensor_tensor(rb[:, s, k, :], ps_l[s][k][:, h * P:(h + 1) * P],
                                               wloop_f[:, bass.ds(HEADS * (TP * q + k) + h, 1)], rb[:, s, k, :],
                                               ALU.mult, ALU.add).then_inc(d3.step, 1)
                n = n + 1 + TP * HEADS
                v.wait_ge(d3.step, n)
                layer_norm(d3, s, n, rb, ub, d3.step)
                n = n + 6
                v.wait_ge(d3.step, n)
                gb = [ln_gb[:, k, :].unsqueeze(1).to_broadcast([TN, TP, P]) for k in range(2)]
                v.tensor_tensor(ub[:, s, :, :], ub[:, s, :, :], gb[0], ALU.mult).then_inc(d3.step, 1)
                v.wait_ge(d3.step, n + 1)
                v.tensor_tensor(ub[:, s, :, :], ub[:, s, :, :], gb[1], ALU.add).then_inc(d3.step, 1)
                v.wait_ge(d3.step, n + 2)
                v.tensor_tensor(ub[:, s, :, :], ub[:, s, :, :], xb[:, s, :, :], ALU.add).then_inc(d3.step, 1)
                v.wait_ge(d3.step, n + 3)
                if not first:
                    v.wait_ge(*d3.stored(s, u))
                layer_norm(d3, s, n + 3, ub, yb, d3.done)
            pairs(v, layer3)


_INS = ["x", "src", "dst", "edge_attr_128", "edge_attr_16", "L0_gnn_W1", "L0_gnn_b1", "L0_gnn_W2", "L0_gnn_b2",
        "L1_gnn_eps", "L1_gnn_W1", "L1_gnn_b1", "L1_gnn_g1", "L1_gnn_be1", "L1_gnn_W2", "L1_gnn_b2", "L1_gnn_g2",
        "L1_gnn_be2", "L2_gnn_W1_l", "L2_gnn_W1_r", "L2_gnn_b1", "L2_gnn_W2_l", "L2_gnn_W2_r", "L2_gnn_b2",
        "L3_gnn_W", "L3_gnn_W_edge", "L3_gnn_att_src", "L3_gnn_att_dst", "L3_gnn_att_edge", "L3_gnn_gat_bias",
        "L3_gnn_lin_W", "L3_gnn_lin_b", "L3_gnn_ln_g", "L3_gnn_ln_b"]


def kernel(**inputs):
    import numpy as _np
    import concourse.bacc as _bacc
    from concourse import mybir as _mybir
    from concourse.bass_utils import run_bass_kernel_spmd as _run

    nc = _bacc.Bacc("TRN2", target_bir_lowering=False, num_devices=1)
    arrays, args = {}, {}
    for name in _INS:
        a = _np.ascontiguousarray(inputs[name])
        if _np.ndim(inputs[name]) == 0:
            a = a.reshape(1, 1)
        arrays[f"in_{name}"] = a
        args[name] = nc.dram_tensor(f"in_{name}", a.shape, _mybir.dt.from_np(a.dtype), kind="ExternalInput").ap()
    shape = inputs["x"].shape
    out = nc.dram_tensor("out", shape, F32, kind="ExternalOutput").ap()
    gnn_stack(nc, args, out)
    r = _run(nc, [arrays], core_ids=[0])
    return r.results[0]["out"]
```
